# Optimizing a Trainium2 kernel written in Bass

```python
import numpy as np
import jax
import jax.numpy as jnp

def _softmax(x, axis=-1):
    return jax.nn.softmax(x, axis=axis)

def _gelu(x):
    return jax.nn.gelu(x, approximate=True)

def _silu(x):
    return jax.nn.silu(x)

def _sigmoid(x):
    return jax.nn.sigmoid(x)

def _layernorm(x, axis=-1, eps=1e-05):
    m = jnp.mean(x, axis=axis, keepdims=True)
    v = jnp.var(x, axis=axis, keepdims=True)
    return (x - m) / jnp.sqrt(v + eps)

def _scatter_add(tgt, idx, src, axis=0):
    return tgt.at[idx].add(src)

def _segment_sum(src, seg, n):
    return jax.ops.segment_sum(src, seg, n)
kernel_name = 'mk_hybrid_d1_jaxref_r8_3e9a73'

def setup_inputs(seed: int=0):
    np.random.seed(seed)
    _w = jnp.asarray

    def _L0_attn_a_setup():
        import jax, jax.numpy as jnp
        import numpy as np
        H = 32
        D = 64
        BS = 32
        LAYER_IDX = 0
        NUM_LAYERS = 32
        EPS = 1e-05

        def _decay_buffers():
            base = 1.0 / 2.0 ** (8.0 / H)
            rate = base ** (jnp.arange(H, dtype=jnp.float32) + 1.0)
            factor = 1.0 - LAYER_IDX / (NUM_LAYERS - 1 + 1e-05) + 1e-05
            slope = (rate * factor)[:, None, None]
            r = jnp.arange(BS, dtype=jnp.float32) + 1.0
            query_decay = jnp.exp(-slope * r[:, None])
            key_decay = jnp.exp(-slope * (BS - r[:, None]))
            dd = r[:, None] - r[None, :]
            dd = slope * dd[None, :, :]
            dd = jnp.where(dd >= 0, -dd, -jnp.inf)
            diagonal_decay = jnp.exp(dd)[None]
            block_decay = jnp.exp(-slope * BS)
            return (slope, query_decay, key_decay, diagonal_decay, block_decay)

        def _rmsnorm(x, w):
            v = jnp.mean(x.astype(jnp.float32) ** 2, axis=-1, keepdims=True)
            return (x * jax.lax.rsqrt(v + EPS)).astype(x.dtype) * w
        key = jax.random.key(seed)
        ks = jax.random.split(key, 4)
        b, s, hid = (2, 512, 256)
        return {'hidden_states': jax.random.normal(ks[0], (b, s, hid), jnp.float32), 'qkv_w': jax.random.normal(ks[1], (3 * H * D, hid), jnp.float32) * 0.02, 'out_w': jax.random.normal(ks[2], (hid, H * D), jnp.float32) * 0.02, 'gate_w': jax.random.normal(ks[3], (H * D, hid), jnp.float32) * 0.02, 'norm_w': jnp.ones((H * D,), jnp.float32)}
    _L0_attn_a_in = _L0_attn_a_setup()

    def _L0_attn_b_setup():
        import jax, jax.numpy as jnp
        import numpy as np
        import math
        N_HEADS = 16

        def _rope_cache(seq_len, head_dim, dtype):
            half = head_dim // 2
            inv_freq = 1.0 / 10000.0 ** (jnp.arange(half, dtype=jnp.float32) / half)
            t = jnp.arange(seq_len, dtype=jnp.float32)
            freqs = jnp.einsum('t,f->tf', t, inv_freq)
            cos = jnp.repeat(jnp.cos(freqs), 2, axis=-1).astype(dtype)
            sin = jnp.repeat(jnp.sin(freqs), 2, axis=-1).astype(dtype)
            return (cos, sin)

        def _rotate_half(x):
            x1 = x[..., ::2]
            x2 = x[..., 1::2]
            return jnp.stack((-x2, x1), axis=-1).reshape(x.shape)
        key = jax.random.key(seed)
        ks = jax.random.split(key, 5)
        B, T, D = (2, 256, 256)
        s = 1.0 / math.sqrt(D)
        return {'x': jax.random.normal(ks[0], (B, T, D), dtype=jnp.float32), 'Wq': jax.random.normal(ks[1], (D, D), dtype=jnp.float32) * s, 'Wk': jax.random.normal(ks[2], (D, D), dtype=jnp.float32) * s, 'Wv': jax.random.normal(ks[3], (D, D), dtype=jnp.float32) * s, 'Wo': jax.random.normal(ks[4], (D, D), dtype=jnp.float32) * s}
    _L0_attn_b_in = _L0_attn_b_setup()

    def _L0_ffn_setup():
        import jax, jax.numpy as jnp
        import numpy as np
        B, S, H, I = (1, 64, 256, 768)

        def _quantized_matmul(x, w, scale):
            wq = w.astype(jnp.float8_e4m3fn).astype(x.dtype)
            y = jnp.einsum('bsi,io->bso', x, wq)
            return y * scale
        key = jax.random.key(seed)
        ks = jax.random.split(key, 7)
        return {'x': jax.random.normal(ks[0], (B, S, H), dtype=jnp.float32), 'gate_w': jax.random.normal(ks[1], (H, I), dtype=jnp.float32) * 0.02, 'up_w': jax.random.normal(ks[2], (H, I), dtype=jnp.float32) * 0.02, 'down_w': jax.random.normal(ks[3], (I, H), dtype=jnp.float32) * 0.02, 'gate_scale': jax.random.uniform(ks[4], (I,), dtype=jnp.float32, minval=0.5, maxval=1.5), 'up_scale': jax.random.uniform(ks[5], (I,), dtype=jnp.float32, minval=0.5, maxval=1.5), 'down_scale': jax.random.uniform(ks[6], (H,), dtype=jnp.float32, minval=0.5, maxval=1.5)}
    _L0_ffn_in = _L0_ffn_setup()
    _d = {'L0_attn_a_hidden_states': _L0_attn_a_in['hidden_states'], 'L0_attn_a_qkv_w': _L0_attn_a_in['qkv_w'], 'L0_attn_a_out_w': _L0_attn_a_in['out_w'], 'L0_attn_a_gate_w': _L0_attn_a_in['gate_w'], 'L0_attn_a_norm_w': _L0_attn_a_in['norm_w'], 'L0_attn_b_Wq': _L0_attn_b_in['Wq'], 'L0_attn_b_Wk': _L0_attn_b_in['Wk'], 'L0_attn_b_Wv': _L0_attn_b_in['Wv'], 'L0_attn_b_Wo': _L0_attn_b_in['Wo'], 'L0_ffn_gate_w': _L0_ffn_in['gate_w'], 'L0_ffn_up_w': _L0_ffn_in['up_w'], 'L0_ffn_down_w': _L0_ffn_in['down_w'], 'L0_ffn_gate_scale': _L0_ffn_in['gate_scale'], 'L0_ffn_up_scale': _L0_ffn_in['up_scale'], 'L0_ffn_down_scale': _L0_ffn_in['down_scale']}
    _x0 = _d['L0_attn_a_hidden_states']
    _d['L0_attn_a_hidden_states'] = jax.random.normal(jax.random.fold_in(jax.random.key(seed), 1), (2, 1024, 256), dtype=_x0.dtype)
    del _x0
    return _d

def reference(L0_attn_a_hidden_states, L0_attn_a_qkv_w, L0_attn_a_out_w, L0_attn_a_gate_w, L0_attn_a_norm_w, L0_attn_b_Wq, L0_attn_b_Wk, L0_attn_b_Wv, L0_attn_b_Wo, L0_ffn_gate_w, L0_ffn_up_w, L0_ffn_down_w, L0_ffn_gate_scale, L0_ffn_up_scale, L0_ffn_down_scale):

    def _L0_attn_a_ref(hidden_states, qkv_w, out_w, gate_w, norm_w):
        import jax, jax.numpy as jnp
        import numpy as np
        H = 32
        D = 64
        BS = 32
        LAYER_IDX = 0
        NUM_LAYERS = 32
        EPS = 1e-05

        def _decay_buffers():
            base = 1.0 / 2.0 ** (8.0 / H)
            rate = base ** (jnp.arange(H, dtype=jnp.float32) + 1.0)
            factor = 1.0 - LAYER_IDX / (NUM_LAYERS - 1 + 1e-05) + 1e-05
            slope = (rate * factor)[:, None, None]
            r = jnp.arange(BS, dtype=jnp.float32) + 1.0
            query_decay = jnp.exp(-slope * r[:, None])
            key_decay = jnp.exp(-slope * (BS - r[:, None]))
            dd = r[:, None] - r[None, :]
            dd = slope * dd[None, :, :]
            dd = jnp.where(dd >= 0, -dd, -jnp.inf)
            diagonal_decay = jnp.exp(dd)[None]
            block_decay = jnp.exp(-slope * BS)
            return (slope, query_decay, key_decay, diagonal_decay, block_decay)

        def _rmsnorm(x, w):
            v = jnp.mean(x.astype(jnp.float32) ** 2, axis=-1, keepdims=True)
            return (x * jax.lax.rsqrt(v + EPS)).astype(x.dtype) * w
        b, s, hid = hidden_states.shape
        nb = s // BS
        _, qd, kd, dd, bd = _decay_buffers()
        qkv = jax.nn.silu(hidden_states @ qkv_w.T)
        qkv = qkv.reshape(b, s, H, 3 * D)
        q, k, v = jnp.split(qkv, 3, axis=-1)

        def to_blocks(t):
            return t.transpose(0, 2, 1, 3).reshape(b, H, nb, BS, D).transpose(2, 0, 1, 3, 4)
        qb, kb, vb = (to_blocks(q), to_blocks(k), to_blocks(v))
        qd_ = qd[None]
        kd_ = kd[None]
        bd_ = bd[None]

        def step(state, blk):
            qi, ki, vi = blk
            aw = jnp.einsum('bhid,bhjd->bhij', qi, ki) * dd
            intra = jnp.einsum('bhij,bhjd->bhid', aw, vi)
            inter = jnp.einsum('bhid,bhde->bhie', qi * qd_, state)
            new_state = state * bd_ + jnp.einsum('bhsd,bhse->bhde', ki * kd_, vi)
            return (new_state, intra + inter)
        state0 = jnp.zeros((b, H, D, D), hidden_states.dtype)
        _, ys = jax.lax.scan(step, state0, (qb, kb, vb))
        attn = ys.transpose(1, 2, 0, 3, 4).reshape(b, H, s, D)
        attn = attn.transpose(0, 2, 1, 3).reshape(b, s, H * D)
        attn = _rmsnorm(attn, norm_w)
        gate = jax.nn.sigmoid(hidden_states @ gate_w.T)
        return gate * attn @ out_w.T

    def _L0_attn_b_ref(x, Wq, Wk, Wv, Wo):
        import jax, jax.numpy as jnp
        import numpy as np
        import math
        N_HEADS = 16

        def _rope_cache(seq_len, head_dim, dtype):
            half = head_dim // 2
            inv_freq = 1.0 / 10000.0 ** (jnp.arange(half, dtype=jnp.float32) / half)
            t = jnp.arange(seq_len, dtype=jnp.float32)
            freqs = jnp.einsum('t,f->tf', t, inv_freq)
            cos = jnp.repeat(jnp.cos(freqs), 2, axis=-1).astype(dtype)
            sin = jnp.repeat(jnp.sin(freqs), 2, axis=-1).astype(dtype)
            return (cos, sin)

        def _rotate_half(x):
            x1 = x[..., ::2]
            x2 = x[..., 1::2]
            return jnp.stack((-x2, x1), axis=-1).reshape(x.shape)
        B, T, D = x.shape
        H = N_HEADS
        hd = D // H

        def proj(W):
            return (x @ W.T).reshape(B, T, H, hd).transpose(0, 2, 1, 3)
        q, k, v = (proj(Wq), proj(Wk), proj(Wv))
        cos, sin = _rope_cache(T, hd, x.dtype)
        q = q * cos + _rotate_half(q) * sin
        k = k * cos + _rotate_half(k) * sin
        att = jnp.einsum('bhqd,bhkd->bhqk', q, k) / math.sqrt(hd)
        mask = jnp.triu(jnp.full((T, T), -jnp.inf, dtype=att.dtype), k=1)
        att = jax.nn.softmax(att + mask, axis=-1)
        out = jnp.einsum('bhqk,bhkd->bhqd', att, v)
        out = out.transpose(0, 2, 1, 3).reshape(B, T, D)
        return out @ Wo.T

    def _L0_ffn_ref(x, gate_w, up_w, down_w, gate_scale, up_scale, down_scale):
        import jax, jax.numpy as jnp
        import numpy as np
        B, S, H, I = (1, 64, 256, 768)

        def _quantized_matmul(x, w, scale):
            wq = w.astype(jnp.float8_e4m3fn).astype(x.dtype)
            y = jnp.einsum('bsi,io->bso', x, wq)
            return y * scale
        gate = jax.nn.silu(_quantized_matmul(x, gate_w, gate_scale))
        up = _quantized_matmul(x, up_w, up_scale)
        fuse = gate * up
        return _quantized_matmul(fuse, down_w, down_scale)
    x = L0_attn_a_hidden_states
    x = x + _L0_attn_a_ref(_layernorm(x, axis=-1), L0_attn_a_qkv_w, L0_attn_a_out_w, L0_attn_a_gate_w, L0_attn_a_norm_w)
    x = x + _L0_ffn_ref(_layernorm(x, axis=-1), L0_ffn_gate_w, L0_ffn_up_w, L0_ffn_down_w, L0_ffn_gate_scale, L0_ffn_up_scale, L0_ffn_down_scale)
    x = x + _L0_attn_b_ref(_layernorm(x, axis=-1), L0_attn_b_Wq, L0_attn_b_Wk, L0_attn_b_Wv, L0_attn_b_Wo)
    x = x + _L0_ffn_ref(_layernorm(x, axis=-1), L0_ffn_gate_w, L0_ffn_up_w, L0_ffn_down_w, L0_ffn_gate_scale, L0_ffn_up_scale, L0_ffn_down_scale)
    return x

_drawn_inputs = setup_inputs


def setup_inputs(seed=0):
    import zlib

    import numpy as np

    out = dict(_drawn_inputs(seed))
    spreads = {'L0_attn_a_norm_w': (1.0, 0.2)}
    factors = {'L0_ffn_gate_scale': 2.979, 'L0_ffn_up_scale': 3.481, 'L0_ffn_down_scale': 3.367}
    for name, (base, spread) in spreads.items():
        noise = np.random.default_rng([zlib.crc32(name.encode()), seed]).standard_normal(out[name].shape)
        drawn = base * np.exp(spread * noise) if base else spread * noise
        out[name] = jnp.asarray(drawn.astype(out[name].dtype))
    for name, factor in factors.items():
        out[name] = (out[name] * factor).astype(out[name].dtype)
    return out
```

```python
import concourse.bass as bass
from concourse import mybir
from contextlib import ExitStack

F32 = mybir.dt.float32
F32R = mybir.dt.float32r
BF16 = mybir.dt.bfloat16
FP8 = mybir.dt.float8e4
ALU = mybir.AluOpType
ACT = mybir.ActivationFunctionType
AXX = mybir.AxisListType.X

P = 128
BATCH, SEQ, HID = 2, 1024, 256
TOK = BATCH * SEQ
NT = TOK // P
KT = HID // P
TB = 512
NTB = TOK // TB
EPS = 1e-5

LH, LD = 32, 64
FEAT = LH * LD
NQ = LH // 4
QW = 8 * P
OFF_Q, OFF_K, OFF_G, OFF_V = 0, 2 * P, 4 * P, 6 * P
GC = 4
NU = BATCH * 2 * 2
CD, CQ, CK, CB = 0, 4 * P, 6 * P, 6 * P + 4
CW = 6 * P + 6

FI = 768
NI = FI // P

SH, SD = 16, 16
NPART = 3
SROWS = 6 * SD
MROWS = NPART
KROWS = SROWS + MROWS
HG = 4
NG = SH // HG
SCALE = SD ** -0.5


def layer_norm_transposed(nc, ctx, name, X, ident, hTh, hTl, load=None, norm=True):
    with ExitStack() as mem:
        sb = lambda n, s, d: mem.enter_context(nc.sbuf_tensor(name + n, s, d))
        sem = lambda n: ctx.enter_context(nc.semaphore(name + n))
        stats = sb("stats", [P, NT, 6], F32)
        mv = sb("mv", [P, NT, 2], F32)
        std = sb("std", [P, NT], F32)
        rstd = sb("rstd", [P, NT], F32)
        epst = sb("epst", [P, 1], F32)
        H = sb("H", [P, NT, HID], F32) if norm else X
        banks = [mem.enter_context(nc.psum_tensor(name + f"T{i}", [P, TB], F32)) for i in range(4)]
        x_in, stats_ok, mv_ok, std_ok, rstd_ok = sem("x_in"), sem("stats_ok"), sem("mv_ok"), sem("std_ok"), sem("rstd_ok")
        eps_ok, h_ok, t_ok, hi_ok, lo_ok = sem("eps_ok"), sem("h_ok"), sem("t_ok"), sem("hi_ok"), sem("lo_ok")
        NB = NTB * KT
        block = mem.enter_context(nc.Block())

        if load is not None:
            @block.sync
            def _(sp):
                sp.dma_start(ident[:], load[1]).then_inc(x_in, 16)
                for b in range(4):
                    sp.dma_start(X[:, 4 * b:4 * b + 4, :],
                                 load[0][:, 4 * b:4 * b + 4, :]).then_inc(x_in, 16)

        @block.vector
        def _(dve):
            dve.memset(epst[:], EPS).then_inc(eps_ok, 1)
            if load is not None:
                dve.wait_ge(x_in, 5 * 16)
            for t in range(NT if norm else 0):
                dve.bn_stats(stats[:, t, :], X[:, t, :]).then_inc(stats_ok, 1)
            for t in range(NT if norm else 0):
                dve.wait_ge(stats_ok, t + 1)
                dve.bn_aggr(mv[:, t, :], stats[:, t, :]).then_inc(mv_ok, 1)
            if norm:
                dve.wait_ge(std_ok, 1)
                dve.reciprocal(rstd[:], std[:]).then_inc(rstd_ok, 1)
                dve.wait_ge(rstd_ok, 1)
            for t in range(NT if norm else 0):
                dve.tensor_scalar(H[:, t, :], X[:, t, :], mv[:, t, 0:1], rstd[:, t:t + 1],
                                  ALU.subtract, ALU.mult).then_inc(h_ok, 1)
            for n in range(NB):
                tb, k = n // KT, n % KT
                dve.wait_ge(hi_ok, n + 1)
                dve.tensor_tensor(hTl[:, k, tb * TB:(tb + 1) * TB], banks[n % 4][:],
                                  hTh[:, k, tb * TB:(tb + 1) * TB].bitcast(F32),
                                  ALU.subtract).then_inc(lo_ok, 1)

        @block.scalar
        def _(act):
            act.wait_ge(eps_ok, 1)
            if norm:
                act.wait_ge(mv_ok, NT)
                act.activation(std[:], mv[:, :, 1], ACT.Sqrt, bias=epst[:]).then_inc(std_ok, 1)
            for n in range(NB):
                tb, k = n // KT, n % KT
                act.wait_ge(t_ok, n + 1)
                act.activation(hTh[:, k, tb * TB:(tb + 1) * TB], banks[n % 4][:],
                               ACT.Copy).then_inc(hi_ok, 1)

        @block.tensor
        def _(pe):
            if load is not None:
                pe.wait_ge(x_in, 5 * 16)
            for n in range(NB):
                tb, k = n // KT, n % KT
                if norm:
                    pe.wait_ge(h_ok, 4 * tb + 4)
                if n >= 4:
                    pe.wait_ge(lo_ok, n - 3)
                for j in range(4):
                    last = pe.transpose(banks[n % 4][:, j * P:(j + 1) * P],
                                        H[:, 4 * tb + j, k * P:(k + 1) * P], ident[:])
                last.then_inc(t_ok, 1)


def linear_attention(nc, ctx, X, ident, hTh, hTl, hidden, w_quads, nw_quads, c_quads):
    with ExitStack() as mem:
        sb = lambda n, s, d: mem.enter_context(nc.sbuf_tensor("la_" + n, s, d))
        sem = lambda n: ctx.enter_context(nc.semaphore("la_" + n))
        WTOT = KT * QW + 2 * HID
        WQ = KT * QW
        Wraw = sb("Wraw", [P, WTOT], F32)
        Wh = sb("Wh", [P, WTOT], F32R)
        Wl = sb("Wl", [P, WTOT], F32R)
        C = sb("C", [P, CW], F32)
        NW = sb("NW", [P, 2], F32)
        q = sb("q", [P, 2, TOK], F32)
        k = sb("k", [P, 2, TOK], F32)
        g = sb("g", [P, 2, TOK], F32)
        v = sb("v", [P, NT, 4 * LD], F32)
        acc = X
        sqacc = sb("sqacc", [P, TOK], F32)
        qd = sb("qd", [P, 2, TB], F32)
        kd = sb("kd", [P, 2, TB], F32)
        A = sb("A", [P, 2, 2, TB], F32)
        S = sb("S", [P, 4, 4, P], F32)
        y = sb("y", [P, 2, TB], F32)
        yh = sb("yh", [P, 4, TB], F32R)
        yl = sb("yl", [P, 4, TB], F32R)
        sq = sb("sq", [P, 2, TB], F32)
        ones = sb("ones", [P, 1], F32)
        epst = sb("epst", [P, 1], F32)
        std = sb("std", [P, NT], F32)
        rstd = sb("rstd", [P, NT], F32)
        pb = lambda n: mem.enter_context(nc.psum_tensor("la_" + n, [P, TB], F32))
        SC = [[pb("SA0"), pb("SB0")], [pb("SA1"), pb("SB1")]]
        PR = [SC[0][0], SC[0][1], SC[1][0], SC[1][1]]
        KB, UB, OB, RB = pb("KB"), pb("UB"), pb("OB"), pb("RB")

        w_in, c_in, x_in = sem("w_in"), sem("c_in"), sem("x_in")
        wh_ok, w_ok, wo_ok = sem("wh_ok"), sem("w_ok"), sem("wo_ok")
        init_ok, zero_ok = sem("init_ok"), sem("zero_ok")
        proj_ok, silu_ok = sem("proj_ok"), sem("silu_ok")
        sc_ok, mask_ok, kb_ok, kd_ok, qd_ok = sem("sc_ok"), sem("mask_ok"), sem("kb_ok"), sem("kd_ok"), sem("qd_ok")
        u_ok, s_link, s_ok, o_ok = sem("u_ok"), sem("s_link"), sem("s_ok"), sem("o_ok")
        sq_ok, y_ok, yh_ok, yl_ok, sqa_ok = sem("sq_ok"), sem("y_ok"), sem("yh_ok"), sem("yl_ok"), sem("sqa_ok")
        r_ok, acc_ok = sem("r_ok"), sem("acc_ok")
        ss_ok, std_ok, rstd_ok = sem("ss_ok"), sem("std_ok"), sem("rstd_ok")

        def unit(u):
            half, b, pr = u // 4, u // 2 % 2, u % 2
            return half, b, pr, b * SEQ + half * TB, b * 2 + pr

        NLINK = 2 * 2 * 2 * (4 + 3)

        block = mem.enter_context(nc.Block())

        @block.sync
        def _(sp):
            for s in (r_ok, o_ok, y_ok, kd_ok, u_ok, sqa_ok, yl_ok, acc_ok, s_ok, sq_ok, mask_ok):
                sp.sem_inc(s, 1)
            sp.dma_start(Wraw[:], w_quads[0, :, :]).then_inc(w_in, 16)
            sp.dma_start(C[:], c_quads[0, :, :]).then_inc(c_in, 16)
            sp.dma_start(NW[:], nw_quads[0, :, :]).then_inc(c_in, 16)
            for i in range(1, NQ):
                sp.wait_ge(wo_ok, i)
                sp.dma_start(Wraw[:], w_quads[i, :, :]).then_inc(w_in, 16)
                sp.wait_ge(kd_ok, 16 * i + 1)
                sp.wait_ge(qd_ok, 8 * i)
                sp.wait_ge(y_ok, 8 * i + 1)
                sp.wait_ge(s_ok, 8 * i + 1)
                sp.dma_start(C[:], c_quads[i, :, :]).then_inc(c_in, 16)
                sp.dma_start(NW[:], nw_quads[i, :, :]).then_inc(c_in, 16)
            sp.wait_ge(sc_ok, 8 * NQ)
            sp.wait_ge(qd_ok, 8 * NQ)
            sp.dma_start(q[:].rearrange("p a n -> p (a n)"), hidden.rearrange("p t n -> p (t n)")).then_inc(x_in, 16)

        @block.gpsimd
        def _(pool):
            pool.memset(acc[:], 0.0).then_inc(init_ok, 1)
            pool.memset(sqacc[:], 0.0).then_inc(init_ok, 1)
            pool.memset(ones[:], 1.0).then_inc(init_ok, 1)
            pool.memset(epst[:], EPS).then_inc(init_ok, 1)
            pool.memset(S[:], 0.0).then_inc(zero_ok, 1)

            pool.wait_ge(wh_ok, 1)
            pool.tensor_tensor(Wl[:, 0:WQ], Wraw[:, 0:WQ], Wh[:, 0:WQ].bitcast(F32),
                               ALU.subtract).then_inc(w_ok, 1)

            def quad(i, last):
                pool.wait_ge(wh_ok, 2 * i + 2)
                pool.tensor_tensor(Wl[:, WQ:WTOT], Wraw[:, WQ:WTOT], Wh[:, WQ:WTOT].bitcast(F32),
                                   ALU.subtract).then_inc(wo_ok, 1)
                pool.wait_ge(silu_ok, 32 * i + 8)
                pool.wait_ge(c_in, 32 * i + 32)
                for u in range(NU + 1):
                    if u < NU:
                        half, b, pr, col, ch = unit(u)
                        if u >= 2:
                            pool.wait_ge(o_ok, 8 * i + u)
                        else:
                            pool.wait_ge(o_ok, 8 * i + 1)
                        pool.tensor_tensor(
                            qd[:, u % 2, :].rearrange("p (c t) -> p c t", c=GC),
                            q[:, pr, col:col + TB].rearrange("p (c t) -> p c t", c=GC),
                            C[:, CQ + pr * P:CQ + (pr + 1) * P].unsqueeze(1).broadcast_to([P, GC, P]),
                            ALU.mult).then_inc(qd_ok, 1)
                    if u == 4 and not last:
                        pool.wait_ge(wh_ok, 2 * i + 3)
                        pool.tensor_tensor(Wl[:, 0:WQ], Wraw[:, 0:WQ], Wh[:, 0:WQ].bitcast(F32),
                                           ALU.subtract).then_inc(w_ok, 1)
                    if u >= 1:
                        w = u - 1
                        half, b, pr, col, ch = unit(w)
                        pool.wait_ge(yh_ok, 8 * i + w + 1)
                        if w >= 4:
                            pool.wait_ge(r_ok, 8 * i + 2 * (w // 2) - 1)
                        else:
                            pool.wait_ge(r_ok, 8 * i + 1)
                        pool.tensor_tensor(yl[:, w % 4, :], y[:, w % 2, :], yh[:, w % 4, :].bitcast(F32),
                                           ALU.subtract).then_inc(yl_ok, 1)
                        pool.wait_ge(sq_ok, 8 * i + w + 2)
                        if w == 0:
                            pool.wait_ge(init_ok, 4)
                        pool.wait_ge(sqa_ok, 8 * i + w + 1)
                        pool.tensor_tensor(sqacc[:, col:col + TB], sqacc[:, col:col + TB], sq[:, w % 2, :],
                                           ALU.add).then_inc(sqa_ok, 1)

            with pool.Fori(0, NQ - 1) as i:
                quad(i, False)
            quad(NQ - 1, True)

        @block.scalar
        def _(act):
            def quad(i):
                for n in range(32):
                    act.wait_ge(proj_ok, 32 * i + n + 1)
                    bank = PR[n % 4]
                    if n < 16:
                        pr, tb = n // 4 % 2, n % 4
                        dst = (q if n < 8 else k)[:, pr, tb * TB:(tb + 1) * TB]
                        act.activation(dst, bank[:], ACT.Silu).then_inc(silu_ok, 1)
                    elif n < 24:
                        t = 2 * (n - 16)
                        act.activation(v[:, t:t + 2, :], bank[:].rearrange("p (t n) -> p t n", t=2),
                                       ACT.Silu).then_inc(silu_ok, 1)
                    else:
                        if n == 24:
                            act.wait_ge(y_ok, 8 * i + 1)
                        pr, tb = n // 4 % 2, n % 4
                        act.activation(g[:, pr, tb * TB:(tb + 1) * TB], bank[:],
                                       ACT.Sigmoid).then_inc(silu_ok, 1)
                act.wait_ge(c_in, 32 * i + 32)

                def keys(u):
                    half, b, pr, col, ch = unit(u)
                    act.wait_ge(kb_ok, 8 * i + u + 1)
                    if u >= 2:
                        act.wait_ge(u_ok, 8 * i + u)
                    else:
                        act.wait_ge(u_ok, 8 * i + 1)
                    kdv = kd[:, u % 2, :].rearrange("p (c n) -> p c n", c=GC)
                    kbv = KB[:].rearrange("p (c n) -> p c n", c=GC)
                    for h in range(2):
                        act.activation(kdv[:, :, h * LD:(h + 1) * LD], kbv[:, :, h * LD:(h + 1) * LD],
                                       ACT.Copy, scale=C[:, CK + 2 * pr + h:CK + 2 * pr + h + 1]
                                       ).then_inc(kd_ok, 1)

                keys(0)
                for u in range(NU):
                    if u + 1 < NU:
                        keys(u + 1)
                    act.wait_ge(y_ok, 8 * i + u + 2)
                    if u >= 2:
                        act.wait_ge(sqa_ok, 8 * i + u)
                    else:
                        act.wait_ge(sqa_ok, 8 * i + 1)
                    act.activation(sq[:, u % 2, :], OB[:], ACT.Square).then_inc(sq_ok, 1)
                    if u >= 4:
                        act.wait_ge(r_ok, 8 * i + 2 * (u // 2) - 1)
                    else:
                        act.wait_ge(r_ok, 8 * i + 1)
                    act.activation(yh[:, u % 4, :], y[:, u % 2, :], ACT.Copy).then_inc(yh_ok, 1)

            with act.Fori(0, NQ) as i:
                quad(i)
            act.wait_ge(init_ok, 4)
            act.wait_ge(ss_ok, 1)
            act.activation(std[:], KB[:, 0:NT], ACT.Sqrt, bias=epst[:], scale=1.0 / FEAT).then_inc(std_ok, 1)

        @block.vector
        def _(dve):
            dve.wait_ge(zero_ok, 1)
            dve.wait_ge(init_ok, 4)

            def high(a, b):
                dve.tensor_copy(Wh[:, a:b], Wraw[:, a:b]).then_inc(wh_ok, 1)

            dve.wait_ge(w_in, 16)
            high(0, WQ)

            def quad(i, last):
                link = [0]
                dve.wait_ge(r_ok, 8 * i + 1)
                high(WQ, WTOT)

                def masks(u):
                    half, b, pr, col, ch = unit(u)
                    dve.wait_ge(sc_ok, 8 * i + u + 1)
                    if u >= 2:
                        dve.wait_ge(o_ok, 8 * i + u)
                    else:
                        dve.wait_ge(o_ok, 8 * i + 1)
                    for h in range(2):
                        d = C[:, CD + (2 * pr + h) * P:CD + (2 * pr + h + 1) * P]
                        dve.tensor_tensor(A[:, u % 2, h, :].rearrange("p (c t) -> p c t", c=GC),
                                          SC[u % 2][h][:].rearrange("p (c t) -> p c t", c=GC),
                                          d.unsqueeze(1).broadcast_to([P, GC, P]),
                                          ALU.mult).then_inc(mask_ok, 1)

                def states(u):
                    half, b, pr, col, ch = unit(u)
                    dve.wait_ge(u_ok, 8 * i + u + 2)
                    cs = range(4 * half, 4 * half + (4 if half == 0 else 3))
                    for c in cs:
                        if link[0] or c > 0:
                            dve.wait_ge(s_link, NLINK * i + link[0])
                        for h in range(2):
                            r = slice(h * LD, (h + 1) * LD)
                            U = UB[r, (c % 4) * P + h * LD:(c % 4) * P + (h + 1) * LD]
                            new = S[r, ch, c % 4, h * LD:(h + 1) * LD]
                            if c == 0:
                                ins = dve.tensor_copy(new, U)
                            else:
                                ins = dve.scalar_tensor_tensor(
                                    new, S[r, ch, (c - 1) % 4, h * LD:(h + 1) * LD],
                                    C[r, CB + pr:CB + pr + 1], U, ALU.mult, ALU.add)
                            ins.then_inc(s_link, 1)
                            link[0] += 1
                    dve.wait_ge(s_link, NLINK * i + link[0])
                    dve.sem_inc(s_ok, 1)

                def gated(u):
                    half, b, pr, col, ch = unit(u)
                    dve.wait_ge(o_ok, 8 * i + u + 2)
                    if u >= 2:
                        dve.wait_ge(yl_ok, 8 * i + u)
                    else:
                        dve.wait_ge(yl_ok, 8 * i + 1)
                    dve.scalar_tensor_tensor(y[:, u % 2, :], OB[:], NW[:, pr:pr + 1], g[:, pr, col:col + TB],
                                             ALU.mult, ALU.mult).then_inc(y_ok, 1)

                def sums(m):
                    half, b, _, col, _ = unit(2 * (m // 2))
                    t = col // P + 2 * (m % 2)
                    dve.wait_ge(r_ok, 8 * i + m + 2)
                    dve.wait_ge(acc_ok, 8 * i + m + 1)
                    dve.tensor_tensor(acc[:, t:t + 2, :], RB[:].rearrange("p (t n) -> p t n", t=2),
                                      acc[:, t:t + 2, :], ALU.add).then_inc(acc_ok, 1)

                dve.wait_ge(c_in, 32 * i + 32)
                masks(0)
                for u in range(NU):
                    states(u)
                    if u + 1 < NU:
                        masks(u + 1)
                    gated(u)
                    if u == 2 and not last:
                        dve.wait_ge(w_in, 16 * i + 32)
                        high(0, WQ)
                    if u >= 2:
                        sums(u - 2)
                sums(NU - 2)
                sums(NU - 1)
                assert link[0] == NLINK

            with dve.Fori(0, NQ - 1) as i:
                quad(i, False)
            quad(NQ - 1, True)
            dve.wait_ge(std_ok, 1)
            dve.reciprocal(rstd[:], std[:]).then_inc(rstd_ok, 1)
            dve.wait_ge(rstd_ok, 1)
            dve.wait_ge(acc_ok, 8 * NQ + 1)
            dve.wait_ge(x_in, 16)
            xin = q[:].rearrange("p a n -> p (a n)").rearrange("p (t n) -> p t n", t=NT)
            for t in range(NT):
                dve.scalar_tensor_tensor(X[:, t, :], acc[:, t, :], rstd[:, t:t + 1], xin[:, t, :],
                                         ALU.mult, ALU.add)

        @block.tensor
        def _(pe):
            def products(out, pairs, first, last, check):
                m = None
                for n, (a, b) in enumerate(pairs):
                    m = pe.matmul(out, a, b, start=first and n == 0, stop=last and n == len(pairs) - 1,
                                  skip_group_check=check)
                return m

            def quad(i):
                pe.wait_ge(w_ok, i + 1)
                wv = [w[:, 0:WQ].rearrange("p (k n) -> p k n", k=KT) for w in (Wh, Wl)]
                for n in range(32):
                    if n < 4:
                        pe.wait_ge(mask_ok, 16 * i + 1)
                    else:
                        pe.wait_ge(silu_ok, 32 * i + n - 3)
                    bank = PR[n % 4]
                    if n < 16 or n >= 24:
                        off = (OFF_Q if n < 8 else OFF_K if n < 16 else OFF_G) + P * (n // 4 % 2)
                        tb = n % 4
                        pairs = []
                        for kt in range(KT):
                            hi, lo = (h[:, kt, tb * TB:(tb + 1) * TB] for h in (hTh, hTl))
                            a, c = (w[:, kt, off:off + P] for w in wv)
                            pairs += [(a, hi), (a, lo), (c, hi)]
                        m = products(bank[:], pairs, True, True, False)
                    else:
                        for j in range(2):
                            t = 2 * (n - 16) + j
                            pairs = []
                            for kt in range(KT):
                                hi, lo = (h[:, kt, t * P:(t + 1) * P] for h in (hTh, hTl))
                                a, c = (w[:, kt, OFF_V:OFF_V + 4 * LD] for w in wv)
                                pairs += [(hi, a), (hi, c), (lo, a)]
                            m = products(bank[:, j * HID:(j + 1) * HID], pairs, True, True, False)
                    m.then_inc(proj_ok, 1)

                def scores(u):
                    half, b, pr, col, ch = unit(u)
                    if u < 2:
                        pe.wait_ge(silu_ok, 32 * i + 32)
                    else:
                        pe.wait_ge(mask_ok, 16 * i + 2 * u - 1)
                    for c in range(GC):
                        cc = slice(col + c * P, col + (c + 1) * P)
                        for h in range(2):
                            r = slice(h * LD, (h + 1) * LD)
                            m = pe.matmul(SC[u % 2][h][:, c * P:(c + 1) * P], k[r, pr, cc], q[r, pr, cc],
                                          start=True, stop=True)
                    m.then_inc(sc_ok, 1)
                    pe.wait_ge(kd_ok, 16 * i + 2 * u + 1)
                    for c in range(GC):
                        m = pe.transpose(KB[:, c * P:(c + 1) * P], k[:, pr, col + c * P:col + (c + 1) * P],
                                         ident[:])
                    m.then_inc(kb_ok, 1)

                def state_sums(u):
                    half, b, pr, col, ch = unit(u)
                    pe.wait_ge(kd_ok, 16 * i + 2 * u + 3)
                    pe.wait_ge(s_ok, 8 * i + u + 1)
                    for c in range(GC):
                        t = col // P + c
                        m = pe.matmul(UB[:, c * P:(c + 1) * P], kd[:, u % 2, c * P:(c + 1) * P],
                                      v[:, t, pr * P:(pr + 1) * P], start=True, stop=True)
                    m.then_inc(u_ok, 1)

                def outputs(u):
                    half, b, pr, col, ch = unit(u)
                    pe.wait_ge(s_ok, 8 * i + u + 2)
                    pe.wait_ge(qd_ok, 8 * i + u + 1)
                    pe.wait_ge(mask_ok, 16 * i + 2 * u + 3)
                    pe.wait_ge(sq_ok, 8 * i + u + 1)
                    c0 = 1 if half == 0 else 0
                    for c in range(c0, GC):
                        pe.matmul(OB[:, c * P:(c + 1) * P], S[:, ch, (4 * half + c - 1) % 4, :],
                                  qd[:, u % 2, c * P:(c + 1) * P], start=c == c0, stop=False,
                                  skip_group_check=True)
                    for c in range(GC):
                        t = col // P + c
                        for h in range(2):
                            r = slice(h * LD, (h + 1) * LD)
                            m = pe.matmul(OB[r, c * P:(c + 1) * P], v[:, t, pr * P + h * LD:pr * P + (h + 1) * LD],
                                          A[:, u % 2, h, c * P:(c + 1) * P], start=False, stop=c == GC - 1,
                                          skip_group_check=True)
                    m.then_inc(o_ok, 1)

                def out_projection(mm):
                    base = 2 * (mm // 2)
                    pe.wait_ge(yl_ok, 8 * i + base + 3)
                    pe.wait_ge(acc_ok, 8 * i + mm + 1)
                    if mm == 0:
                        pe.wait_ge(wo_ok, i + 1)
                    for j in range(2):
                        cols = slice((2 * (mm % 2) + j) * P, (2 * (mm % 2) + j + 1) * P)
                        pairs = []
                        for pr in range(2):
                            hi, lo = (z[:, (base + pr) % 4, cols] for z in (yh, yl))
                            a, c = (w[:, WQ + pr * HID:WQ + (pr + 1) * HID] for w in (Wh, Wl))
                            pairs += [(hi, a), (hi, c), (lo, a)]
                        m = products(RB[:, j * HID:(j + 1) * HID], pairs, True, True, False)
                    m.then_inc(r_ok, 1)

                scores(0)
                for u in range(NU):
                    state_sums(u)
                    if u + 1 < NU:
                        scores(u + 1)
                    outputs(u)
                    if u >= 2:
                        out_projection(u - 2)
                out_projection(NU - 2)
                out_projection(NU - 1)

            with pe.Fori(0, NQ) as i:
                quad(i)
            pe.wait_ge(sqa_ok, 8 * NQ + 1)
            pe.wait_ge(init_ok, 4)
            for t in range(NT):
                m = pe.matmul(KB[:, t:t + 1], sqacc[:, t * P:(t + 1) * P], ones[:], start=True, stop=True)
            m.then_inc(ss_ok, 1)


def ffn(nc, ctx, name, X, hTh, hTl, WF, SCL, DS, out=None):
    with ExitStack() as mem:
        sb = lambda n, s, d: mem.enter_context(nc.sbuf_tensor(name + n, s, d))
        sem = lambda n: ctx.enter_context(nc.semaphore(name + n))
        pb = lambda n: mem.enter_context(nc.psum_tensor(name + n, [P, TB], F32))
        sg = sb("sg", [P, 2, TB], F32)
        f = sb("f", [P, 2, TB], F32)
        fh = sb("fh", [P, 2, NI, TB], F32R)
        fl = sb("fl", [P, 2, NI, TB], F32R)
        o = sb("o", [P, 2, 2, HID], F32)
        GB, UB, DB = [pb("G0"), pb("G1")], [pb("U0"), pb("U1")], [pb("D0"), pb("D1")]
        g_ok, u_ok, sg_ok, f_ok, fh_ok, fl_ok = sem("g_ok"), sem("u_ok"), sem("sg_ok"), sem("f_ok"), sem("fh_ok"), sem("fl_ok")
        d_ok, o_ok, x_ok, st_ok = sem("d_ok"), sem("o_ok"), sem("x_ok"), sem("st_ok")
        wg = WF[:, 0:KT * FI].rearrange("p (k n) -> p k n", k=KT)
        wu = WF[:, KT * FI:2 * KT * FI].rearrange("p (k n) -> p k n", k=KT)
        wd = WF[:, 2 * KT * FI:].rearrange("p (k n) -> p k n", k=NI)
        block = mem.enter_context(nc.Block())

        @block.tensor
        def _(pe):
            def up(tb):
                for it in range(NI):
                    n = tb * NI + it
                    if n >= 2:
                        pe.wait_ge(sg_ok, n - 1)
                        pe.wait_ge(f_ok, n - 1)
                    for w, bank, done in ((wg, GB[n % 2], g_ok), (wu, UB[n % 2], u_ok)):
                        for kt in range(KT):
                            a = w[:, kt, it * P:(it + 1) * P]
                            pe.matmul(bank[:], a, hTh[:, kt, tb * TB:(tb + 1) * TB], start=kt == 0, stop=False)
                            m = pe.matmul(bank[:], a, hTl[:, kt, tb * TB:(tb + 1) * TB], start=False,
                                          stop=kt == KT - 1)
                        m.then_inc(done, 1)

            def down(tb):
                pe.wait_ge(fl_ok, (tb + 1) * NI)
                for half in range(2):
                    n = 2 * tb + half
                    if n >= 2:
                        pe.wait_ge(o_ok, n - 1)
                    for j in range(2):
                        c = slice((2 * half + j) * P, (2 * half + j + 1) * P)
                        for it in range(NI):
                            pe.matmul(DB[n % 2][:, j * HID:(j + 1) * HID], fh[:, tb % 2, it, c], wd[:, it, :],
                                      start=it == 0, stop=False)
                            m = pe.matmul(DB[n % 2][:, j * HID:(j + 1) * HID], fl[:, tb % 2, it, c],
                                          wd[:, it, :], start=False, stop=it == NI - 1)
                    m.then_inc(d_ok, 1)

            up(0)
            for tb in range(NTB):
                if tb + 1 < NTB:
                    up(tb + 1)
                down(tb)

        @block.scalar
        def _(act):
            def high(n):
                tb, it = n // NI, n % NI
                act.wait_ge(f_ok, n + 1)
                if tb >= 2:
                    act.wait_ge(d_ok, 2 * (tb - 1))
                act.activation(fh[:, tb % 2, it, :], f[:, n % 2, :], ACT.Copy).then_inc(fh_ok, 1)

            for n in range(NTB * NI):
                act.wait_ge(g_ok, n + 1)
                if n >= 2:
                    act.wait_ge(f_ok, n - 1)
                act.activation(sg[:, n % 2, :], GB[n % 2][:], ACT.Silu,
                               scale=SCL[:, n % NI:n % NI + 1]).then_inc(sg_ok, 1)
                if n >= 1:
                    high(n - 1)
            high(NTB * NI - 1)

        @block.vector
        def _(dve):
            def scaled(n):
                dve.wait_ge(d_ok, n + 1)
                if n >= 2:
                    dve.wait_ge(x_ok, n - 1)
                dve.tensor_tensor(o[:, n % 2, :, :], DB[n % 2][:].rearrange("p (t n) -> p t n", t=2),
                                  DS[:].unsqueeze(1).broadcast_to([P, 2, HID]), ALU.mult).then_inc(o_ok, 1)

            for n in range(NTB * NI):
                tb, it = n // NI, n % NI
                dve.wait_ge(sg_ok, n + 1)
                dve.wait_ge(u_ok, n + 1)
                if n >= 2:
                    dve.wait_ge(fl_ok, n - 1)
                dve.scalar_tensor_tensor(f[:, n % 2, :], UB[n % 2][:], SCL[:, NI + it:NI + it + 1],
                                         sg[:, n % 2, :], ALU.mult, ALU.mult).then_inc(f_ok, 1)
                if tb >= 1 and it == NI - 1:
                    scaled(2 * (tb - 1))
                    scaled(2 * (tb - 1) + 1)
            scaled(2 * NTB - 2)
            scaled(2 * NTB - 1)

        @block.gpsimd
        def _(pool):
            def add(n):
                pool.wait_ge(o_ok, n + 1)
                pool.tensor_tensor(X[:, 2 * n:2 * n + 2, :], X[:, 2 * n:2 * n + 2, :], o[:, n % 2, :, :],
                                   ALU.add).then_inc(x_ok, 1)

            for n in range(NTB * NI):
                tb, it = n // NI, n % NI
                pool.wait_ge(fh_ok, n + 1)
                if tb >= 2:
                    pool.wait_ge(d_ok, 2 * (tb - 1))
                pool.tensor_tensor(fl[:, tb % 2, it, :], f[:, n % 2, :], fh[:, tb % 2, it, :].bitcast(F32),
                                   ALU.subtract).then_inc(fl_ok, 1)
                if tb >= 1 and it == NI - 1:
                    add(2 * (tb - 1))
                    add(2 * (tb - 1) + 1)
            add(2 * NTB - 2)
            add(2 * NTB - 1)

        if out is not None:
            @block.sync
            def _(sp):
                for n in range(2 * NTB):
                    sp.wait_ge(x_ok, n + 1)
                    sp.dma_start(out[:, 2 * n:2 * n + 2, :], X[:, 2 * n:2 * n + 2, :]).then_inc(st_ok, 16)
                sp.wait_ge(st_ok, 16 * 2 * NTB)


def quantised_weights(nc, ctx, w_ffn, s_ffn, d_ffn, WF, SCL, DS):
    with ExitStack() as mem:
        sb = lambda n, s, d: mem.enter_context(nc.sbuf_tensor("qw_" + n, s, d))
        sem = lambda n: ctx.enter_context(nc.semaphore("qw_" + n))
        N = (2 * KT * FI + NI * HID)
        w = sb("w", [P, N], F32)
        c = sb("c", [P, N], F32)
        e = sb("e", [P, N], FP8)
        wh8 = sb("wh8", [P, N], FP8)
        ch8 = sb("ch8", [P, N], FP8)
        d = sb("d", [P, N], F32)
        z = sb("z", [P, N], F32)
        lim = sb("lim", [P, 1], F32)
        w_in, c_ok, e_ok, h_ok, z_ok, d_ok, q_ok, l_ok = (sem(n) for n in
            ("w_in", "c_ok", "e_ok", "h_ok", "z_ok", "d_ok", "q_ok", "l_ok"))
        block = mem.enter_context(nc.Block())

        @block.sync
        def _(sp):
            sp.dma_start(w[:], w_ffn).then_inc(w_in, 16)
            sp.dma_start(SCL[:], s_ffn).then_inc(w_in, 16)
            sp.dma_start(DS[:], d_ffn).then_inc(w_in, 16)

        @block.scalar
        def _(act):
            act.wait_ge(w_in, 48)
            act.activation(wh8[:], w[:], ACT.Copy, scale=0.5, saturate=False).then_inc(h_ok, 1)
            act.wait_ge(c_ok, 1)
            act.activation(ch8[:], c[:], ACT.Copy, scale=0.5, saturate=False).then_inc(h_ok, 1)
            act.activation(e[:], c[:], ACT.Copy, saturate=False).then_inc(e_ok, 1)
            act.activation(z[:], w[:], ACT.Abs).then_inc(z_ok, 1)
            act.wait_ge(l_ok, 1)
            act.wait_ge(z_ok, 1)
            act.activation(z[:], z[:], ACT.Relu, bias=lim[:]).then_inc(z_ok, 1)

        @block.gpsimd
        def _(pool):
            pool.wait_ge(h_ok, 2)
            pool.tensor_tensor(d[:], wh8[:], ch8[:], ALU.subtract).then_inc(d_ok, 1)

        @block.vector
        def _(dve):
            dve.memset(lim[:], -464.0).then_inc(l_ok, 1)
            dve.wait_ge(w_in, 48)
            dve.tensor_scalar(c[:], w[:], 128.0, -128.0, ALU.min, ALU.max).then_inc(c_ok, 1)
            dve.wait_ge(z_ok, 2)
            dve.tensor_scalar(z[:], z[:], 3e38, 3e38, ALU.mult, ALU.mult).then_inc(z_ok, 1)
            dve.wait_ge(e_ok, 1)
            dve.wait_ge(z_ok, 3)
            dve.scalar_tensor_tensor(z[:], z[:], 0.0, e[:], ALU.mult, ALU.add).then_inc(z_ok, 1)
            dve.wait_ge(d_ok, 1)
            dve.wait_ge(z_ok, 4)
            dve.scalar_tensor_tensor(WF[:], d[:], 2.0, z[:], ALU.mult, ALU.add).then_inc(q_ok, 1)


def rotary_projections(nc, ctx, hTh, hTl, w_att, rope, QP, KP, V, WOh, WOl):
    with ExitStack() as mem:
        sb = lambda n, s, d: mem.enter_context(nc.sbuf_tensor("rp_" + n, s, d))
        sem = lambda n: ctx.enter_context(nc.semaphore("rp_" + n))
        pb = lambda n: mem.enter_context(nc.psum_tensor("rp_" + n, [P, TB], F32))
        NW5 = KT * 5 * HID
        Wh = sb("Wh", [P, NW5], F32R)
        Wl = sb("Wl", [P, NW5], F32R)
        WQ5 = KT * 6 * HID
        Wraw = sb("Wraw", [P, WQ5], F32)
        CS = sb("CS", [P, 2, SEQ], F32)
        t1 = sb("t1", [P, 2, TB], F32)
        t2 = sb("t2", [P, 2, TB], F32)
        r = sb("r", [P, 2, TB], F32)
        QB, SB_, VB = [pb("Q0"), pb("Q1")], [pb("S0"), pb("S1")], [pb("V0"), pb("V1")]
        w_in, h_ok, l_ok, v0_ok = sem("w_in"), sem("h_ok"), sem("l_ok"), sem("v0_ok")
        p_ok, m_ok, a_ok, p1_ok, r1_ok, p2_ok, p3_ok = (sem(n) for n in
            ("p_ok", "m_ok", "a_ok", "p1_ok", "r1_ok", "p2_ok", "p3_ok"))
        vb_ok, ve_ok = sem("vb_ok"), sem("ve_ok")
        steps = [(dst, x, mt, tb) for x, dst in ((0, QP), (2, KP)) for mt in range(2) for tb in range(NTB)]
        NS = len(steps)
        col = lambda w, kt, x, mt: w[:, (kt * 5 + x) * HID + mt * P:(kt * 5 + x) * HID + (mt + 1) * P]
        block = mem.enter_context(nc.Block())

        @block.sync
        def _(sp):
            sp.dma_start(Wraw[:], w_att).then_inc(w_in, 16)
            sp.dma_start(CS[:], rope).then_inc(w_in, 16)

        @block.tensor
        def _(pe):
            pe.wait_ge(l_ok, 2)
            for n, (dst, x, mt, tb) in enumerate(steps):
                if n >= 2:
                    pe.wait_ge(m_ok, 2 * (n - 1))
                for s, bank in ((x, QB[n % 2]), (x + 1, SB_[n % 2])):
                    for kt in range(KT):
                        hi, lo = (h[:, kt, tb * TB:(tb + 1) * TB] for h in (hTh, hTl))
                        a, c = col(Wh, kt, s, mt), col(Wl, kt, s, mt)
                        pe.matmul(bank[:], a, hi, start=kt == 0, stop=False)
                        pe.matmul(bank[:], a, lo, start=False, stop=False)
                        m = pe.matmul(bank[:], c, hi, start=False, stop=kt == KT - 1)
                m.then_inc(p_ok, 1)
            for n in range(NT // 2):
                if n >= 2:
                    pe.wait_ge(ve_ok, n - 1)
                for j in range(2):
                    t = 2 * n + j
                    for kt in range(KT):
                        hi, lo = (h[:, kt, t * P:(t + 1) * P] for h in (hTh, hTl))
                        a, c = (w[:, (kt * 5 + 4) * HID:(kt * 5 + 5) * HID] for w in (Wh, Wl))
                        o = VB[n % 2][:, j * HID:(j + 1) * HID]
                        pe.matmul(o, hi, a, start=kt == 0, stop=False)
                        pe.matmul(o, hi, c, start=False, stop=False)
                        m = pe.matmul(o, lo, a, start=False, stop=kt == KT - 1)
                m.then_inc(vb_ok, 1)

        @block.vector
        def _(dve):
            dve.memset(V[:], 0.0).then_inc(v0_ok, 1)
            dve.wait_ge(v0_ok, 1)
            dve.memset(V[:, :, :, SD:SD + 1], 1.0).then_inc(v0_ok, 1)
            for n, (dst, x, mt, tb) in enumerate(steps):
                dve.wait_ge(p_ok, n + 1)
                if n >= 2:
                    dve.wait_ge(p3_ok, n - 1)
                c = (tb % 2) * TB
                dve.tensor_tensor(t1[:, n % 2, :], QB[n % 2][:], CS[:, 0, c:c + TB], ALU.mult).then_inc(m_ok, 1)
                dve.tensor_tensor(t2[:, n % 2, :], SB_[n % 2][:], CS[:, 1, c:c + TB], ALU.mult).then_inc(m_ok, 1)

        @block.scalar
        def _(act):
            act.wait_ge(w_in, 32)
            act.activation(Wh[:], Wraw[:, 0:NW5], ACT.Copy).then_inc(h_ok, 1)
            act.activation(WOh[:], Wraw[:, NW5:WQ5], ACT.Copy).then_inc(h_ok, 1)
            for n, (dst, x, mt, tb) in enumerate(steps):
                c = slice(tb * TB, (tb + 1) * TB)
                act.wait_ge(a_ok, n + 1)
                act.activation(dst[:, 0, mt, c], t1[:, n % 2, :], ACT.Copy).then_inc(p1_ok, 1)
                act.wait_ge(r1_ok, n + 1)
                act.activation(dst[:, 1, mt, c], r[:, n % 2, :], ACT.Copy).then_inc(p2_ok, 1)
            act.wait_ge(v0_ok, 2)
            for n in range(NT // 2):
                act.wait_ge(vb_ok, n + 1)
                act.activation(V[:, 2 * n:2 * n + 2, :, 0:SD],
                               VB[n % 2][:].rearrange("p (t h d) -> p t h d", t=2, h=SH),
                               ACT.Copy).then_inc(ve_ok, 1)

        @block.gpsimd
        def _(pool):
            pool.wait_ge(h_ok, 2)
            pool.tensor_tensor(Wl[:], Wraw[:, 0:NW5], Wh[:].bitcast(F32), ALU.subtract).then_inc(l_ok, 1)
            pool.tensor_tensor(WOl[:], Wraw[:, NW5:WQ5], WOh[:].bitcast(F32), ALU.subtract).then_inc(l_ok, 1)
            for n, (dst, x, mt, tb) in enumerate(steps):
                c = slice(tb * TB, (tb + 1) * TB)
                pool.wait_ge(m_ok, 2 * n + 2)
                pool.tensor_tensor(t1[:, n % 2, :], t1[:, n % 2, :], t2[:, n % 2, :], ALU.add).then_inc(a_ok, 1)
                pool.wait_ge(p1_ok, n + 1)
                pool.tensor_tensor(r[:, n % 2, :], t1[:, n % 2, :], dst[:, 0, mt, c], ALU.subtract).then_inc(r1_ok, 1)
                pool.wait_ge(p2_ok, n + 1)
                pool.tensor_tensor(dst[:, 2, mt, c], r[:, n % 2, :], dst[:, 1, mt, c], ALU.subtract).then_inc(p3_ok, 1)


def causal_attention(nc, ctx, ident, masks_in, QP, KP, V, ATT):
    with ExitStack() as mem:
        sb = lambda n, s, d: mem.enter_context(nc.sbuf_tensor("ca_" + n, s, d))
        sem = lambda n: ctx.enter_context(nc.semaphore("ca_" + n))
        QS = [sb(f"QS{i}", [P, HG, SEQ], BF16) for i in range(2)]
        KS = [sb(f"KS{i}", [P, HG, SEQ], BF16) for i in range(2)]
        VG = [sb(f"VG{i}", [P, SEQ // P, HG, 32], F32) for i in range(2)]
        MK = sb("MK", [P, 3, P], BF16)
        MKf = sb("MKf", [P, 3, P], F32)
        PT = sb("PT", [P, 2, HG, TB], F32)
        mx = sb("mx", [P, HG, 8, 2], F32)
        m = sb("m", [P, 8, HG], F32)
        mr = sb("mr", [P, 2, 8, HG], F32)
        NM = sb("NM", [P, 8, HG, MROWS], BF16)
        MT = [sb(f"MT{i}", [HG * MROWS, SEQ], BF16) for i in range(2)]
        OT = sb("OT", [P, 2, TB], F32)
        rec = sb("rec", [P, 4, HG], F32)
        pb = lambda n, w=TB: mem.enter_context(nc.psum_tensor("ca_" + n, [P, w], F32))
        S1 = [pb("S10"), pb("S11")]
        ST = [pb("ST0", 2 * TB), pb("ST1", 2 * TB)]
        OB, AUX = pb("OB"), pb("AUX")
        AUXB = AUX[:].bitcast(BF16)
        mk_in, mk_ok, init_ok, one_ok = sem("mk_in"), sem("mk_ok"), sem("init_ok"), sem("one_ok")
        sq_in = [[sem(f"sq_in{b}{i}") for i in range(2)] for b in range(2)]
        sk_in = [[sem(f"sk_in{b}{i}") for i in range(2)] for b in range(2)]
        sp_in = [[sem(f"sp_in{b}{i}") for i in range(2)] for b in range(2)]
        v_in = [sem("v_in0"), sem("v_in1")]
        mr_in = [sem("mr_in0"), sem("mr_in1")]
        s1_ok, mx_ok, ch_ok, nm_ok, mt_ok, mtc_ok = (sem(n) for n in ("s1_ok", "mx_ok", "ch_ok", "nm_ok", "mt_ok", "mtc_ok"))
        st_ok, exp_ok, pv_ok, oc_ok, t_ok, rec_ok, nrm_ok = (sem(n) for n in
            ("st_ok", "exp_ok", "pv_ok", "oc_ok", "t_ok", "rec_ok", "nrm_ok"))
        QI, KI = (0, 0, 0, 1, 1, 2), (0, 1, 2, 0, 1, 0)
        ND = 6 * 16
        segs = [(j, qt, s) for j in range(HG) for qt in range(8) for s in range(1 + (qt >= 4))]
        NSEG = len(segs)
        blocks = [(qb, kt) for qb in range(2) for kt in range(4 * qb + 4)]
        NM2 = len(blocks)
        NST = 2 * NM2
        SEG0, SEGN = 4, 3
        N_T1, N_T0, N_MT = 4, 12, 21

        def after(gp, b):
            return (gp, 1) if b == 0 else (gp + 1, 0)

        def before(gp, b):
            return (gp, 0) if b == 1 else (gp - 1, 1)

        def next_segs(n):
            return range(max(0, (n - SEG0) * SEGN), min(NSEG, max(0, n - SEG0 + 1) * SEGN))

        def span(qb, kt):
            q0 = max(qb * TB, kt * P)
            return q0, (qb + 1) * TB - q0

        block = mem.enter_context(nc.Block())

        def stack(eng, g, i, dst, src, parts, sems):
            hg, b = g // 2, g % 2
            rows = slice((2 * hg + i) * SD, (2 * hg + i + 1) * SD)
            for blk in range(6):
                eng.dma_start(dst[b][SD * blk:SD * (blk + 1), 2 * i:2 * i + 2, :],
                              src[rows, parts[blk], :, b * SEQ:(b + 1) * SEQ]).then_inc(sems[b][i], 16)

        @block.sync
        def _(sp):
            def load(g):
                stack(sp, g, 0, QS, QP, QI, sq_in)
                stack(sp, g, 0, KS, KP, KI, sk_in)
                stack(sp, g, 1, QS, QP, QI, sq_in)
                if g == 0:
                    stack(sp, g, 1, KS, KP, KI, sk_in)
                if g >= 2:
                    sp.wait_ge(pv_ok, NM2 * (g - 1))
                sp.dma_start(VG[g % 2][:], V[:, 8 * (g % 2):8 * (g % 2) + 8, HG * (g // 2):HG * (g // 2) + HG, :]
                             ).then_inc(v_in[g % 2], 16)

            def maxima(g):
                b = g % 2
                sp.wait_ge(mtc_ok, g + 1)
                for j in range(HG):
                    sp.dma_start(QS[b][SROWS:KROWS, j, :], MT[b][MROWS * j:MROWS * (j + 1), :]).then_inc(mr_in[b], 16)

            sp.dma_start(MKf[:], masks_in).then_inc(mk_in, 16)
            load(0)
            load(1)
            maxima(0)
            for g in range(2 * NG - 1):
                maxima(g + 1)
                if g + 2 < 2 * NG:
                    sp.wait_ge(st_ok, NST * (g + 1))
                    load(g + 2)

        @block.gpsimd
        def _(pool):
            for b in range(2):
                if b:
                    pool.wait_ge(one_ok, 1)
                pool.memset(KS[b][SROWS:KROWS, :, :], 1.0).then_inc(one_ok, 1)
            pool.wait_ge(one_ok, 2)
            for g in range(1, 2 * NG):
                if g >= 2:
                    pool.wait_ge(st_ok, NST * (g - 1))
                stack(pool, g, 1, KS, KP, KI, sp_in)

        @block.tensor
        def _(pe):
            def pass1(gp, b, s):
                j, qt, half = segs[s]
                bank = S1[s % 2]
                if s in (0, NSEG // 2):
                    i = s // (NSEG // 2)
                    pe.wait_ge(sq_in[b][i], ND * gp + ND)
                    if i == 0:
                        pe.wait_ge(sk_in[b][0], ND * gp + ND)
                    elif isinstance(gp, int) and gp == 0 and b == 0:
                        pe.wait_ge(sk_in[b][1], ND)
                    else:
                        pe.wait_ge(sp_in[b][1], ND * gp + (ND if b else 0))
                if not (isinstance(gp, int) and gp == 0 and b == 0 and s < 2):
                    pe.wait_ge(mx_ok, 2 * NSEG * gp + NSEG * b + s - 1)
                k0, k1 = half * TB, min((half + 1) * TB, (qt + 1) * P)
                diag = k1 == (qt + 1) * P
                ins = pe.matmul(bank[:, 0:k1 - k0], QS[b][0:SROWS, j, qt * P:(qt + 1) * P],
                                KS[b][0:SROWS, j, k0:k1], start=True, stop=True)
                if diag:
                    ins = pe.matmul(bank[:, k1 - P - k0:k1 - k0], MK[:, 0, :], MK[:, 1, :], start=False, stop=True,
                                    skip_group_check=True)
                ins.then_inc(s1_ok, 1)

            def maxima(gp, b):
                pe.wait_ge(nm_ok, 2 * gp + b + 1)
                if not (isinstance(gp, int) and gp == 0 and b == 0):
                    pe.wait_ge(nrm_ok, 4 * gp + 2 * b)
                for qt in range(8):
                    ins = pe.transpose(AUXB[0:HG * MROWS, qt * P:(qt + 1) * P],
                                       NM[:, qt, :, :].rearrange("p j r -> p (j r)"), MK[:, 0, :])
                ins.then_inc(mt_ok, 1)

            def pass2(gp, b, n, h, first):
                qb, kt = blocks[n // 2]
                q0, w = span(qb, kt)
                if n == 0 and h == 0:
                    pe.wait_ge(mr_in[b], 16 * HG * gp + 16 * HG)
                if h == 0 and not (first and n < 2):
                    pe.wait_ge(exp_ok, 2 * NST * gp + NST * b + n - 1)
                j = 2 * (n % 2) + h
                out = ST[n % 2][:, h * TB:h * TB + w]
                ins = pe.matmul(out, KS[b][0:KROWS, j, kt * P:(kt + 1) * P], QS[b][0:KROWS, j, q0:q0 + w],
                                start=True, stop=True)
                if kt >= 4 * qb:
                    ins = pe.matmul(out[:, 0:P], MK[:, 0, :], MK[:, 2, :], start=False, stop=True,
                                    skip_group_check=True)
                if h == 1:
                    ins.then_inc(st_ok, 1)

            def values(gp, b, mm, first=False):
                qb, kt = blocks[mm]
                q0, w = span(qb, kt)
                pe.wait_ge(exp_ok, 2 * NST * gp + NST * b + 2 * mm + 2)
                if mm == 0:
                    pe.wait_ge(v_in[b], 16 * gp + 16)
                if kt == 0 and not (first and qb == 0):
                    pe.wait_ge(oc_ok, 4 * gp + 2 * b + qb)
                for j in range(HG):
                    ins = pe.matmul(OB[32 * j:32 * j + 32, q0 - qb * TB:q0 - qb * TB + w], VG[b][:, kt, j, :],
                                    PT[:, mm % 2, j, 0:w], start=kt == 0, stop=kt == 4 * qb + 3,
                                    skip_group_check=True)
                ins.then_inc(pv_ok, 1)

            def back(gp, b, qb, last):
                pe.wait_ge(oc_ok, 4 * gp + 2 * b + qb + 1)
                if qb == 0:
                    pe.wait_ge(nrm_ok, 4 * gp + 2 * b + 1)
                elif last:
                    pe.wait_ge(nrm_ok, 4 * gp + 2 * b + 2)
                else:
                    pe.wait_ge(mtc_ok, 2 * gp + b + 2)
                for t in range(4):
                    ins = pe.transpose(AUX[:, t * P:(t + 1) * P], OT[:, qb, t * P:(t + 1) * P], ident[:])
                ins.then_inc(t_ok, 1)

            pe.wait_ge(mk_ok, 1)
            pe.wait_ge(one_ok, 2)
            pe.sem_inc(nrm_ok, 1)
            for s in range(NSEG):
                pass1(0, 0, s)
            maxima(0, 0)

            def group(gp, b, first=False, last=False):
                (gn, bn), (go, bo) = after(gp, b), before(gp, b)
                for n in range(NST):
                    todo = [] if last else list(next_segs(n))
                    pass2(gp, b, n, 0, first)
                    for s in todo[0:1]:
                        pass1(gn, bn, s)
                    pass2(gp, b, n, 1, first)
                    for s in todo[1:2]:
                        pass1(gn, bn, s)
                    if n == 1 and not first:
                        values(go, bo, NM2 - 1)
                    if n % 2 == 1 and n >= 3:
                        values(gp, b, (n - 3) // 2, first)
                    for s in todo[2:]:
                        pass1(gn, bn, s)
                    if n == N_T1 and not first:
                        back(go, bo, 1, False)
                    if n == N_T0:
                        back(gp, b, 0, last)
                    if n == N_MT and not last:
                        maxima(gn, bn)
                if last:
                    values(gp, b, NM2 - 1)
                    back(gp, b, 1, True)

            group(0, 0, first=True)
            with pe.Fori(0, NG - 1) as gp:
                group(gp, 1)
                group(gp + 1, 0)
            group(NG - 1, 1, last=True)

        @block.scalar
        def _(act):
            def maxima(gp, b):
                act.wait_ge(mt_ok, 2 * gp + b + 1)
                if not (isinstance(gp, int) and gp == 0):
                    act.wait_ge(mr_in[b], 16 * HG * gp)
                act.activation(MT[b][:], AUXB[0:HG * MROWS, :], ACT.Copy).then_inc(mtc_ok, 1)

            def outputs(gp, b, qb):
                act.wait_ge(pv_ok, 2 * NM2 * gp + NM2 * b + (NM2 if qb else 4))
                act.activation(OT[:, qb, :], OB[:], ACT.Copy).then_inc(oc_ok, 1)

            def group(gp, b, first=False, last=False):
                (gn, bn), (go, bo) = after(gp, b), before(gp, b)
                for n in range(NST):
                    mm = n // 2
                    q0, w = span(*blocks[mm])
                    act.wait_ge(st_ok, 2 * NST * gp + NST * b + n + 1)
                    if n % 2 == 0 and not (first and mm < 2):
                        act.wait_ge(pv_ok, 2 * NM2 * gp + NM2 * b + mm - 1)
                    hh = n % 2
                    act.activation(PT[:, mm % 2, 2 * hh:2 * hh + 2, 0:w],
                                   ST[n % 2][:].rearrange("p (h q) -> p h q", h=2)[:, :, 0:w],
                                   ACT.Exp, scale=SCALE).then_inc(exp_ok, 1)
                    if n == 1 and not first:
                        outputs(go, bo, 1)
                    if n == N_T0 - 2:
                        outputs(gp, b, 0)
                    if n == N_MT and not last:
                        maxima(gn, bn)
                if last:
                    outputs(gp, b, 1)

            maxima(0, 0)
            group(0, 0, first=True)
            with act.Fori(0, NG - 1) as gp:
                group(gp, 1)
                group(gp + 1, 0)
            group(NG - 1, 1, last=True)

        @block.vector
        def _(dve):
            def pass1(gp, b, s):
                j, qt, half = segs[s]
                dve.wait_ge(s1_ok, 2 * NSEG * gp + NSEG * b + s + 1)
                w = min(TB, (qt + 1) * P - half * TB)
                dve.reduce_max(mx[:, j, qt, half:half + 1], S1[s % 2][:, 0:w], AXX).then_inc(mx_ok, 1)

            def parts(gp, b):
                n = 5 * 2 * gp + 5 * b
                dve.wait_ge(mx_ok, 2 * NSEG * gp + NSEG * b + NSEG)
                mq = m[:].rearrange("p q j -> p j q")
                dve.tensor_tensor(mq, mx[:, :, :, 0], mx[:, :, :, 1], ALU.max).then_inc(ch_ok, 1)
                dve.wait_ge(ch_ok, n + 1)
                dve.tensor_scalar(NM[:, :, :, 0], m[:], -1.0, None, ALU.mult).then_inc(ch_ok, 1)
                dve.wait_ge(ch_ok, n + 2)
                dve.scalar_tensor_tensor(mr[:, 0, :, :], m[:], -1.0, NM[:, :, :, 0], ALU.mult,
                                         ALU.subtract).then_inc(ch_ok, 1)
                dve.wait_ge(ch_ok, n + 3)
                dve.tensor_copy(NM[:, :, :, 1], mr[:, 0, :, :]).then_inc(ch_ok, 1)
                dve.wait_ge(ch_ok, n + 4)
                dve.tensor_tensor(mr[:, 1, :, :], mr[:, 0, :, :], NM[:, :, :, 1], ALU.subtract).then_inc(ch_ok, 1)
                dve.wait_ge(ch_ok, n + 5)
                dve.tensor_copy(NM[:, :, :, 2], mr[:, 1, :, :]).then_inc(nm_ok, 1)

            def normalise(gp, b, qb):
                dve.wait_ge(t_ok, 4 * gp + 2 * b + qb + 1)
                o = AUX[:].rearrange("p (t j e) -> p t j e", t=4, j=HG)
                dve.reciprocal(rec[:], o[:, :, :, SD]).then_inc(rec_ok, 1)
                dve.wait_ge(rec_ok, 4 * gp + 2 * b + qb + 1)
                t = 8 * b + 4 * qb
                cols = slice(64 * gp, 64 * gp + 64) if isinstance(gp, int) else bass.ds(64 * gp, 64)
                dve.tensor_tensor(ATT[:, t:t + 4, cols].rearrange("p t (j d) -> p t j d", j=HG),
                                  o[:, :, :, 0:SD], rec[:].unsqueeze(3).broadcast_to([P, 4, HG, SD]),
                                  ALU.mult).then_inc(nrm_ok, 1)

            def group(gp, b, first=False, last=False):
                (gn, bn), (go, bo) = after(gp, b), before(gp, b)
                for n in range(NST):
                    for s in () if last else next_segs(n):
                        pass1(gn, bn, s)
                        if s == NSEG - 1:
                            parts(gn, bn)
                    if n == N_T1 and not first:
                        normalise(go, bo, 1)
                    if n == N_T0:
                        normalise(gp, b, 0)
                if last:
                    normalise(gp, b, 1)

            dve.memset(mx[:], -3e38).then_inc(init_ok, 1)
            dve.wait_ge(mk_in, 16)
            dve.tensor_copy(MK[:], MKf[:]).then_inc(mk_ok, 1)
            dve.wait_ge(init_ok, 1)
            for s in range(NSEG):
                pass1(0, 0, s)
            parts(0, 0)
            group(0, 0, first=True)
            with dve.Fori(0, NG - 1) as gp:
                group(gp, 1)
                group(gp + 1, 0)
            group(NG - 1, 1, last=True)


def out_projection(nc, ctx, X, hTh, hTl, WOh, WOl):
    with ExitStack() as mem:
        sem = lambda n: ctx.enter_context(nc.semaphore("op_" + n))
        banks = [mem.enter_context(nc.psum_tensor(f"op_{i}", [P, TB], F32)) for i in range(4)]
        p_ok, x_ok = sem("p_ok"), sem("x_ok")
        block = mem.enter_context(nc.Block())

        @block.tensor
        def _(pe):
            for n in range(NT // 2):
                if n >= 4:
                    pe.wait_ge(x_ok, n - 3)
                for j in range(2):
                    t = 2 * n + j
                    o = banks[n % 4][:, j * HID:(j + 1) * HID]
                    for kt in range(KT):
                        hi, lo = (h[:, kt, t * P:(t + 1) * P] for h in (hTh, hTl))
                        a, c = (w[:, kt * HID:(kt + 1) * HID] for w in (WOh, WOl))
                        pe.matmul(o, hi, a, start=kt == 0, stop=False)
                        pe.matmul(o, hi, c, start=False, stop=False)
                        m = pe.matmul(o, lo, a, start=False, stop=kt == KT - 1)
                m.then_inc(p_ok, 1)

        @block.vector
        def _(dve):
            for n in range(NT // 2):
                dve.wait_ge(p_ok, n + 1)
                dve.tensor_tensor(X[:, 2 * n:2 * n + 2, :], banks[n % 4][:].rearrange("p (t n) -> p t n", t=2),
                                  X[:, 2 * n:2 * n + 2, :], ALU.add).then_inc(x_ok, 1)


def program(nc, hidden, ident_in, w_quads, nw_quads, c_quads, w_ffn, s_ffn, d_ffn, w_att, rope, masks, out):
    with ExitStack() as ctx:
        sb = lambda n, s, d, c=ctx: c.enter_context(nc.sbuf_tensor(n, s, d))
        X = sb("X", [P, NT, HID], F32)
        ident = sb("ident", [P, P], F32)

        def normed(c, name):
            return sb(name + "hTh", [P, KT, TOK], F32R, c), sb(name + "hTl", [P, KT, TOK], F32R, c)

        with ExitStack() as part:
            hTh, hTl = normed(part, "a_")
            layer_norm_transposed(nc, ctx, "ln1_", X, ident, hTh, hTl, load=(hidden, ident_in))
            linear_attention(nc, ctx, X, ident, hTh, hTl, hidden, w_quads, nw_quads, c_quads)

        WF = sb("WF", [P, 2 * KT * FI + NI * HID], F32R)
        SCL = sb("SCL", [P, 2 * NI], F32)
        DS = sb("DS", [P, HID], F32)
        quantised_weights(nc, ctx, w_ffn, s_ffn, d_ffn, WF, SCL, DS)
        with ExitStack() as part:
            hTh, hTl = normed(part, "b_")
            layer_norm_transposed(nc, ctx, "ln2_", X, ident, hTh, hTl)
            ffn(nc, ctx, "f1_", X, hTh, hTl, WF, SCL, DS)

        with ExitStack() as att:
            WOh = sb("WOh", [P, KT * HID], F32R, att)
            WOl = sb("WOl", [P, KT * HID], F32R, att)
            with ExitStack() as heads:
                QP = sb("QP", [P, NPART, 2, TOK], BF16, heads)
                KP = sb("KP", [P, NPART, 2, TOK], BF16, heads)
                V = sb("V", [P, NT, SH, 32], F32, heads)
                with ExitStack() as part:
                    hTh, hTl = normed(part, "c_")
                    layer_norm_transposed(nc, ctx, "ln3_", X, ident, hTh, hTl)
                    rotary_projections(nc, ctx, hTh, hTl, w_att, rope, QP, KP, V, WOh, WOl)
                ATT = sb("ATT", [P, NT, HID], F32, heads)
                causal_attention(nc, ctx, ident, masks, QP, KP, V, ATT)
                with ExitStack() as part:
                    hTh, hTl = normed(part, "d_")
                    layer_norm_transposed(nc, ctx, "at_", ATT, ident, hTh, hTl, norm=False)
                    out_projection(nc, ctx, X, hTh, hTl, WOh, WOl)

        with ExitStack() as part:
            hTh, hTl = normed(part, "e_")
            layer_norm_transposed(nc, ctx, "ln4_", X, ident, hTh, hTl)
            ffn(nc, ctx, "f2_", X, hTh, hTl, WF, SCL, DS, out)


def rotary_constants():
    import numpy as np
    half = SD // 2
    inv = (np.float32(1.0) / np.float32(10000.0) ** (np.arange(half, dtype=np.float32) / np.float32(half)))
    f = (np.arange(SEQ, dtype=np.float32)[None, :] * inv.astype(np.float32)[:, None]).astype(np.float32)
    row = np.arange(P) % SD
    cos = np.cos(f.astype(np.float64))[row // 2]
    sin = np.sin(f.astype(np.float64))[row // 2] * np.where(row % 2 == 0, -1.0, 1.0)[:, None]
    rope = np.stack([cos, sin], 1).astype(np.float32)
    masks = np.zeros((P, 3, P), np.float32)
    masks[:, 0] = np.eye(P)
    masks[:, 1] = np.triu(np.full((P, P), -1e30), 1)
    masks[:, 2] = np.tril(np.full((P, P), -1e30), -1)
    return rope, masks


def linear_constants():
    import numpy as np
    r = (1.0 / 2.0 ** (8.0 / LH)) ** (np.arange(LH, dtype=np.float64) + 1.0)
    slope = np.float32(r * (1.0 + 1e-5)).astype(np.float64)
    i = np.arange(P, dtype=np.float64)
    diff = i[None, :] - i[:, None]
    D = np.where(diff >= 0, np.exp(-slope[:, None, None] * np.maximum(diff, 0)), 0.0)
    QD = np.exp(-slope[:, None] * (i + 1))
    KD = np.exp(-slope[:, None] * (P - 1 - i))
    BD = np.exp(-slope * P)
    c = np.zeros((NQ, P, CW), np.float32)
    for n in range(NQ):
        for h in range(4):
            c[n, :, CD + h * P:CD + (h + 1) * P] = D[4 * n + h]
            c[n, :, CK + h] = KD[4 * n + h]
            rows = slice((h % 2) * LD, (h % 2 + 1) * LD)
            c[n, rows, CQ + (h // 2) * P:CQ + (h // 2 + 1) * P] = QD[4 * n + h]
            c[n, rows, CB + h // 2] = BD[4 * n + h]
    return c


def kernel(**inputs):
    import numpy as np
    import concourse.bacc as bacc
    from concourse.bass_utils import run_bass_kernel_spmd

    a = {n: np.asarray(x) for n, x in inputs.items()}
    hidden = a["L0_attn_a_hidden_states"].reshape(NT, P, HID).transpose(1, 0, 2)
    qkv = a["L0_attn_a_qkv_w"].reshape(NQ, 2, 2, 3, LD, KT, P)
    gate = a["L0_attn_a_gate_w"].reshape(NQ, 4 * LD, KT, P)
    cols = [qkv[:, :, :, 0].reshape(NQ, 4 * LD, KT, P), qkv[:, :, :, 1].reshape(NQ, 4 * LD, KT, P), gate,
            qkv[:, :, :, 2].reshape(NQ, 4 * LD, KT, P)]
    wq = np.concatenate(cols, 1).transpose(0, 3, 2, 1).reshape(NQ, P, KT * QW)
    wo = a["L0_attn_a_out_w"].T.reshape(NQ, 2, P, HID).transpose(0, 2, 1, 3).reshape(NQ, P, 2 * HID)
    arrays = {
        "hidden": hidden, "ident": np.eye(P, dtype=np.float32),
        "w_quads": np.concatenate([wq, wo], 2),
        "nw_quads": a["L0_attn_a_norm_w"].reshape(NQ, 2, P).transpose(0, 2, 1),
        "c_quads": linear_constants(),
    }
    up = [a["L0_ffn_" + n].reshape(KT, P, FI).transpose(1, 0, 2).reshape(P, KT * FI) for n in ("gate_w", "up_w")]
    down = a["L0_ffn_down_w"].reshape(NI, P, HID).transpose(1, 0, 2).reshape(P, NI * HID)
    arrays["w_ffn"] = np.concatenate(up + [down], 1)
    arrays["s_ffn"] = np.concatenate([a["L0_ffn_" + n].reshape(NI, P).T for n in ("gate_scale", "up_scale")], 1)
    arrays["d_ffn"] = np.broadcast_to(a["L0_ffn_down_scale"], (P, HID))
    pairs = np.arange(HID) ^ 1
    wq, wk, wv, wo = (a["L0_attn_b_W" + n] for n in "qkvo")
    order = np.arange(SH).reshape(NG, 2, 2).transpose(2, 0, 1).ravel()
    wq, wk = (w.reshape(SH, SD, HID)[order].reshape(HID, HID) for w in (wq, wk))
    w5 = np.stack([w.T.reshape(KT, P, HID) for w in (wq, wq[pairs], wk, wk[pairs], wv)], 2)
    wo = wo.T.reshape(KT, P, HID).transpose(1, 0, 2).reshape(P, KT * HID)
    arrays["w_att"] = np.concatenate([w5.transpose(1, 0, 2, 3).reshape(P, KT * 5 * HID), wo], 1)
    rope, masks = rotary_constants()
    arrays["rope"] = rope
    arrays["masks"] = masks
    nc = bacc.Bacc("TRN2", target_bir_lowering=False, num_devices=1)
    args, arr = [], {}
    for name, x in arrays.items():
        x = np.ascontiguousarray(x)
        arr[name + "_dram"] = x
        args.append(nc.dram_tensor(name + "_dram", x.shape, mybir.dt.from_np(x.dtype), kind="ExternalInput").ap())
    args.append(nc.dram_tensor("out_dram", (P, NT, HID), F32, kind="ExternalOutput").ap())
    program(nc, *args)
    r = run_bass_kernel_spmd(nc, [arr], core_ids=[0])
    return r.results[0]["out_dram"].transpose(1, 0, 2).reshape(BATCH, SEQ, HID)
```

```python
import concourse.bass as bass
from concourse import mybir
from contextlib import ExitStack

F32 = mybir.dt.float32
F32R = mybir.dt.float32r
BF16 = mybir.dt.bfloat16
FP8 = mybir.dt.float8e4
ALU = mybir.AluOpType
ACT = mybir.ActivationFunctionType
AXX = mybir.AxisListType.X

P = 128
BATCH, SEQ, HID = 2, 1024, 256
TOK = BATCH * SEQ
NT = TOK // P
KT = HID // P
TB = 512
NTB = TOK // TB
EPS = 1e-5

LH, LD = 32, 64
FEAT = LH * LD
NQ = LH // 4
QW = 8 * P
OFF_Q, OFF_K, OFF_G, OFF_V = 0, 2 * P, 4 * P, 6 * P
GC = 4
NU = BATCH * 2 * 2
CD, CQ, CK, CB = 0, 4 * P, 6 * P, 6 * P + 4
CW = 6 * P + 6

FI = 768
NI = FI // P

SH, SD = 16, 16
NPART = 3
SROWS = 6 * SD
MROWS = NPART
KROWS = SROWS + MROWS
HG = 4
NG = SH // HG
SCALE = SD ** -0.5


def layer_norm_transposed(nc, ctx, name, X, ident, hTh, hTl, load=None, norm=True):
    with ExitStack() as mem:
        sb = lambda n, s, d: mem.enter_context(nc.sbuf_tensor(name + n, s, d))
        sem = lambda n: ctx.enter_context(nc.semaphore(name + n))
        stats = sb("stats", [P, NT, 6], F32)
        mv = sb("mv", [P, NT, 2], F32)
        std = sb("std", [P, NT], F32)
        rstd = sb("rstd", [P, NT], F32)
        epst = sb("epst", [P, 1], F32)
        H = sb("H", [P, NT, HID], F32) if norm else X
        banks = [mem.enter_context(nc.psum_tensor(name + f"T{i}", [P, TB], F32)) for i in range(4)]
        x_in, stats_ok, mv_ok, std_ok, rstd_ok = sem("x_in"), sem("stats_ok"), sem("mv_ok"), sem("std_ok"), sem("rstd_ok")
        eps_ok, h_ok, t_ok, hi_ok, lo_ok = sem("eps_ok"), sem("h_ok"), sem("t_ok"), sem("hi_ok"), sem("lo_ok")
        NB = NTB * KT
        block = mem.enter_context(nc.Block())

        if load is not None:
            @block.sync
            def _(sp):
                sp.dma_start(ident[:], load[1]).then_inc(x_in, 16)
                for b in range(4):
                    sp.dma_start(X[:, 4 * b:4 * b + 4, :],
                                 load[0][:, 4 * b:4 * b + 4, :]).then_inc(x_in, 16)

        @block.vector
        def _(dve):
            dve.memset(epst[:], EPS).then_inc(eps_ok, 1)
            if load is not None:
                dve.wait_ge(x_in, 5 * 16)
            for t in range(NT if norm else 0):
                dve.bn_stats(stats[:, t, :], X[:, t, :]).then_inc(stats_ok, 1)
            for t in range(NT if norm else 0):
                dve.wait_ge(stats_ok, t + 1)
                dve.bn_aggr(mv[:, t, :], stats[:, t, :]).then_inc(mv_ok, 1)
            if norm:
                dve.wait_ge(std_ok, 1)
                dve.reciprocal(rstd[:], std[:]).then_inc(rstd_ok, 1)
                dve.wait_ge(rstd_ok, 1)
            for t in range(NT if norm else 0):
                dve.tensor_scalar(H[:, t, :], X[:, t, :], mv[:, t, 0:1], rstd[:, t:t + 1],
                                  ALU.subtract, ALU.mult).then_inc(h_ok, 1)
            for n in range(NB):
                tb, k = n // KT, n % KT
                dve.wait_ge(hi_ok, n + 1)
                dve.tensor_tensor(hTl[:, k, tb * TB:(tb + 1) * TB], banks[n % 4][:],
                                  hTh[:, k, tb * TB:(tb + 1) * TB].bitcast(F32),
                                  ALU.subtract).then_inc(lo_ok, 1)

        @block.scalar
        def _(act):
            act.wait_ge(eps_ok, 1)
            if norm:
                act.wait_ge(mv_ok, NT)
                act.activation(std[:], mv[:, :, 1], ACT.Sqrt, bias=epst[:]).then_inc(std_ok, 1)
            for n in range(NB):
                tb, k = n // KT, n % KT
                act.wait_ge(t_ok, n + 1)
                act.activation(hTh[:, k, tb * TB:(tb + 1) * TB], banks[n % 4][:],
                               ACT.Copy).then_inc(hi_ok, 1)

        @block.tensor
        def _(pe):
            if load is not None:
                pe.wait_ge(x_in, 5 * 16)
            for n in range(NB):
                tb, k = n // KT, n % KT
                if norm:
                    pe.wait_ge(h_ok, 4 * tb + 4)
                if n >= 4:
                    pe.wait_ge(lo_ok, n - 3)
                for j in range(4):
                    last = pe.transpose(banks[n % 4][:, j * P:(j + 1) * P],
                                        H[:, 4 * tb + j, k * P:(k + 1) * P], ident[:])
                last.then_inc(t_ok, 1)


def linear_attention(nc, ctx, X, ident, hTh, hTl, hidden, w_quads, nw_quads, c_quads):
    with ExitStack() as mem:
        sb = lambda n, s, d: mem.enter_context(nc.sbuf_tensor("la_" + n, s, d))
        sem = lambda n: ctx.enter_context(nc.semaphore("la_" + n))
        WTOT = KT * QW + 2 * HID
        WQ = KT * QW
        Wraw = sb("Wraw", [P, WTOT], F32)
        Wh = sb("Wh", [P, WTOT], F32R)
        Wl = sb("Wl", [P, WTOT], F32R)
        C = sb("C", [P, CW], F32)
        NW = sb("NW", [P, 2], F32)
        q = sb("q", [P, 2, TOK], F32)
        k = sb("k", [P, 2, TOK], F32)
        g = sb("g", [P, 2, TOK], F32)
        v = sb("v", [P, NT, 4 * LD], F32)
        acc = X
        sqacc = sb("sqacc", [P, TOK], F32)
        qd = sb("qd", [P, 2, TB], F32)
        kd = sb("kd", [P, 2, TB], F32)
        A = sb("A", [P, 2, 2, TB], F32)
        S = sb("S", [P, 4, 4, P], F32)
        y = sb("y", [P, 2, TB], F32)
        yh = sb("yh", [P, 4, TB], F32R)
        yl = sb("yl", [P, 4, TB], F32R)
        sq = sb("sq", [P, 2, TB], F32)
        ones = sb("ones", [P, 1], F32)
        epst = sb("epst", [P, 1], F32)
        std = sb("std", [P, NT], F32)
        rstd = sb("rstd", [P, NT], F32)
        pb = lambda n: mem.enter_context(nc.psum_tensor("la_" + n, [P, TB], F32))
        SC = [[pb("SA0"), pb("SB0")], [pb("SA1"), pb("SB1")]]
        PR = [SC[0][0], SC[0][1], SC[1][0], SC[1][1]]
        KB, UB, OB, RB = pb("KB"), pb("UB"), pb("OB"), pb("RB")

        w_in, c_in, x_in = sem("w_in"), sem("c_in"), sem("x_in")
        wh_ok, w_ok, wo_ok = sem("wh_ok"), sem("w_ok"), sem("wo_ok")
        init_ok, zero_ok = sem("init_ok"), sem("zero_ok")
        proj_ok, silu_ok = sem("proj_ok"), sem("silu_ok")
        sc_ok, mask_ok, kb_ok, kd_ok, qd_ok = sem("sc_ok"), sem("mask_ok"), sem("kb_ok"), sem("kd_ok"), sem("qd_ok")
        u_ok, s_link, s_ok, o_ok = sem("u_ok"), sem("s_link"), sem("s_ok"), sem("o_ok")
        sq_ok, y_ok, yh_ok, yl_ok, sqa_ok = sem("sq_ok"), sem("y_ok"), sem("yh_ok"), sem("yl_ok"), sem("sqa_ok")
        r_ok, acc_ok = sem("r_ok"), sem("acc_ok")
        ss_ok, std_ok, rstd_ok = sem("ss_ok"), sem("std_ok"), sem("rstd_ok")

        def unit(u):
            half, b, pr = u // 4, u // 2 % 2, u % 2
            return half, b, pr, b * SEQ + half * TB, b * 2 + pr

        BANK = [n % 4 for n in range(28)] + [2, 3, 2, 3]
        NLINK = 2 * 2 * 2 * (4 + 3)

        block = mem.enter_context(nc.Block())

        @block.sync
        def _(sp):
            for s in (r_ok, o_ok, y_ok, kd_ok, u_ok, sqa_ok, yl_ok, acc_ok, s_ok, sq_ok, mask_ok):
                sp.sem_inc(s, 1)
            sp.dma_start(Wraw[:], w_quads[0, :, :]).then_inc(w_in, 16)
            sp.dma_start(C[:], c_quads[0, :, :]).then_inc(c_in, 16)
            sp.dma_start(NW[:], nw_quads[0, :, :]).then_inc(c_in, 16)
            for i in range(1, NQ):
                sp.wait_ge(wo_ok, i)
                sp.dma_start(Wraw[:], w_quads[i, :, :]).then_inc(w_in, 16)
                sp.wait_ge(kd_ok, 16 * i + 1)
                sp.wait_ge(qd_ok, 8 * i)
                sp.wait_ge(y_ok, 8 * i + 1)
                sp.wait_ge(s_ok, 8 * i + 1)
                sp.dma_start(C[:], c_quads[i, :, :]).then_inc(c_in, 16)
                sp.dma_start(NW[:], nw_quads[i, :, :]).then_inc(c_in, 16)
            sp.wait_ge(sc_ok, 8 * NQ)
            sp.wait_ge(qd_ok, 8 * NQ)
            sp.dma_start(q[:].rearrange("p a n -> p (a n)"), hidden.rearrange("p t n -> p (t n)")).then_inc(x_in, 16)

        @block.gpsimd
        def _(pool):
            pool.memset(acc[:], 0.0).then_inc(init_ok, 1)
            pool.memset(sqacc[:], 0.0).then_inc(init_ok, 1)
            pool.memset(ones[:], 1.0).then_inc(init_ok, 1)
            pool.memset(epst[:], EPS).then_inc(init_ok, 1)
            pool.memset(S[:], 0.0).then_inc(zero_ok, 1)

            pool.wait_ge(wh_ok, 1)
            pool.tensor_tensor(Wl[:, 0:WQ], Wraw[:, 0:WQ], Wh[:, 0:WQ].bitcast(F32),
                               ALU.subtract).then_inc(w_ok, 1)

            def quad(i, last):
                pool.wait_ge(wh_ok, 2 * i + 2)
                pool.tensor_tensor(Wl[:, WQ:WTOT], Wraw[:, WQ:WTOT], Wh[:, WQ:WTOT].bitcast(F32),
                                   ALU.subtract).then_inc(wo_ok, 1)
                pool.wait_ge(silu_ok, 32 * i + 8)
                pool.wait_ge(c_in, 32 * i + 32)
                for u in range(NU + 1):
                    if u < NU:
                        half, b, pr, col, ch = unit(u)
                        if u >= 2:
                            pool.wait_ge(o_ok, 8 * i + u)
                        else:
                            pool.wait_ge(o_ok, 8 * i + 1)
                        pool.tensor_tensor(
                            qd[:, u % 2, :].rearrange("p (c t) -> p c t", c=GC),
                            q[:, pr, col:col + TB].rearrange("p (c t) -> p c t", c=GC),
                            C[:, CQ + pr * P:CQ + (pr + 1) * P].unsqueeze(1).broadcast_to([P, GC, P]),
                            ALU.mult).then_inc(qd_ok, 1)
                    if u == 4 and not last:
                        pool.wait_ge(wh_ok, 2 * i + 3)
                        pool.tensor_tensor(Wl[:, 0:WQ], Wraw[:, 0:WQ], Wh[:, 0:WQ].bitcast(F32),
                                           ALU.subtract).then_inc(w_ok, 1)
                    if u >= 1:
                        w = u - 1
                        half, b, pr, col, ch = unit(w)
                        pool.wait_ge(yh_ok, 8 * i + w + 1)
                        if w >= 4:
                            pool.wait_ge(r_ok, 8 * i + 2 * (w // 2) - 1)
                        else:
                            pool.wait_ge(r_ok, 8 * i + 1)
                        pool.tensor_tensor(yl[:, w % 4, :], y[:, w % 2, :], yh[:, w % 4, :].bitcast(F32),
                                           ALU.subtract).then_inc(yl_ok, 1)
                        pool.wait_ge(sq_ok, 8 * i + w + 2)
                        if w == 0:
                            pool.wait_ge(init_ok, 4)
                        pool.wait_ge(sqa_ok, 8 * i + w + 1)
                        pool.tensor_tensor(sqacc[:, col:col + TB], sqacc[:, col:col + TB], sq[:, w % 2, :],
                                           ALU.add).then_inc(sqa_ok, 1)

            with pool.Fori(0, NQ - 1) as i:
                quad(i, False)
            quad(NQ - 1, True)

        @block.scalar
        def _(act):
            def quad(i):
                def keys(u):
                    half, b, pr, col, ch = unit(u)
                    act.wait_ge(kb_ok, 8 * i + u + 1)
                    if u >= 2:
                        act.wait_ge(u_ok, 8 * i + u)
                    else:
                        act.wait_ge(u_ok, 8 * i + 1)
                    kdv = kd[:, u % 2, :].rearrange("p (c n) -> p c n", c=GC)
                    kbv = KB[:].rearrange("p (c n) -> p c n", c=GC)
                    for h in range(2):
                        act.activation(kdv[:, :, h * LD:(h + 1) * LD], kbv[:, :, h * LD:(h + 1) * LD],
                                       ACT.Copy, scale=C[:, CK + 2 * pr + h:CK + 2 * pr + h + 1]
                                       ).then_inc(kd_ok, 1)

                for n in range(32):
                    act.wait_ge(proj_ok, 32 * i + n + 1)
                    bank = PR[BANK[n]]
                    if n < 16:
                        pr, tb = n // 4 % 2, n % 4
                        dst = (q if n < 8 else k)[:, pr, tb * TB:(tb + 1) * TB]
                        act.activation(dst, bank[:], ACT.Silu).then_inc(silu_ok, 1)
                    elif n < 24:
                        t = 2 * (n - 16)
                        act.activation(v[:, t:t + 2, :], bank[:].rearrange("p (t n) -> p t n", t=2),
                                       ACT.Silu).then_inc(silu_ok, 1)
                    else:
                        if n == 24:
                            act.wait_ge(y_ok, 8 * i + 1)
                        pr, tb = n // 4 % 2, n % 4
                        act.activation(g[:, pr, tb * TB:(tb + 1) * TB], bank[:],
                                       ACT.Sigmoid).then_inc(silu_ok, 1)
                    if n == 29:
                        act.wait_ge(c_in, 32 * i + 32)
                        keys(0)

                for u in range(NU):
                    if u + 1 < NU:
                        keys(u + 1)
                    act.wait_ge(y_ok, 8 * i + u + 2)
                    if u >= 2:
                        act.wait_ge(sqa_ok, 8 * i + u)
                    else:
                        act.wait_ge(sqa_ok, 8 * i + 1)
                    act.activation(sq[:, u % 2, :], OB[:], ACT.Square).then_inc(sq_ok, 1)
                    if u >= 4:
                        act.wait_ge(r_ok, 8 * i + 2 * (u // 2) - 1)
                    else:
                        act.wait_ge(r_ok, 8 * i + 1)
                    act.activation(yh[:, u % 4, :], y[:, u % 2, :], ACT.Copy).then_inc(yh_ok, 1)

            with act.Fori(0, NQ) as i:
                quad(i)
            act.wait_ge(init_ok, 4)
            act.wait_ge(ss_ok, 1)
            act.activation(std[:], KB[:, 0:NT], ACT.Sqrt, bias=epst[:], scale=1.0 / FEAT).then_inc(std_ok, 1)

        @block.vector
        def _(dve):
            dve.wait_ge(zero_ok, 1)
            dve.wait_ge(init_ok, 4)

            def high(a, b):
                dve.tensor_copy(Wh[:, a:b], Wraw[:, a:b]).then_inc(wh_ok, 1)

            dve.wait_ge(w_in, 16)
            high(0, WQ)

            def quad(i, last):
                link = [0]
                dve.wait_ge(r_ok, 8 * i + 1)
                high(WQ, WTOT)

                def masks(u):
                    half, b, pr, col, ch = unit(u)
                    dve.wait_ge(sc_ok, 8 * i + u + 1)
                    if u >= 2:
                        dve.wait_ge(o_ok, 8 * i + u)
                    else:
                        dve.wait_ge(o_ok, 8 * i + 1)
                    for h in range(2):
                        d = C[:, CD + (2 * pr + h) * P:CD + (2 * pr + h + 1) * P]
                        dve.tensor_tensor(A[:, u % 2, h, :].rearrange("p (c t) -> p c t", c=GC),
                                          SC[u % 2][h][:].rearrange("p (c t) -> p c t", c=GC),
                                          d.unsqueeze(1).broadcast_to([P, GC, P]),
                                          ALU.mult).then_inc(mask_ok, 1)

                def states(u):
                    half, b, pr, col, ch = unit(u)
                    dve.wait_ge(u_ok, 8 * i + u + 2)
                    cs = range(4 * half, 4 * half + (4 if half == 0 else 3))
                    for c in cs:
                        if link[0] or c > 0:
                            dve.wait_ge(s_link, NLINK * i + link[0])
                        for h in range(2):
                            r = slice(h * LD, (h + 1) * LD)
                            U = UB[r, (c % 4) * P + h * LD:(c % 4) * P + (h + 1) * LD]
                            new = S[r, ch, c % 4, h * LD:(h + 1) * LD]
                            if c == 0:
                                ins = dve.tensor_copy(new, U)
                            else:
                                ins = dve.scalar_tensor_tensor(
                                    new, S[r, ch, (c - 1) % 4, h * LD:(h + 1) * LD],
                                    C[r, CB + pr:CB + pr + 1], U, ALU.mult, ALU.add)
                            ins.then_inc(s_link, 1)
                            link[0] += 1
                    dve.wait_ge(s_link, NLINK * i + link[0])
                    dve.sem_inc(s_ok, 1)

                def gated(u):
                    half, b, pr, col, ch = unit(u)
                    dve.wait_ge(o_ok, 8 * i + u + 2)
                    if u >= 2:
                        dve.wait_ge(yl_ok, 8 * i + u)
                    else:
                        dve.wait_ge(yl_ok, 8 * i + 1)
                    dve.scalar_tensor_tensor(y[:, u % 2, :], OB[:], NW[:, pr:pr + 1], g[:, pr, col:col + TB],
                                             ALU.mult, ALU.mult).then_inc(y_ok, 1)

                def sums(m):
                    half, b, _, col, _ = unit(2 * (m // 2))
                    t = col // P + 2 * (m % 2)
                    dve.wait_ge(r_ok, 8 * i + m + 2)
                    dve.wait_ge(acc_ok, 8 * i + m + 1)
                    dve.tensor_tensor(acc[:, t:t + 2, :], RB[:].rearrange("p (t n) -> p t n", t=2),
                                      acc[:, t:t + 2, :], ALU.add).then_inc(acc_ok, 1)

                dve.wait_ge(c_in, 32 * i + 32)
                masks(0)
                for u in range(NU):
                    states(u)
                    if u + 1 < NU:
                        masks(u + 1)
                    gated(u)
                    if u == 2 and not last:
                        dve.wait_ge(w_in, 16 * i + 32)
                        high(0, WQ)
                    if u >= 2:
                        sums(u - 2)
                sums(NU - 2)
                sums(NU - 1)
                assert link[0] == NLINK

            with dve.Fori(0, NQ - 1) as i:
                quad(i, False)
            quad(NQ - 1, True)
            dve.wait_ge(std_ok, 1)
            dve.reciprocal(rstd[:], std[:]).then_inc(rstd_ok, 1)
            dve.wait_ge(rstd_ok, 1)
            dve.wait_ge(acc_ok, 8 * NQ + 1)
            dve.wait_ge(x_in, 16)
            xin = q[:].rearrange("p a n -> p (a n)").rearrange("p (t n) -> p t n", t=NT)
            for t in range(NT):
                dve.scalar_tensor_tensor(X[:, t, :], acc[:, t, :], rstd[:, t:t + 1], xin[:, t, :],
                                         ALU.mult, ALU.add)

        @block.tensor
        def _(pe):
            def products(out, pairs, first, last, check):
                m = None
                for n, (a, b) in enumerate(pairs):
                    m = pe.matmul(out, a, b, start=first and n == 0, stop=last and n == len(pairs) - 1,
                                  skip_group_check=check)
                return m

            def projection(i, n):
                if n == 0:
                    pe.wait_ge(w_ok, i + 1)
                if n < 4:
                    pe.wait_ge(mask_ok, 16 * i + 1)
                else:
                    pe.wait_ge(silu_ok, 32 * i + (n - 3 if n < 28 else n - 1))
                wv = [w[:, 0:WQ].rearrange("p (k n) -> p k n", k=KT) for w in (Wh, Wl)]
                bank = PR[BANK[n]]
                if n < 16 or n >= 24:
                    off = (OFF_Q if n < 8 else OFF_K if n < 16 else OFF_G) + P * (n // 4 % 2)
                    tb = n % 4
                    pairs = []
                    for kt in range(KT):
                        hi, lo = (h[:, kt, tb * TB:(tb + 1) * TB] for h in (hTh, hTl))
                        a, c = (w[:, kt, off:off + P] for w in wv)
                        pairs += [(a, hi), (a, lo), (c, hi)]
                    m = products(bank[:], pairs, True, True, False)
                else:
                    for j in range(2):
                        t = 2 * (n - 16) + j
                        pairs = []
                        for kt in range(KT):
                            hi, lo = (h[:, kt, t * P:(t + 1) * P] for h in (hTh, hTl))
                            a, c = (w[:, kt, OFF_V:OFF_V + 4 * LD] for w in wv)
                            pairs += [(hi, a), (hi, c), (lo, a)]
                        m = products(bank[:, j * HID:(j + 1) * HID], pairs, True, True, False)
                m.then_inc(proj_ok, 1)

            def quad(i, last):
                def scores(u):
                    half, b, pr, col, ch = unit(u)
                    if u < 2:
                        pe.wait_ge(silu_ok, 32 * i + (28 if u == 0 else 32))
                    else:
                        pe.wait_ge(mask_ok, 16 * i + 2 * u - 1)
                    for c in range(GC):
                        cc = slice(col + c * P, col + (c + 1) * P)
                        for h in range(2):
                            r = slice(h * LD, (h + 1) * LD)
                            m = pe.matmul(SC[u % 2][h][:, c * P:(c + 1) * P], k[r, pr, cc], q[r, pr, cc],
                                          start=True, stop=True)
                    m.then_inc(sc_ok, 1)
                    pe.wait_ge(kd_ok, 16 * i + 2 * u + 1)
                    for c in range(GC):
                        m = pe.transpose(KB[:, c * P:(c + 1) * P], k[:, pr, col + c * P:col + (c + 1) * P],
                                         ident[:])
                    m.then_inc(kb_ok, 1)

                def state_sums(u):
                    half, b, pr, col, ch = unit(u)
                    pe.wait_ge(kd_ok, 16 * i + 2 * u + 3)
                    pe.wait_ge(s_ok, 8 * i + u + 1)
                    for c in range(GC):
                        t = col // P + c
                        m = pe.matmul(UB[:, c * P:(c + 1) * P], kd[:, u % 2, c * P:(c + 1) * P],
                                      v[:, t, pr * P:(pr + 1) * P], start=True, stop=True)
                    m.then_inc(u_ok, 1)

                def outputs(u):
                    half, b, pr, col, ch = unit(u)
                    pe.wait_ge(s_ok, 8 * i + u + 2)
                    pe.wait_ge(qd_ok, 8 * i + u + 1)
                    pe.wait_ge(mask_ok, 16 * i + 2 * u + 3)
                    pe.wait_ge(sq_ok, 8 * i + u + 1)
                    c0 = 1 if half == 0 else 0
                    for c in range(c0, GC):
                        pe.matmul(OB[:, c * P:(c + 1) * P], S[:, ch, (4 * half + c - 1) % 4, :],
                                  qd[:, u % 2, c * P:(c + 1) * P], start=c == c0, stop=False,
                                  skip_group_check=True)
                    for c in range(GC):
                        t = col // P + c
                        for h in range(2):
                            r = slice(h * LD, (h + 1) * LD)
                            m = pe.matmul(OB[r, c * P:(c + 1) * P], v[:, t, pr * P + h * LD:pr * P + (h + 1) * LD],
                                          A[:, u % 2, h, c * P:(c + 1) * P], start=False, stop=c == GC - 1,
                                          skip_group_check=True)
                    m.then_inc(o_ok, 1)

                def out_projection(mm):
                    base = 2 * (mm // 2)
                    pe.wait_ge(yl_ok, 8 * i + base + 3)
                    pe.wait_ge(acc_ok, 8 * i + mm + 1)
                    if mm == 0:
                        pe.wait_ge(wo_ok, i + 1)
                    for j in range(2):
                        cols = slice((2 * (mm % 2) + j) * P, (2 * (mm % 2) + j + 1) * P)
                        pairs = []
                        for pr in range(2):
                            hi, lo = (z[:, (base + pr) % 4, cols] for z in (yh, yl))
                            a, c = (w[:, WQ + pr * HID:WQ + (pr + 1) * HID] for w in (Wh, Wl))
                            pairs += [(hi, a), (hi, c), (lo, a)]
                        m = products(RB[:, j * HID:(j + 1) * HID], pairs, True, True, False)
                    m.then_inc(r_ok, 1)

                scores(0)
                for n in range(28, 32):
                    projection(i, n)
                for u in range(NU):
                    state_sums(u)
                    if u + 1 < NU:
                        scores(u + 1)
                    else:
                        out_projection(u - 2)
                        if not last:
                            projection(i + 1, 0)
                    outputs(u)
                    if 2 <= u < NU - 1:
                        out_projection(u - 2)
                for n in range(1, 28):
                    if not last:
                        projection(i + 1, n)
                    if n == 2:
                        out_projection(NU - 2)
                    if n == 3:
                        out_projection(NU - 1)

            for n in range(28):
                projection(0, n)
            with pe.Fori(0, NQ - 1) as i:
                quad(i, False)
            quad(NQ - 1, True)
            pe.wait_ge(sqa_ok, 8 * NQ + 1)
            pe.wait_ge(init_ok, 4)
            for t in range(NT):
                m = pe.matmul(KB[:, t:t + 1], sqacc[:, t * P:(t + 1) * P], ones[:], start=True, stop=True)
            m.then_inc(ss_ok, 1)


def ffn(nc, ctx, name, X, hTh, hTl, WF, SCL, DS, out=None):
    with ExitStack() as mem:
        sb = lambda n, s, d: mem.enter_context(nc.sbuf_tensor(name + n, s, d))
        sem = lambda n: ctx.enter_context(nc.semaphore(name + n))
        pb = lambda n: mem.enter_context(nc.psum_tensor(name + n, [P, TB], F32))
        sg = sb("sg", [P, 2, TB], F32)
        f = sb("f", [P, 2, TB], F32)
        fh = sb("fh", [P, 2, NI, TB], F32R)
        fl = sb("fl", [P, 2, NI, TB], F32R)
        o = sb("o", [P, 2, 2, HID], F32)
        GB, UB, DB = [pb("G0"), pb("G1")], [pb("U0"), pb("U1")], [pb("D0"), pb("D1")]
        g_ok, u_ok, sg_ok, f_ok, fh_ok, fl_ok = sem("g_ok"), sem("u_ok"), sem("sg_ok"), sem("f_ok"), sem("fh_ok"), sem("fl_ok")
        d_ok, o_ok, x_ok, st_ok = sem("d_ok"), sem("o_ok"), sem("x_ok"), sem("st_ok")
        wg = WF[:, 0:KT * FI].rearrange("p (k n) -> p k n", k=KT)
        wu = WF[:, KT * FI:2 * KT * FI].rearrange("p (k n) -> p k n", k=KT)
        wd = WF[:, 2 * KT * FI:].rearrange("p (k n) -> p k n", k=NI)
        block = mem.enter_context(nc.Block())

        @block.tensor
        def _(pe):
            def up(tb):
                for it in range(NI):
                    n = tb * NI + it
                    if n >= 2:
                        pe.wait_ge(sg_ok, n - 1)
                        pe.wait_ge(f_ok, n - 1)
                    for w, bank, done in ((wg, GB[n % 2], g_ok), (wu, UB[n % 2], u_ok)):
                        for kt in range(KT):
                            a = w[:, kt, it * P:(it + 1) * P]
                            pe.matmul(bank[:], a, hTh[:, kt, tb * TB:(tb + 1) * TB], start=kt == 0, stop=False)
                            m = pe.matmul(bank[:], a, hTl[:, kt, tb * TB:(tb + 1) * TB], start=False,
                                          stop=kt == KT - 1)
                        m.then_inc(done, 1)

            def down(tb):
                pe.wait_ge(fl_ok, (tb + 1) * NI)
                for half in range(2):
                    n = 2 * tb + half
                    if n >= 2:
                        pe.wait_ge(o_ok, n - 1)
                    for j in range(2):
                        c = slice((2 * half + j) * P, (2 * half + j + 1) * P)
                        for it in range(NI):
                            pe.matmul(DB[n % 2][:, j * HID:(j + 1) * HID], fh[:, tb % 2, it, c], wd[:, it, :],
                                      start=it == 0, stop=False)
                            m = pe.matmul(DB[n % 2][:, j * HID:(j + 1) * HID], fl[:, tb % 2, it, c],
                                          wd[:, it, :], start=False, stop=it == NI - 1)
                    m.then_inc(d_ok, 1)

            up(0)
            for tb in range(NTB):
                if tb + 1 < NTB:
                    up(tb + 1)
                down(tb)

        @block.scalar
        def _(act):
            def high(n):
                tb, it = n // NI, n % NI
                act.wait_ge(f_ok, n + 1)
                if tb >= 2:
                    act.wait_ge(d_ok, 2 * (tb - 1))
                act.activation(fh[:, tb % 2, it, :], f[:, n % 2, :], ACT.Copy).then_inc(fh_ok, 1)

            for n in range(NTB * NI):
                act.wait_ge(g_ok, n + 1)
                if n >= 2:
                    act.wait_ge(f_ok, n - 1)
                act.activation(sg[:, n % 2, :], GB[n % 2][:], ACT.Silu,
                               scale=SCL[:, n % NI:n % NI + 1]).then_inc(sg_ok, 1)
                if n >= 1:
                    high(n - 1)
            high(NTB * NI - 1)

        @block.vector
        def _(dve):
            def scaled(n):
                dve.wait_ge(d_ok, n + 1)
                if n >= 2:
                    dve.wait_ge(x_ok, n - 1)
                dve.tensor_tensor(o[:, n % 2, :, :], DB[n % 2][:].rearrange("p (t n) -> p t n", t=2),
                                  DS[:].unsqueeze(1).broadcast_to([P, 2, HID]), ALU.mult).then_inc(o_ok, 1)

            for n in range(NTB * NI):
                tb, it = n // NI, n % NI
                dve.wait_ge(sg_ok, n + 1)
                dve.wait_ge(u_ok, n + 1)
                if n >= 2:
                    dve.wait_ge(fl_ok, n - 1)
                dve.scalar_tensor_tensor(f[:, n % 2, :], UB[n % 2][:], SCL[:, NI + it:NI + it + 1],
                                         sg[:, n % 2, :], ALU.mult, ALU.mult).then_inc(f_ok, 1)
                if tb >= 1 and it == NI - 1:
                    scaled(2 * (tb - 1))
                    scaled(2 * (tb - 1) + 1)
            scaled(2 * NTB - 2)
            scaled(2 * NTB - 1)

        @block.gpsimd
        def _(pool):
            def add(n):
                pool.wait_ge(o_ok, n + 1)
                pool.tensor_tensor(X[:, 2 * n:2 * n + 2, :], X[:, 2 * n:2 * n + 2, :], o[:, n % 2, :, :],
                                   ALU.add).then_inc(x_ok, 1)

            for n in range(NTB * NI):
                tb, it = n // NI, n % NI
                pool.wait_ge(fh_ok, n + 1)
                if tb >= 2:
                    pool.wait_ge(d_ok, 2 * (tb - 1))
                pool.tensor_tensor(fl[:, tb % 2, it, :], f[:, n % 2, :], fh[:, tb % 2, it, :].bitcast(F32),
                                   ALU.subtract).then_inc(fl_ok, 1)
                if tb >= 1 and it == NI - 1:
                    add(2 * (tb - 1))
                    add(2 * (tb - 1) + 1)
            add(2 * NTB - 2)
            add(2 * NTB - 1)

        if out is not None:
            @block.sync
            def _(sp):
                for n in range(2 * NTB):
                    sp.wait_ge(x_ok, n + 1)
                    sp.dma_start(out[:, 2 * n:2 * n + 2, :], X[:, 2 * n:2 * n + 2, :]).then_inc(st_ok, 16)
                sp.wait_ge(st_ok, 16 * 2 * NTB)


def quantised_weights(nc, ctx, w_ffn, s_ffn, d_ffn, WF, SCL, DS):
    with ExitStack() as mem:
        sb = lambda n, s, d: mem.enter_context(nc.sbuf_tensor("qw_" + n, s, d))
        sem = lambda n: ctx.enter_context(nc.semaphore("qw_" + n))
        N = (2 * KT * FI + NI * HID)
        w = sb("w", [P, N], F32)
        c = sb("c", [P, N], F32)
        e = sb("e", [P, N], FP8)
        wh8 = sb("wh8", [P, N], FP8)
        ch8 = sb("ch8", [P, N], FP8)
        d = sb("d", [P, N], F32)
        z = sb("z", [P, N], F32)
        lim = sb("lim", [P, 1], F32)
        w_in, c_ok, e_ok, h_ok, z_ok, d_ok, q_ok, l_ok = (sem(n) for n in
            ("w_in", "c_ok", "e_ok", "h_ok", "z_ok", "d_ok", "q_ok", "l_ok"))
        block = mem.enter_context(nc.Block())

        @block.sync
        def _(sp):
            sp.dma_start(w[:], w_ffn).then_inc(w_in, 16)
            sp.dma_start(SCL[:], s_ffn).then_inc(w_in, 16)
            sp.dma_start(DS[:], d_ffn).then_inc(w_in, 16)

        @block.scalar
        def _(act):
            act.wait_ge(w_in, 48)
            act.activation(wh8[:], w[:], ACT.Copy, scale=0.5, saturate=False).then_inc(h_ok, 1)
            act.wait_ge(c_ok, 1)
            act.activation(ch8[:], c[:], ACT.Copy, scale=0.5, saturate=False).then_inc(h_ok, 1)
            act.activation(e[:], c[:], ACT.Copy, saturate=False).then_inc(e_ok, 1)
            act.activation(z[:], w[:], ACT.Abs).then_inc(z_ok, 1)
            act.wait_ge(l_ok, 1)
            act.wait_ge(z_ok, 1)
            act.activation(z[:], z[:], ACT.Relu, bias=lim[:]).then_inc(z_ok, 1)

        @block.gpsimd
        def _(pool):
            pool.wait_ge(h_ok, 2)
            pool.tensor_tensor(d[:], wh8[:], ch8[:], ALU.subtract).then_inc(d_ok, 1)

        @block.vector
        def _(dve):
            dve.memset(lim[:], -464.0).then_inc(l_ok, 1)
            dve.wait_ge(w_in, 48)
            dve.tensor_scalar(c[:], w[:], 128.0, -128.0, ALU.min, ALU.max).then_inc(c_ok, 1)
            dve.wait_ge(z_ok, 2)
            dve.tensor_scalar(z[:], z[:], 3e38, 3e38, ALU.mult, ALU.mult).then_inc(z_ok, 1)
            dve.wait_ge(e_ok, 1)
            dve.wait_ge(z_ok, 3)
            dve.scalar_tensor_tensor(z[:], z[:], 0.0, e[:], ALU.mult, ALU.add).then_inc(z_ok, 1)
            dve.wait_ge(d_ok, 1)
            dve.wait_ge(z_ok, 4)
            dve.scalar_tensor_tensor(WF[:], d[:], 2.0, z[:], ALU.mult, ALU.add).then_inc(q_ok, 1)


def rotary_projections(nc, ctx, hTh, hTl, w_att, rope, q_parts, k_parts, V, WOh, WOl):
    with ExitStack() as mem:
        sb = lambda n, s, d: mem.enter_context(nc.sbuf_tensor("rp_" + n, s, d))
        sem = lambda n: ctx.enter_context(nc.semaphore("rp_" + n))
        pb = lambda n: mem.enter_context(nc.psum_tensor("rp_" + n, [P, TB], F32))
        NW5 = KT * 5 * HID
        Wh = sb("Wh", [P, NW5], F32R)
        Wl = sb("Wl", [P, NW5], F32R)
        WQ5 = KT * 6 * HID
        Wraw = sb("Wraw", [P, WQ5], F32)
        CS = sb("CS", [P, 2, SEQ], F32)
        QP = sb("QP", [P, NPART, BATCH, 2, SEQ], BF16)
        KP = sb("KP", [P, NPART, BATCH, 2, SEQ], BF16)
        RS = 4
        t1 = sb("t1", [P, RS, TB], F32)
        t2 = sb("t2", [P, RS, TB], F32)
        QB, SB_, VB = [pb("Q0"), pb("Q1")], [pb("S0"), pb("S1")], [pb("V0"), pb("V1")]
        w_in, h_ok, l_ok, v0_ok = sem("w_in"), sem("h_ok"), sem("l_ok"), sem("v0_ok")
        p_ok, m_ok, a_ok, p1_ok, r1_ok, p2_ok, p3_ok, out_ok = (sem(n) for n in
            ("p_ok", "m_ok", "a_ok", "p1_ok", "r1_ok", "p2_ok", "p3_ok", "out_ok"))
        vb_ok, ve_ok = sem("vb_ok"), sem("ve_ok")
        part = lambda dst, p, mt, tb: dst[:, p, tb // 2, mt, (tb % 2) * TB:(tb % 2 + 1) * TB]
        steps = [(dst, x, mt, 2 * b + t) for b in range(BATCH) for x, dst in ((0, QP), (2, KP))
                 for mt in range(2) for t in range(2)]
        NS = len(steps)
        col = lambda w, kt, x, mt: w[:, (kt * 5 + x) * HID + mt * P:(kt * 5 + x) * HID + (mt + 1) * P]
        block = mem.enter_context(nc.Block())

        @block.sync
        def _(sp):
            sp.dma_start(Wraw[:], w_att).then_inc(w_in, 16)
            sp.dma_start(CS[:], rope).then_inc(w_in, 16)
            for n in range(1, NS, 2):
                dst, x, mt, tb = steps[n]
                sp.wait_ge(p3_ok, n + 1)
                b = tb // 2
                sp.dma_start((q_parts, k_parts)[x // 2][b, :, :, :, mt].rearrange("r d i t -> (d i) r t"),
                             dst[:, :, b, mt]).then_inc(out_ok, 16)
            sp.wait_ge(out_ok, 16 * NS // 2)

        @block.tensor
        def _(pe):
            pe.wait_ge(l_ok, 2)
            for n, (dst, x, mt, tb) in enumerate(steps):
                if n >= 2:
                    pe.wait_ge(m_ok, 2 * (n - 1))
                for s, bank in ((x, QB[n % 2]), (x + 1, SB_[n % 2])):
                    for kt in range(KT):
                        hi, lo = (h[:, kt, tb * TB:(tb + 1) * TB] for h in (hTh, hTl))
                        a, c = col(Wh, kt, s, mt), col(Wl, kt, s, mt)
                        pe.matmul(bank[:], a, hi, start=kt == 0, stop=False)
                        pe.matmul(bank[:], a, lo, start=False, stop=False)
                        m = pe.matmul(bank[:], c, hi, start=False, stop=kt == KT - 1)
                m.then_inc(p_ok, 1)
            for n in range(NT // 2):
                if n >= 2:
                    pe.wait_ge(ve_ok, n - 1)
                for j in range(2):
                    t = 2 * n + j
                    for kt in range(KT):
                        hi, lo = (h[:, kt, t * P:(t + 1) * P] for h in (hTh, hTl))
                        a, c = (w[:, (kt * 5 + 4) * HID:(kt * 5 + 5) * HID] for w in (Wh, Wl))
                        o = VB[n % 2][:, j * HID:(j + 1) * HID]
                        pe.matmul(o, hi, a, start=kt == 0, stop=False)
                        pe.matmul(o, hi, c, start=False, stop=False)
                        m = pe.matmul(o, lo, a, start=False, stop=kt == KT - 1)
                m.then_inc(vb_ok, 1)

        @block.vector
        def _(dve):
            dve.memset(V[:], 0.0).then_inc(v0_ok, 1)
            dve.wait_ge(v0_ok, 1)
            dve.memset(V[:, :, :, SD:SD + 1], 1.0).then_inc(v0_ok, 1)
            for n in range(NS + 2):
                if n < NS:
                    dst, x, mt, tb = steps[n]
                    dve.wait_ge(p_ok, n + 1)
                    if n >= RS:
                        dve.wait_ge(p3_ok, n - RS + 1)
                    c = (tb % 2) * TB
                    dve.tensor_tensor(t1[:, n % RS, :], QB[n % 2][:], CS[:, 0, c:c + TB], ALU.mult).then_inc(m_ok, 1)
                    dve.tensor_tensor(t2[:, n % RS, :], SB_[n % 2][:], CS[:, 1, c:c + TB], ALU.mult).then_inc(m_ok, 1)
                if 1 <= n <= NS:
                    dst, x, mt, tb = steps[n - 1]
                    dve.wait_ge(p1_ok, n)
                    t = t1[:, (n - 1) % RS, :]
                    dve.tensor_tensor(t, t, part(dst, 0, mt, tb), ALU.subtract).then_inc(r1_ok, 1)
                if n >= 2:
                    dst, x, mt, tb = steps[n - 2]
                    dve.wait_ge(p2_ok, n - 1)
                    dve.tensor_tensor(part(dst, 2, mt, tb), t1[:, (n - 2) % RS, :], part(dst, 1, mt, tb),
                                      ALU.subtract).then_inc(p3_ok, 1)

        @block.scalar
        def _(act):
            act.wait_ge(w_in, 32)
            act.activation(Wh[:], Wraw[:, 0:NW5], ACT.Copy).then_inc(h_ok, 1)
            act.activation(WOh[:], Wraw[:, NW5:WQ5], ACT.Copy).then_inc(h_ok, 1)
            for n in range(NS + 1):
                if n < NS:
                    dst, x, mt, tb = steps[n]
                    act.wait_ge(a_ok, n + 1)
                    act.activation(part(dst, 0, mt, tb), t1[:, n % RS, :],
                                   ACT.Copy).then_inc(p1_ok, 1)
                if n >= 1:
                    dst, x, mt, tb = steps[n - 1]
                    act.wait_ge(r1_ok, n)
                    act.activation(part(dst, 1, mt, tb), t1[:, (n - 1) % RS, :],
                                   ACT.Copy).then_inc(p2_ok, 1)
            act.wait_ge(v0_ok, 2)
            for n in range(NT // 2):
                act.wait_ge(vb_ok, n + 1)
                act.activation(V[:, 2 * n:2 * n + 2, :, 0:SD],
                               VB[n % 2][:].rearrange("p (t h d) -> p t h d", t=2, h=SH),
                               ACT.Copy).then_inc(ve_ok, 1)

        @block.gpsimd
        def _(pool):
            pool.wait_ge(h_ok, 2)
            pool.tensor_tensor(Wl[:], Wraw[:, 0:NW5], Wh[:].bitcast(F32), ALU.subtract).then_inc(l_ok, 1)
            pool.tensor_tensor(WOl[:], Wraw[:, NW5:WQ5], WOh[:].bitcast(F32), ALU.subtract).then_inc(l_ok, 1)
            for n in range(NS):
                pool.wait_ge(m_ok, 2 * n + 2)
                pool.tensor_tensor(t1[:, n % RS, :], t1[:, n % RS, :], t2[:, n % RS, :], ALU.add).then_inc(a_ok, 1)


def causal_attention(nc, ctx, ident, masks_in, q_parts, k_parts, V, ATT):
    with ExitStack() as mem:
        sb = lambda n, s, d: mem.enter_context(nc.sbuf_tensor("ca_" + n, s, d))
        sem = lambda n: ctx.enter_context(nc.semaphore("ca_" + n))
        NG2 = BATCH * NG
        NSL = 3
        QS = [sb(f"QS{i}", [P, HG, SEQ], BF16) for i in range(NSL)]
        KS = [sb(f"KS{i}", [P, HG, SEQ], BF16) for i in range(NSL)]
        VG = [sb(f"VG{i}", [P, SEQ // P, HG, 32], F32) for i in range(2)]
        MK = sb("MK", [P, 3, P], BF16)
        MKf = sb("MKf", [P, 3, P], F32)
        PT = sb("PT", [P, 2, HG, TB], F32)
        mx = sb("mx", [P, 2, HG, 8, 2], F32)
        m = sb("m", [P, 2, 8], F32)
        mr = sb("mr", [P, 2, 2, 8], F32)
        NM = sb("NM", [P, HG, 8, MROWS], BF16)
        OT = sb("OT", [P, 2, TB], F32)
        rec = sb("rec", [P, 4, HG], F32)
        pb = lambda n, w=TB: mem.enter_context(nc.psum_tensor("ca_" + n, [P, w], F32))
        S1 = [pb("S10"), pb("S11")]
        ST = [pb("ST0", 2 * TB), pb("ST1", 2 * TB)]
        OB, AUX = pb("OB"), pb("AUX")
        AUXB = AUX[:].bitcast(BF16)
        mk_in, mk_ok, init_ok, one_ok = sem("mk_in"), sem("mk_ok"), sem("init_ok"), sem("one_ok")
        s_in = [sem(f"s_in{i}") for i in range(NSL)]
        v_in = [sem(f"v_in{i}") for i in range(2)]
        s1_ok, mx_ok, ch_ok, nm_ok, mt_ok, mtc_ok = (sem(n) for n in ("s1_ok", "mx_ok", "ch_ok", "nm_ok", "mt_ok", "mtc_ok"))
        st_ok, exp_ok, pv_ok, oc_ok, t_ok, rec_ok, nrm_ok = (sem(n) for n in
            ("st_ok", "exp_ok", "pv_ok", "oc_ok", "t_ok", "rec_ok", "nrm_ok"))
        Q_RUNS = ((0, 3), (0, 2), (0, 1))
        K_RUNS = ((0, 2), (0, 2), (0, 1), (2, 1))
        ND = len(Q_RUNS) + len(K_RUNS)
        segs = [(j, qt, s) for j in range(HG) for qt in range(8) for s in range(1 + (qt >= 4))]
        NSEG = len(segs)
        blocks = [(qb, kt) for qb in range(2) for kt in range(4 * qb + 4)]
        NM2 = len(blocks)
        NST = 2 * NM2
        BANKS = S1 + [t[:, h * TB:(h + 1) * TB] for t in ST for h in range(2)]
        SEGN = NSEG // NST
        LEAD = 10
        N_T1, N_T0 = 4, 13
        N_MX = {9: 0, 11: 1, 21: 2, 23: 3}

        def span(qb, kt):
            q0 = max(qb * TB, kt * P)
            return q0, (qb + 1) * TB - q0

        def segments(g, n):
            a = NSEG + LEAD + (g * NST + n) * SEGN
            return [(x // NSEG, x % NSEG) for x in range(a, a + SEGN) if x < NSEG * NG2]

        ahead = [(x // NSEG, x % NSEG) for x in range(NSEG + LEAD)]
        AUX_USES = [("mx", 0, j) for j in range(HG)]
        for g in range(NG2):
            for n in range(NST):
                if n == N_T1 and g >= 1:
                    AUX_USES.append(("out", g - 1, 1))
                if n == N_T0:
                    AUX_USES.append(("out", g, 0))
                if n in N_MX and g + 1 < NG2:
                    AUX_USES.append(("mx", g + 1, N_MX[n]))
        AUX_USES.append(("out", NG2 - 1, 1))

        def pass1_bank(at):
            if at < len(ahead):
                return BANKS[at % len(BANKS)], len(BANKS)
            return S1[at % 2], 1 if at < len(ahead) + 2 else 2

        block = mem.enter_context(nc.Block())

        @block.sync
        def _(sp):
            def load(g):
                hg, b = g // 2, g % 2
                for dst, src, runs in ((QS, q_parts, Q_RUNS), (KS, k_parts, K_RUNS)):
                    row = 0
                    for p0, np_ in runs:
                        sp.dma_start(dst[g % NSL][row:row + SD * np_, :, :].rearrange("r j t -> r (j t)"),
                                     src[b, p0:p0 + np_, :, 2 * hg:2 * hg + 2].rearrange("r d i m t -> (r d) (i m t)")
                                     ).then_inc(s_in[g % NSL], 16)
                        row += SD * np_

            def values(g):
                if g >= 2:
                    sp.wait_ge(pv_ok, NM2 * (g - 1))
                sp.dma_start(VG[g % 2][:], V[:, 8 * (g % 2):8 * (g % 2) + 8, HG * (g // 2):HG * (g // 2) + HG, :]
                             ).then_inc(v_in[g % 2], 16)

            sp.dma_start(MKf[:], masks_in).then_inc(mk_in, 16)
            load(0)
            load(1)
            values(0)
            load(2)
            values(1)
            for g in range(3, NG2):
                sp.wait_ge(st_ok, NST * (g - 2))
                load(g)
                values(g - 1)
            values(NG2 - 1)

        @block.gpsimd
        def _(pool):
            for b in range(NSL):
                if b:
                    pool.wait_ge(one_ok, b)
                pool.memset(KS[b][SROWS:KROWS, :, :], 1.0).then_inc(one_ok, 1)

        @block.tensor
        def _(pe):
            def aux_free(use):
                at = AUX_USES.index(use)
                if at:
                    kind = AUX_USES[at - 1][0]
                    count = sum(u[0] == kind for u in AUX_USES[:at])
                    pe.wait_ge(mtc_ok if kind == "mx" else nrm_ok, count)

            def pass1(g, s):
                j, qt, half = segs[s]
                at = NSEG * g + s
                if s == 0:
                    pe.wait_ge(s_in[g % NSL], 16 * ND * (g // NSL + 1))
                bank, behind = pass1_bank(at)
                if at >= behind:
                    pe.wait_ge(mx_ok, at - behind + 1)
                Q, K = QS[g % NSL], KS[g % NSL]
                k0, k1 = half * TB, min((half + 1) * TB, (qt + 1) * P)
                ins = pe.matmul(bank[:, 0:k1 - k0], Q[0:SROWS, j, qt * P:(qt + 1) * P], K[0:SROWS, j, k0:k1],
                                start=True, stop=True)
                if k1 == (qt + 1) * P:
                    ins = pe.matmul(bank[:, k1 - P - k0:k1 - k0], MK[:, 0, :], MK[:, 1, :], start=False, stop=True,
                                    skip_group_check=True)
                ins.then_inc(s1_ok, 1)

            def maxima(g, j):
                if j % 2 == 0:
                    pe.wait_ge(nm_ok, 2 * g + j // 2 + 1)
                aux_free(("mx", g, j))
                for qt in range(8):
                    ins = pe.transpose(AUXB[SROWS:KROWS, qt * P:(qt + 1) * P], NM[:, j, qt, :], MK[:, 0, :])
                ins.then_inc(mt_ok, 1)

            def pass2(g, n, h):
                qb, kt = blocks[n // 2]
                q0, w = span(qb, kt)
                if n < 2 and h == 0:
                    pe.wait_ge(mtc_ok, HG * g + 2 * n + 2)
                if h == 0 and NST * g + n >= 2:
                    pe.wait_ge(exp_ok, NST * g + n - 1)
                j = 2 * (n % 2) + h
                out = ST[n % 2][:, h * TB:h * TB + w]
                ins = pe.matmul(out, KS[g % NSL][0:KROWS, j, kt * P:(kt + 1) * P], QS[g % NSL][0:KROWS, j, q0:q0 + w],
                                start=True, stop=True)
                if kt >= 4 * qb:
                    ins = pe.matmul(out[:, 0:P], MK[:, 0, :], MK[:, 2, :], start=False, stop=True,
                                    skip_group_check=True)
                if h == 1:
                    ins.then_inc(st_ok, 1)

            def values(g, mm):
                qb, kt = blocks[mm]
                q0, w = span(qb, kt)
                pe.wait_ge(exp_ok, NST * g + 2 * mm + 2)
                if mm == 0:
                    pe.wait_ge(v_in[g % 2], 16 * (g // 2 + 1))
                if kt == 0 and 2 * g + qb >= 1:
                    pe.wait_ge(oc_ok, 2 * g + qb)
                for j in range(HG):
                    ins = pe.matmul(OB[32 * j:32 * j + 32, q0 - qb * TB:q0 - qb * TB + w], VG[g % 2][:, kt, j, :],
                                    PT[:, mm % 2, j, 0:w], start=kt == 0, stop=kt == 4 * qb + 3,
                                    skip_group_check=True)
                ins.then_inc(pv_ok, 1)

            def back(g, qb):
                pe.wait_ge(oc_ok, 2 * g + qb + 1)
                aux_free(("out", g, qb))
                for t in range(4):
                    ins = pe.transpose(AUX[:, t * P:(t + 1) * P], OT[:, qb, t * P:(t + 1) * P], ident[:])
                ins.then_inc(t_ok, 1)

            pe.wait_ge(mk_ok, 1)
            pe.wait_ge(one_ok, NSL)
            for g, s in ahead:
                pass1(g, s)
            for j in range(HG):
                maxima(0, j)
            pe.wait_ge(mx_ok, len(ahead))
            for g in range(NG2):
                for n in range(NST):
                    todo = segments(g, n)
                    for h in range(2):
                        pass2(g, n, h)
                        for gs, s in todo[h:h + 1]:
                            pass1(gs, s)
                    if n == 1 and g >= 1:
                        values(g - 1, NM2 - 1)
                    if n % 2 == 1 and n >= 3:
                        values(g, (n - 3) // 2)
                    if n == N_T1 and g >= 1:
                        back(g - 1, 1)
                    if n == N_T0:
                        back(g, 0)
                    if n in N_MX and g + 1 < NG2:
                        maxima(g + 1, N_MX[n])
            values(NG2 - 1, NM2 - 1)
            back(NG2 - 1, 1)

        @block.scalar
        def _(act):
            def maxima(g, j):
                act.wait_ge(mt_ok, HG * g + j + 1)
                act.activation(QS[g % NSL][SROWS:KROWS, j, :], AUXB[SROWS:KROWS, :], ACT.Copy).then_inc(mtc_ok, 1)

            def outputs(g, qb):
                act.wait_ge(pv_ok, NM2 * g + (NM2 if qb else 4))
                act.activation(OT[:, qb, :], OB[:], ACT.Copy).then_inc(oc_ok, 1)

            for j in range(HG):
                maxima(0, j)
            for g in range(NG2):
                for n in range(NST):
                    mm = n // 2
                    q0, w = span(*blocks[mm])
                    act.wait_ge(st_ok, NST * g + n + 1)
                    if n % 2 == 0 and NM2 * g + mm >= 2:
                        act.wait_ge(pv_ok, NM2 * g + mm - 1)
                    hh = n % 2
                    act.activation(PT[:, mm % 2, 2 * hh:2 * hh + 2, 0:w],
                                   ST[n % 2][:].rearrange("p (h q) -> p h q", h=2)[:, :, 0:w],
                                   ACT.Exp, scale=SCALE).then_inc(exp_ok, 1)
                    if n == 1 and g >= 1:
                        outputs(g - 1, 1)
                    if n == N_T0 - 3:
                        outputs(g, 0)
                    if n in N_MX and g + 1 < NG2:
                        maxima(g + 1, N_MX[n])
            outputs(NG2 - 1, 1)

        @block.vector
        def _(dve):
            def pass1(g, s):
                j, qt, half = segs[s]
                at = NSEG * g + s
                dve.wait_ge(s1_ok, at + 1)
                w = min(TB, (qt + 1) * P - half * TB)
                dve.reduce_max(mx[:, g % 2, j, qt, half:half + 1], pass1_bank(at)[0][:, 0:w], AXX).then_inc(mx_ok, 1)
                if s % (NSEG // 2) == NSEG // 2 - 1:
                    parts(g, j // 2)

            def parts(g, i):
                n = 5 * (2 * g + i)
                j = slice(2 * i, 2 * i + 2)
                dve.wait_ge(mx_ok, NSEG * g + (i + 1) * NSEG // 2)
                if g >= 1:
                    dve.wait_ge(mt_ok, HG * (g - 1) + 2 * i + 2)
                dve.tensor_tensor(m[:], mx[:, g % 2, j, :, 0], mx[:, g % 2, j, :, 1], ALU.max).then_inc(ch_ok, 1)
                dve.wait_ge(ch_ok, n + 1)
                dve.tensor_scalar(NM[:, j, :, 0], m[:], -1.0, None, ALU.mult).then_inc(ch_ok, 1)
                dve.wait_ge(ch_ok, n + 2)
                dve.scalar_tensor_tensor(mr[:, 0, :, :], m[:], -1.0, NM[:, j, :, 0], ALU.mult,
                                         ALU.subtract).then_inc(ch_ok, 1)
                dve.wait_ge(ch_ok, n + 3)
                dve.tensor_copy(NM[:, j, :, 1], mr[:, 0, :, :]).then_inc(ch_ok, 1)
                dve.wait_ge(ch_ok, n + 4)
                dve.tensor_tensor(mr[:, 1, :, :], mr[:, 0, :, :], NM[:, j, :, 1], ALU.subtract).then_inc(ch_ok, 1)
                dve.wait_ge(ch_ok, n + 5)
                dve.tensor_copy(NM[:, j, :, 2], mr[:, 1, :, :]).then_inc(nm_ok, 1)

            def normalise(g, qb):
                dve.wait_ge(t_ok, 2 * g + qb + 1)
                o = AUX[:].rearrange("p (t j e) -> p t j e", t=4, j=HG)
                dve.reciprocal(rec[:], o[:, :, :, SD]).then_inc(rec_ok, 1)
                dve.wait_ge(rec_ok, 2 * g + qb + 1)
                t = 8 * (g % 2) + 4 * qb
                dve.tensor_tensor(ATT[:, t:t + 4, 64 * (g // 2):64 * (g // 2) + 64].rearrange(
                                      "p t (j d) -> p t j d", j=HG),
                                  o[:, :, :, 0:SD], rec[:].unsqueeze(3).broadcast_to([P, 4, HG, SD]),
                                  ALU.mult).then_inc(nrm_ok, 1)

            dve.memset(mx[:], -3e38).then_inc(init_ok, 1)
            dve.wait_ge(mk_in, 16)
            dve.tensor_copy(MK[:], MKf[:]).then_inc(mk_ok, 1)
            dve.wait_ge(init_ok, 1)
            for g, s in ahead:
                pass1(g, s)
            for g in range(NG2):
                for n in range(NST):
                    for gs, s in segments(g, n):
                        pass1(gs, s)
                    if n == N_T1 and g >= 1:
                        normalise(g - 1, 1)
                    if n == N_T0:
                        normalise(g, 0)
            normalise(NG2 - 1, 1)


def out_projection(nc, ctx, X, hTh, hTl, WOh, WOl):
    with ExitStack() as mem:
        sem = lambda n: ctx.enter_context(nc.semaphore("op_" + n))
        banks = [mem.enter_context(nc.psum_tensor(f"op_{i}", [P, TB], F32)) for i in range(4)]
        p_ok, x_ok = sem("p_ok"), sem("x_ok")
        block = mem.enter_context(nc.Block())

        @block.tensor
        def _(pe):
            for n in range(NT // 2):
                if n >= 4:
                    pe.wait_ge(x_ok, n - 3)
                for j in range(2):
                    t = 2 * n + j
                    o = banks[n % 4][:, j * HID:(j + 1) * HID]
                    for kt in range(KT):
                        hi, lo = (h[:, kt, t * P:(t + 1) * P] for h in (hTh, hTl))
                        a, c = (w[:, kt * HID:(kt + 1) * HID] for w in (WOh, WOl))
                        pe.matmul(o, hi, a, start=kt == 0, stop=False)
                        pe.matmul(o, hi, c, start=False, stop=False)
                        m = pe.matmul(o, lo, a, start=False, stop=kt == KT - 1)
                m.then_inc(p_ok, 1)

        @block.vector
        def _(dve):
            for n in range(NT // 2):
                dve.wait_ge(p_ok, n + 1)
                dve.tensor_tensor(X[:, 2 * n:2 * n + 2, :], banks[n % 4][:].rearrange("p (t n) -> p t n", t=2),
                                  X[:, 2 * n:2 * n + 2, :], ALU.add).then_inc(x_ok, 1)


def program(nc, hidden, ident_in, w_quads, nw_quads, c_quads, w_ffn, s_ffn, d_ffn, w_att, rope, masks, out):
    with ExitStack() as ctx:
        sb = lambda n, s, d, c=ctx: c.enter_context(nc.sbuf_tensor(n, s, d))
        X = sb("X", [P, NT, HID], F32)
        ident = sb("ident", [P, P], F32)

        def normed(c, name):
            return sb(name + "hTh", [P, KT, TOK], F32R, c), sb(name + "hTl", [P, KT, TOK], F32R, c)

        with ExitStack() as part:
            hTh, hTl = normed(part, "a_")
            layer_norm_transposed(nc, ctx, "ln1_", X, ident, hTh, hTl, load=(hidden, ident_in))
            linear_attention(nc, ctx, X, ident, hTh, hTl, hidden, w_quads, nw_quads, c_quads)

        WF = sb("WF", [P, 2 * KT * FI + NI * HID], F32R)
        SCL = sb("SCL", [P, 2 * NI], F32)
        DS = sb("DS", [P, HID], F32)
        quantised_weights(nc, ctx, w_ffn, s_ffn, d_ffn, WF, SCL, DS)
        with ExitStack() as part:
            hTh, hTl = normed(part, "b_")
            layer_norm_transposed(nc, ctx, "ln2_", X, ident, hTh, hTl)
            ffn(nc, ctx, "f1_", X, hTh, hTl, WF, SCL, DS)

        with ExitStack() as att:
            WOh = sb("WOh", [P, KT * HID], F32R, att)
            WOl = sb("WOl", [P, KT * HID], F32R, att)
            with ExitStack() as heads:
                q_parts, k_parts = (nc.dram_tensor(n, (BATCH, NPART, SD, SH // 2, 2, SEQ), BF16).ap()
                                    for n in ("q_parts", "k_parts"))
                V = sb("V", [P, NT, SH, 32], F32, heads)
                with ExitStack() as part:
                    hTh, hTl = normed(part, "c_")
                    layer_norm_transposed(nc, ctx, "ln3_", X, ident, hTh, hTl)
                    rotary_projections(nc, ctx, hTh, hTl, w_att, rope, q_parts, k_parts, V, WOh, WOl)
                ATT = sb("ATT", [P, NT, HID], F32, heads)
                causal_attention(nc, ctx, ident, masks, q_parts, k_parts, V, ATT)
                with ExitStack() as part:
                    hTh, hTl = normed(part, "d_")
                    layer_norm_transposed(nc, ctx, "at_", ATT, ident, hTh, hTl, norm=False)
                    out_projection(nc, ctx, X, hTh, hTl, WOh, WOl)

        with ExitStack() as part:
            hTh, hTl = normed(part, "e_")
            layer_norm_transposed(nc, ctx, "ln4_", X, ident, hTh, hTl)
            ffn(nc, ctx, "f2_", X, hTh, hTl, WF, SCL, DS, out)


def rotary_constants():
    import numpy as np
    half = SD // 2
    inv = (np.float32(1.0) / np.float32(10000.0) ** (np.arange(half, dtype=np.float32) / np.float32(half)))
    f = (np.arange(SEQ, dtype=np.float32)[None, :] * inv.astype(np.float32)[:, None]).astype(np.float32)
    row = np.arange(P) // (SH // 2)
    cos = np.cos(f.astype(np.float64))[row // 2]
    sin = np.sin(f.astype(np.float64))[row // 2] * np.where(row % 2 == 0, -1.0, 1.0)[:, None]
    rope = np.stack([cos, sin], 1).astype(np.float32)
    masks = np.zeros((P, 3, P), np.float32)
    masks[:, 0] = np.eye(P)
    masks[:, 1] = np.triu(np.full((P, P), -1e30), 1)
    masks[:, 2] = np.tril(np.full((P, P), -1e30), -1)
    return rope, masks


def linear_constants():
    import numpy as np
    r = (1.0 / 2.0 ** (8.0 / LH)) ** (np.arange(LH, dtype=np.float64) + 1.0)
    slope = np.float32(r * (1.0 + 1e-5)).astype(np.float64)
    i = np.arange(P, dtype=np.float64)
    diff = i[None, :] - i[:, None]
    D = np.where(diff >= 0, np.exp(-slope[:, None, None] * np.maximum(diff, 0)), 0.0)
    QD = np.exp(-slope[:, None] * (i + 1))
    KD = np.exp(-slope[:, None] * (P - 1 - i))
    BD = np.exp(-slope * P)
    c = np.zeros((NQ, P, CW), np.float32)
    for n in range(NQ):
        for h in range(4):
            c[n, :, CD + h * P:CD + (h + 1) * P] = D[4 * n + h]
            c[n, :, CK + h] = KD[4 * n + h]
            rows = slice((h % 2) * LD, (h % 2 + 1) * LD)
            c[n, rows, CQ + (h // 2) * P:CQ + (h // 2 + 1) * P] = QD[4 * n + h]
            c[n, rows, CB + h // 2] = BD[4 * n + h]
    return c


def kernel(**inputs):
    import numpy as np
    import concourse.bacc as bacc
    from concourse.bass_utils import run_bass_kernel_spmd

    a = {n: np.asarray(x) for n, x in inputs.items()}
    hidden = a["L0_attn_a_hidden_states"].reshape(NT, P, HID).transpose(1, 0, 2)
    qkv = a["L0_attn_a_qkv_w"].reshape(NQ, 2, 2, 3, LD, KT, P)
    gate = a["L0_attn_a_gate_w"].reshape(NQ, 4 * LD, KT, P)
    cols = [qkv[:, :, :, 0].reshape(NQ, 4 * LD, KT, P), qkv[:, :, :, 1].reshape(NQ, 4 * LD, KT, P), gate,
            qkv[:, :, :, 2].reshape(NQ, 4 * LD, KT, P)]
    wq = np.concatenate(cols, 1).transpose(0, 3, 2, 1).reshape(NQ, P, KT * QW)
    wo = a["L0_attn_a_out_w"].T.reshape(NQ, 2, P, HID).transpose(0, 2, 1, 3).reshape(NQ, P, 2 * HID)
    arrays = {
        "hidden": hidden, "ident": np.eye(P, dtype=np.float32),
        "w_quads": np.concatenate([wq, wo], 2),
        "nw_quads": a["L0_attn_a_norm_w"].reshape(NQ, 2, P).transpose(0, 2, 1),
        "c_quads": linear_constants(),
    }
    up = [a["L0_ffn_" + n].reshape(KT, P, FI).transpose(1, 0, 2).reshape(P, KT * FI) for n in ("gate_w", "up_w")]
    down = a["L0_ffn_down_w"].reshape(NI, P, HID).transpose(1, 0, 2).reshape(P, NI * HID)
    arrays["w_ffn"] = np.concatenate(up + [down], 1)
    arrays["s_ffn"] = np.concatenate([a["L0_ffn_" + n].reshape(NI, P).T for n in ("gate_scale", "up_scale")], 1)
    arrays["d_ffn"] = np.broadcast_to(a["L0_ffn_down_scale"], (P, HID))
    pairs = np.arange(HID) ^ (SH // 2)
    wq, wk, wv, wo = (a["L0_attn_b_W" + n] for n in "qkvo")
    wq, wk = (w.reshape(SH // 2, 2, SD, HID).transpose(1, 2, 0, 3).reshape(HID, HID) for w in (wq, wk))
    w5 = np.stack([w.T.reshape(KT, P, HID) for w in (wq, wq[pairs], wk, wk[pairs], wv)], 2)
    wo = wo.T.reshape(KT, P, HID).transpose(1, 0, 2).reshape(P, KT * HID)
    arrays["w_att"] = np.concatenate([w5.transpose(1, 0, 2, 3).reshape(P, KT * 5 * HID), wo], 1)
    rope, masks = rotary_constants()
    arrays["rope"] = rope
    arrays["masks"] = masks
    nc = bacc.Bacc("TRN2", target_bir_lowering=False, num_devices=1)
    args, arr = [], {}
    for name, x in arrays.items():
        x = np.ascontiguousarray(x)
        arr[name + "_dram"] = x
        args.append(nc.dram_tensor(name + "_dram", x.shape, mybir.dt.from_np(x.dtype), kind="ExternalInput").ap())
    args.append(nc.dram_tensor("out_dram", (P, NT, HID), F32, kind="ExternalOutput").ap())
    program(nc, *args)
    r = run_bass_kernel_spmd(nc, [arr], core_ids=[0])
    return r.results[0]["out_dram"].transpose(1, 0, 2).reshape(BATCH, SEQ, HID)
```

```python
import concourse.bass as bass
from concourse import mybir
from contextlib import ExitStack

F32 = mybir.dt.float32
F32R = mybir.dt.float32r
BF16 = mybir.dt.bfloat16
FP8 = mybir.dt.float8e4
ALU = mybir.AluOpType
ACT = mybir.ActivationFunctionType
AXX = mybir.AxisListType.X

P = 128
BATCH, SEQ, HID = 2, 1024, 256
TOK = BATCH * SEQ
NT = TOK // P
KT = HID // P
TB = 512
NTB = TOK // TB
EPS = 1e-5

LH, LD = 32, 64
FEAT = LH * LD
NQ = LH // 4
QW = 8 * P
OFF_Q, OFF_K, OFF_G, OFF_V = 0, 2 * P, 4 * P, 6 * P
GC = 4
NU = BATCH * 2 * 2
CD, CQ, CK, CB = 0, 4 * P, 6 * P, 6 * P + 4
CW = 6 * P + 6
WQ = KT * QW
WTOT = WQ + 2 * HID

FI = 768
NI = FI // P

SH, SD = 16, 16
NPART = 3
SROWS = 6 * SD
MROWS = NPART
KROWS = SROWS + MROWS
HG = 4
NG = SH // HG
SCALE = SD ** -0.5


def norm_steps(nc, ctx, mem, name, X, ident, hTh, hTl, banks, load=None, norm=True, H=None):
    sb = lambda n, s, d: mem.enter_context(nc.sbuf_tensor(name + n, s, d))
    sem = lambda n: ctx.enter_context(nc.semaphore(name + n))
    if norm:
        stats = sb("stats", [P, NT, 6], F32)
        mv = sb("mv", [P, NT, 2], F32)
        std = sb("std", [P, NT], F32)
        rstd = sb("rstd", [P, NT], F32)
        epst = sb("epst", [P, 1], F32)
        eps_ok, stats_ok, mv_ok, std_ok = sem("eps_ok"), sem("stats_ok"), sem("mv_ok"), sem("std_ok")
        rstd_ok, h_ok = sem("rstd_ok"), sem("h_ok")
    if H is None:
        H = sb("H", [P, NT, HID], F32) if norm else X
    if load is not None:
        id_in, x_in = sem("id_in"), [sem(f"x_in{b}") for b in range(NTB)]
    t_ok, hi_ok, lo_ok = sem("t_ok"), sem("hi_ok"), sem("lo_ok")
    NBK = len(banks)
    TPB = NT // NTB
    at = lambda b: slice(TPB * b, TPB * (b + 1))

    def sync(sp, b):
        sp.dma_start(X[:, at(b), :], load[0][:, at(b), :]).then_inc(x_in[b], 16)
        if b == 0:
            sp.dma_start(ident[:], load[1]).then_inc(id_in, 16)

    def moments(dve, b):
        if b == 0:
            dve.memset(epst[:], EPS).then_inc(eps_ok, 1)
        if load is not None:
            dve.wait_ge(x_in[b], 16)
        for t in range(TPB * b, TPB * (b + 1)):
            dve.bn_stats(stats[:, t, :], X[:, t, :]).then_inc(stats_ok, 1)
        for t in range(TPB * b, TPB * (b + 1)):
            dve.wait_ge(stats_ok, t + 1)
            dve.bn_aggr(mv[:, t, :], stats[:, t, :]).then_inc(mv_ok, 1)

    def deviation(act, b):
        if b == 0:
            act.wait_ge(eps_ok, 1)
        act.wait_ge(mv_ok, TPB * (b + 1))
        act.activation(std[:, at(b)], mv[:, at(b), 1], ACT.Sqrt, bias=epst[:]).then_inc(std_ok, 1)

    def normalise(dve, b):
        dve.wait_ge(std_ok, b + 1)
        dve.reciprocal(rstd[:, at(b)], std[:, at(b)]).then_inc(rstd_ok, 1)
        dve.wait_ge(rstd_ok, b + 1)
        for t in range(TPB * b, TPB * (b + 1)):
            dve.tensor_scalar(H[:, t, :], X[:, t, :], mv[:, t, 0:1], rstd[:, t:t + 1],
                              ALU.subtract, ALU.mult).then_inc(h_ok, 1)

    def turn(pe, b):
        if load is not None and b == 0:
            pe.wait_ge(id_in, 16)
        if norm:
            pe.wait_ge(h_ok, TPB * (b + 1))
        for k in range(KT):
            n = b * KT + k
            if n >= NBK:
                pe.wait_ge(lo_ok, n - NBK + 1)
            for j in range(TPB):
                last = pe.transpose(banks[n % NBK][:, j * P:(j + 1) * P],
                                    H[:, TPB * b + j, k * P:(k + 1) * P], ident[:])
            last.then_inc(t_ok, 1)

    def high(act, b):
        for k in range(KT):
            n = b * KT + k
            act.wait_ge(t_ok, n + 1)
            act.activation(hTh[:, k, b * TB:(b + 1) * TB], banks[n % NBK][:], ACT.Copy).then_inc(hi_ok, 1)

    def low(dve, b):
        for k in range(KT):
            n = b * KT + k
            dve.wait_ge(hi_ok, n + 1)
            dve.tensor_tensor(hTl[:, k, b * TB:(b + 1) * TB], banks[n % NBK][:],
                              hTh[:, k, b * TB:(b + 1) * TB].bitcast(F32), ALU.subtract).then_inc(lo_ok, 1)

    def ready(pe, b):
        pe.wait_ge(lo_ok, KT * (b + 1))

    return {"sync": sync, "moments": moments, "deviation": deviation, "normalise": normalise, "turn": turn,
            "high": high, "low": low, "ready": ready, "h_ok": h_ok if norm else None}


def linear_attention(nc, ctx, X, ident, ident_in, hTh, hTl, hidden, w_quads, nw_quads, c_quads):
    with ExitStack() as mem:
        sb = lambda n, s, d: mem.enter_context(nc.sbuf_tensor("la_" + n, s, d))
        sem = lambda n: ctx.enter_context(nc.semaphore("la_" + n))
        Wraw = sb("Wraw", [P, WTOT], F32)
        Wh = sb("Wh", [P, WTOT], F32R)
        Wl = sb("Wl", [P, WTOT], F32R)
        C = sb("C", [P, CW], F32)
        NW = sb("NW", [P, 2], F32)
        q = sb("q", [P, 2, TOK], F32)
        k = sb("k", [P, 2, TOK], F32)
        g = sb("g", [P, 2, TOK], F32)
        v = sb("v", [P, NT, 4 * LD], F32)
        acc = X
        sqacc = sb("sqacc", [P, TOK], F32)
        qd = sb("qd", [P, 2, TB], F32)
        kd = sb("kd", [P, 2, TB], F32)
        A = sb("A", [P, 2, 2, TB], F32)
        S = sb("S", [P, 4, 4, P], F32)
        y = sb("y", [P, 2, TB], F32)
        yh = sb("yh", [P, 4, TB], F32R)
        yl = sb("yl", [P, 4, TB], F32R)
        sq = sb("sq", [P, 2, TB], F32)
        ones = sb("ones", [P, 1], F32)
        epst = sb("epst", [P, 1], F32)
        std = sb("std", [P, NT], F32)
        rstd = sb("rstd", [P, NT], F32)
        pb = lambda n: mem.enter_context(nc.psum_tensor("la_" + n, [P, TB], F32))
        SC = [[pb("SA0"), pb("SB0")], [pb("SA1"), pb("SB1")]]
        PR = [SC[0][0], SC[0][1], SC[1][0], SC[1][1]]
        KB, UB, OB, RB = pb("KB"), pb("UB"), pb("OB"), pb("RB")

        w_in, c_in, x_in = sem("w_in"), sem("c_in"), sem("x_in")
        wh_ok, w_ok, wo_ok = sem("wh_ok"), sem("w_ok"), sem("wo_ok")
        init_ok, zero_ok = sem("init_ok"), sem("zero_ok")
        proj_ok, silu_ok = sem("proj_ok"), sem("silu_ok")
        sc_ok, mask_ok, kb_ok, kd_ok, qd_ok = sem("sc_ok"), sem("mask_ok"), sem("kb_ok"), sem("kd_ok"), sem("qd_ok")
        u_ok, s_link, s_ok, o_ok = sem("u_ok"), sem("s_link"), sem("s_ok"), sem("o_ok")
        sq_ok, y_ok, yh_ok, yl_ok, sqa_ok = sem("sq_ok"), sem("y_ok"), sem("yh_ok"), sem("yl_ok"), sem("sqa_ok")
        r_ok, acc_ok = sem("r_ok"), sem("acc_ok")
        ss_ok, std_ok, rstd_ok = sem("ss_ok"), sem("std_ok"), sem("rstd_ok")

        ln = norm_steps(nc, ctx, mem, "ln1_", X, ident, hTh, hTl, [KB, UB, OB, RB], (hidden, ident_in), H=v)

        def unit(u):
            half, b, pr = u // 4, u // 2 % 2, u % 2
            return half, b, pr, b * SEQ + half * TB, b * 2 + pr

        BANK = [n % 4 for n in range(28)] + [2, 3, 2, 3]
        def token_tiles(half):
            return [b * (SEQ // P) + half * GC + c for b in range(BATCH) for c in range(GC)]

        NLINK = 2 * 2 * 2 * (4 + 3)

        block = mem.enter_context(nc.Block())

        @block.sync
        def _(sp):
            for s in (r_ok, o_ok, y_ok, kd_ok, u_ok, sqa_ok, yl_ok, acc_ok, s_ok, sq_ok, mask_ok):
                sp.sem_inc(s, 1)
            for b in range(NTB):
                ln["sync"](sp, b)
                if b == 1:
                    sp.dma_start(Wraw[:], w_quads[0, :, :]).then_inc(w_in, 16)
            sp.dma_start(C[:], c_quads[0, :, :]).then_inc(c_in, 16)
            sp.dma_start(NW[:], nw_quads[0, :, :]).then_inc(c_in, 16)
            for i in range(1, NQ):
                sp.wait_ge(wo_ok, i)
                sp.dma_start(Wraw[:], w_quads[i, :, :]).then_inc(w_in, 16)
                sp.wait_ge(kd_ok, 16 * i + 1)
                sp.wait_ge(qd_ok, 8 * i)
                sp.wait_ge(y_ok, 8 * i + 1)
                sp.wait_ge(s_ok, 8 * i + 1)
                sp.dma_start(C[:], c_quads[i, :, :]).then_inc(c_in, 16)
                sp.dma_start(NW[:], nw_quads[i, :, :]).then_inc(c_in, 16)
            sp.wait_ge(sc_ok, 8 * NQ)
            sp.wait_ge(qd_ok, 8 * NQ)
            sp.dma_start(q[:].rearrange("p a n -> p (a n)"), hidden.rearrange("p t n -> p (t n)")).then_inc(x_in, 16)

        @block.gpsimd
        def _(pool):
            pool.wait_ge(wh_ok, 1)
            pool.tensor_tensor(Wl[:, 0:WQ], Wraw[:, 0:WQ], Wh[:, 0:WQ].bitcast(F32),
                               ALU.subtract).then_inc(w_ok, 1)
            pool.wait_ge(ln["h_ok"], NT)
            pool.memset(acc[:], 0.0).then_inc(init_ok, 1)
            pool.memset(sqacc[:], 0.0).then_inc(init_ok, 1)
            pool.memset(ones[:], 1.0).then_inc(init_ok, 1)
            pool.memset(epst[:], EPS).then_inc(init_ok, 1)
            pool.memset(S[:], 0.0).then_inc(zero_ok, 1)

            def quad(i, last):
                pool.wait_ge(wh_ok, 2 * i + 2)
                pool.tensor_tensor(Wl[:, WQ:WTOT], Wraw[:, WQ:WTOT], Wh[:, WQ:WTOT].bitcast(F32),
                                   ALU.subtract).then_inc(wo_ok, 1)
                pool.wait_ge(silu_ok, 32 * i + 8)
                pool.wait_ge(c_in, 32 * i + 32)
                for u in range(NU + 1):
                    if u < NU:
                        half, b, pr, col, ch = unit(u)
                        if u >= 2:
                            pool.wait_ge(o_ok, 8 * i + u)
                        else:
                            pool.wait_ge(o_ok, 8 * i + 1)
                        pool.tensor_tensor(
                            qd[:, u % 2, :].rearrange("p (c t) -> p c t", c=GC),
                            q[:, pr, col:col + TB].rearrange("p (c t) -> p c t", c=GC),
                            C[:, CQ + pr * P:CQ + (pr + 1) * P].unsqueeze(1).broadcast_to([P, GC, P]),
                            ALU.mult).then_inc(qd_ok, 1)
                    if u == 4 and not last:
                        pool.wait_ge(wh_ok, 2 * i + 3)
                        pool.tensor_tensor(Wl[:, 0:WQ], Wraw[:, 0:WQ], Wh[:, 0:WQ].bitcast(F32),
                                           ALU.subtract).then_inc(w_ok, 1)
                    if u >= 1:
                        w = u - 1
                        half, b, pr, col, ch = unit(w)
                        pool.wait_ge(yh_ok, 8 * i + w + 1)
                        if w >= 4:
                            pool.wait_ge(r_ok, 8 * i + 2 * (w // 2) - 1)
                        else:
                            pool.wait_ge(r_ok, 8 * i + 1)
                        pool.tensor_tensor(yl[:, w % 4, :], y[:, w % 2, :], yh[:, w % 4, :].bitcast(F32),
                                           ALU.subtract).then_inc(yl_ok, 1)
                        pool.wait_ge(sq_ok, 8 * i + w + 2)
                        if w == 0:
                            pool.wait_ge(init_ok, 4)
                        pool.wait_ge(sqa_ok, 8 * i + w + 1)
                        pool.tensor_tensor(sqacc[:, col:col + TB], sqacc[:, col:col + TB], sq[:, w % 2, :],
                                           ALU.add).then_inc(sqa_ok, 1)

            with pool.Fori(0, NQ - 1) as i:
                quad(i, False)
            quad(NQ - 1, True)

        @block.scalar
        def _(act):
            def quad(i):
                def keys(u):
                    half, b, pr, col, ch = unit(u)
                    act.wait_ge(kb_ok, 8 * i + u + 1)
                    if u >= 2:
                        act.wait_ge(u_ok, 8 * i + u)
                    else:
                        act.wait_ge(u_ok, 8 * i + 1)
                    kdv = kd[:, u % 2, :].rearrange("p (c n) -> p c n", c=GC)
                    kbv = KB[:].rearrange("p (c n) -> p c n", c=GC)
                    for h in range(2):
                        act.activation(kdv[:, :, h * LD:(h + 1) * LD], kbv[:, :, h * LD:(h + 1) * LD],
                                       ACT.Copy, scale=C[:, CK + 2 * pr + h:CK + 2 * pr + h + 1]
                                       ).then_inc(kd_ok, 1)

                for n in range(32):
                    act.wait_ge(proj_ok, 32 * i + n + 1)
                    bank = PR[BANK[n]]
                    if n < 16:
                        pr, tb = n // 4 % 2, n % 4
                        dst = (q if n < 8 else k)[:, pr, tb * TB:(tb + 1) * TB]
                        act.activation(dst, bank[:], ACT.Silu).then_inc(silu_ok, 1)
                    elif n < 24:
                        t = 2 * (n - 16)
                        act.activation(v[:, t:t + 2, :], bank[:].rearrange("p (t n) -> p t n", t=2),
                                       ACT.Silu).then_inc(silu_ok, 1)
                    else:
                        if n == 24:
                            act.wait_ge(y_ok, 8 * i + 1)
                        pr, tb = n // 4 % 2, n % 4
                        act.activation(g[:, pr, tb * TB:(tb + 1) * TB], bank[:],
                                       ACT.Sigmoid).then_inc(silu_ok, 1)
                    if n == 29:
                        act.wait_ge(c_in, 32 * i + 32)
                        keys(0)

                for u in range(NU):
                    if u + 1 < NU:
                        keys(u + 1)
                    act.wait_ge(y_ok, 8 * i + u + 2)
                    if u >= 2:
                        act.wait_ge(sqa_ok, 8 * i + u)
                    else:
                        act.wait_ge(sqa_ok, 8 * i + 1)
                    act.activation(sq[:, u % 2, :], OB[:], ACT.Square).then_inc(sq_ok, 1)
                    if u >= 4:
                        act.wait_ge(r_ok, 8 * i + 2 * (u // 2) - 1)
                    else:
                        act.wait_ge(r_ok, 8 * i + 1)
                    act.activation(yh[:, u % 4, :], y[:, u % 2, :], ACT.Copy).then_inc(yh_ok, 1)

            for b in range(2):
                ln["deviation"](act, b)
            for b in range(NTB):
                if b == 0:
                    act.wait_ge(w_in, 16)
                    act.activation(Wh[:, 0:WQ], Wraw[:, 0:WQ], ACT.Copy).then_inc(wh_ok, 1)
                ln["high"](act, b)
                if b + 2 < NTB:
                    ln["deviation"](act, b + 2)
            with act.Fori(0, NQ) as i:
                quad(i)
            act.wait_ge(init_ok, 4)
            act.wait_ge(ss_ok, 2)
            act.activation(std[:], KB[:, 0:NT], ACT.Sqrt, bias=epst[:], scale=1.0 / FEAT).then_inc(std_ok, 1)

        @block.vector
        def _(dve):
            ln["moments"](dve, 0)
            ln["moments"](dve, 1)
            ln["normalise"](dve, 0)
            for b in range(NTB):
                if b + 1 < NTB:
                    ln["normalise"](dve, b + 1)
                ln["low"](dve, b)
                if b + 2 < NTB:
                    ln["moments"](dve, b + 2)
            dve.wait_ge(zero_ok, 1)
            dve.wait_ge(init_ok, 4)

            def high(a, b):
                dve.tensor_copy(Wh[:, a:b], Wraw[:, a:b]).then_inc(wh_ok, 1)

            def quad(i, last):
                link = [0]
                dve.wait_ge(r_ok, 8 * i + 1)
                high(WQ, WTOT)

                def masks(u):
                    half, b, pr, col, ch = unit(u)
                    dve.wait_ge(sc_ok, 8 * i + u + 1)
                    if u >= 2:
                        dve.wait_ge(o_ok, 8 * i + u)
                    else:
                        dve.wait_ge(o_ok, 8 * i + 1)
                    for h in range(2):
                        d = C[:, CD + (2 * pr + h) * P:CD + (2 * pr + h + 1) * P]
                        dve.tensor_tensor(A[:, u % 2, h, :].rearrange("p (c t) -> p c t", c=GC),
                                          SC[u % 2][h][:].rearrange("p (c t) -> p c t", c=GC),
                                          d.unsqueeze(1).broadcast_to([P, GC, P]),
                                          ALU.mult).then_inc(mask_ok, 1)

                def states(u):
                    half, b, pr, col, ch = unit(u)
                    dve.wait_ge(u_ok, 8 * i + u + 2)
                    cs = range(4 * half, 4 * half + (4 if half == 0 else 3))
                    for c in cs:
                        if link[0] or c > 0:
                            dve.wait_ge(s_link, NLINK * i + link[0])
                        for h in range(2):
                            r = slice(h * LD, (h + 1) * LD)
                            U = UB[r, (c % 4) * P + h * LD:(c % 4) * P + (h + 1) * LD]
                            new = S[r, ch, c % 4, h * LD:(h + 1) * LD]
                            if c == 0:
                                ins = dve.tensor_copy(new, U)
                            else:
                                ins = dve.scalar_tensor_tensor(
                                    new, S[r, ch, (c - 1) % 4, h * LD:(h + 1) * LD],
                                    C[r, CB + pr:CB + pr + 1], U, ALU.mult, ALU.add)
                            ins.then_inc(s_link, 1)
                            link[0] += 1
                    dve.wait_ge(s_link, NLINK * i + link[0])
                    dve.sem_inc(s_ok, 1)

                def gated(u):
                    half, b, pr, col, ch = unit(u)
                    dve.wait_ge(o_ok, 8 * i + u + 2)
                    if u >= 2:
                        dve.wait_ge(yl_ok, 8 * i + u)
                    else:
                        dve.wait_ge(yl_ok, 8 * i + 1)
                    dve.scalar_tensor_tensor(y[:, u % 2, :], OB[:], NW[:, pr:pr + 1], g[:, pr, col:col + TB],
                                             ALU.mult, ALU.mult).then_inc(y_ok, 1)

                def sums(m):
                    half, b, _, col, _ = unit(2 * (m // 2))
                    t = col // P + 2 * (m % 2)
                    dve.wait_ge(r_ok, 8 * i + m + 2)
                    dve.wait_ge(acc_ok, 8 * i + m + 1)
                    dve.tensor_tensor(acc[:, t:t + 2, :], RB[:].rearrange("p (t n) -> p t n", t=2),
                                      acc[:, t:t + 2, :], ALU.add).then_inc(acc_ok, 1)

                def finish(rest=False):
                    xin = q[:].rearrange("p a n -> p (a n)").rearrange("p (t n) -> p t n", t=NT)
                    tail = token_tiles(1)[-2:]
                    if not rest:
                        dve.wait_ge(std_ok, 1)
                        dve.reciprocal(rstd[:], std[:]).then_inc(rstd_ok, 1)
                        dve.wait_ge(rstd_ok, 1)
                        dve.wait_ge(x_in, 16)
                    dve.wait_ge(acc_ok, 8 * NQ + (1 if rest else 0))
                    for t in tail if rest else [t for t in range(NT) if t not in tail]:
                        dve.scalar_tensor_tensor(X[:, t, :], acc[:, t, :], rstd[:, t:t + 1], xin[:, t, :],
                                                 ALU.mult, ALU.add)

                dve.wait_ge(c_in, 32 * i + 32)
                masks(0)
                for u in range(NU):
                    states(u)
                    if u + 1 < NU:
                        masks(u + 1)
                    gated(u)
                    if u == 2 and not last:
                        dve.wait_ge(w_in, 16 * i + 32)
                        high(0, WQ)
                    if u >= 2:
                        sums(u - 2)
                sums(NU - 2)
                if last:
                    finish()
                sums(NU - 1)
                if last:
                    finish(True)
                assert link[0] == NLINK

            with dve.Fori(0, NQ - 1) as i:
                quad(i, False)
            quad(NQ - 1, True)

        @block.tensor
        def _(pe):
            def products(out, pairs, first, last, check):
                m = None
                for n, (a, b) in enumerate(pairs):
                    m = pe.matmul(out, a, b, start=first and n == 0, stop=last and n == len(pairs) - 1,
                                  skip_group_check=check)
                return m

            def projection(i, n):
                if n == 0:
                    pe.wait_ge(w_ok, i + 1)
                if n < 4:
                    pe.wait_ge(mask_ok, 16 * i + 1)
                else:
                    pe.wait_ge(silu_ok, 32 * i + (n - 3 if n < 28 else n - 1))
                wv = [w[:, 0:WQ].rearrange("p (k n) -> p k n", k=KT) for w in (Wh, Wl)]
                bank = PR[BANK[n]]
                if n < 16 or n >= 24:
                    off = (OFF_Q if n < 8 else OFF_K if n < 16 else OFF_G) + P * (n // 4 % 2)
                    tb = n % 4
                    pairs = []
                    for kt in range(KT):
                        hi, lo = (h[:, kt, tb * TB:(tb + 1) * TB] for h in (hTh, hTl))
                        a, c = (w[:, kt, off:off + P] for w in wv)
                        pairs += [(a, hi), (a, lo), (c, hi)]
                    m = products(bank[:], pairs, True, True, False)
                else:
                    for j in range(2):
                        t = 2 * (n - 16) + j
                        pairs = []
                        for kt in range(KT):
                            hi, lo = (h[:, kt, t * P:(t + 1) * P] for h in (hTh, hTl))
                            a, c = (w[:, kt, OFF_V:OFF_V + 4 * LD] for w in wv)
                            pairs += [(hi, a), (hi, c), (lo, a)]
                        m = products(bank[:, j * HID:(j + 1) * HID], pairs, True, True, False)
                m.then_inc(proj_ok, 1)

            def quad(i, last):
                def scores(u):
                    half, b, pr, col, ch = unit(u)
                    if u < 2:
                        pe.wait_ge(silu_ok, 32 * i + (28 if u == 0 else 32))
                    else:
                        pe.wait_ge(mask_ok, 16 * i + 2 * u - 1)
                    for c in range(GC):
                        cc = slice(col + c * P, col + (c + 1) * P)
                        for h in range(2):
                            r = slice(h * LD, (h + 1) * LD)
                            m = pe.matmul(SC[u % 2][h][:, c * P:(c + 1) * P], k[r, pr, cc], q[r, pr, cc],
                                          start=True, stop=True)
                    m.then_inc(sc_ok, 1)
                    pe.wait_ge(kd_ok, 16 * i + 2 * u + 1)
                    for c in range(GC):
                        m = pe.transpose(KB[:, c * P:(c + 1) * P], k[:, pr, col + c * P:col + (c + 1) * P],
                                         ident[:])
                    m.then_inc(kb_ok, 1)

                def state_sums(u):
                    half, b, pr, col, ch = unit(u)
                    pe.wait_ge(kd_ok, 16 * i + 2 * u + 3)
                    pe.wait_ge(s_ok, 8 * i + u + 1)
                    for c in range(GC):
                        t = col // P + c
                        m = pe.matmul(UB[:, c * P:(c + 1) * P], kd[:, u % 2, c * P:(c + 1) * P],
                                      v[:, t, pr * P:(pr + 1) * P], start=True, stop=True)
                    m.then_inc(u_ok, 1)

                def outputs(u):
                    half, b, pr, col, ch = unit(u)
                    pe.wait_ge(s_ok, 8 * i + u + 2)
                    pe.wait_ge(qd_ok, 8 * i + u + 1)
                    pe.wait_ge(mask_ok, 16 * i + 2 * u + 3)
                    pe.wait_ge(sq_ok, 8 * i + u + 1)
                    c0 = 1 if half == 0 else 0
                    for c in range(c0, GC):
                        pe.matmul(OB[:, c * P:(c + 1) * P], S[:, ch, (4 * half + c - 1) % 4, :],
                                  qd[:, u % 2, c * P:(c + 1) * P], start=c == c0, stop=False,
                                  skip_group_check=True)
                    for c in range(GC):
                        t = col // P + c
                        for h in range(2):
                            r = slice(h * LD, (h + 1) * LD)
                            m = pe.matmul(OB[r, c * P:(c + 1) * P], v[:, t, pr * P + h * LD:pr * P + (h + 1) * LD],
                                          A[:, u % 2, h, c * P:(c + 1) * P], start=False, stop=c == GC - 1,
                                          skip_group_check=True)
                    m.then_inc(o_ok, 1)

                def squares(half):
                    pe.wait_ge(sqa_ok, 8 * i + 4 * half + 5)
                    pe.wait_ge(init_ok, 4)
                    for t in token_tiles(half):
                        m = pe.matmul(KB[:, t:t + 1], sqacc[:, t * P:(t + 1) * P], ones[:], start=True, stop=True)
                    m.then_inc(ss_ok, 1)

                def out_projection(mm):
                    base = 2 * (mm // 2)
                    pe.wait_ge(yl_ok, 8 * i + base + 3)
                    pe.wait_ge(acc_ok, 8 * i + mm + 1)
                    if mm == 0:
                        pe.wait_ge(wo_ok, i + 1)
                    for j in range(2):
                        cols = slice((2 * (mm % 2) + j) * P, (2 * (mm % 2) + j + 1) * P)
                        pairs = []
                        for pr in range(2):
                            hi, lo = (z[:, (base + pr) % 4, cols] for z in (yh, yl))
                            a, c = (w[:, WQ + pr * HID:WQ + (pr + 1) * HID] for w in (Wh, Wl))
                            pairs += [(hi, a), (hi, c), (lo, a)]
                        m = products(RB[:, j * HID:(j + 1) * HID], pairs, True, True, False)
                    m.then_inc(r_ok, 1)

                scores(0)
                for n in range(28, 32):
                    projection(i, n)
                for u in range(NU):
                    state_sums(u)
                    if u + 1 < NU:
                        scores(u + 1)
                    else:
                        out_projection(u - 2)
                        if not last:
                            projection(i + 1, 0)
                    outputs(u)
                    if 2 <= u < NU - 1:
                        out_projection(u - 2)
                if last:
                    squares(0)
                for n in range(1, 28):
                    if not last:
                        projection(i + 1, n)
                    if n == 2:
                        out_projection(NU - 2)
                    if n == 2 and last:
                        squares(1)
                    if n == 3:
                        out_projection(NU - 1)

            for n in range(28):
                if n < NTB:
                    if n == 0:
                        ln["turn"](pe, 0)
                    if n + 1 < NTB:
                        ln["turn"](pe, n + 1)
                    ln["ready"](pe, n)
                projection(0, n)
            with pe.Fori(0, NQ - 1) as i:
                quad(i, False)
            quad(NQ - 1, True)


def ffn(nc, ctx, name, X, ident, hTh, hTl, WF, SCL, DS, out=None, weights=None):
    with ExitStack() as mem:
        sb = lambda n, s, d: mem.enter_context(nc.sbuf_tensor(name + n, s, d))
        sem = lambda n: ctx.enter_context(nc.semaphore(name + n))
        pb = lambda n: mem.enter_context(nc.psum_tensor(name + n, [P, TB], F32))
        sg = sb("sg", [P, 2, TB], F32)
        f = sb("f", [P, 2, TB], F32)
        fh = sb("fh", [P, 2, NI, TB], F32R)
        fl = sb("fl", [P, 2, NI, TB], F32R)
        o = sb("o", [P, 2, 2, HID], F32)
        GB, UB, DB = [pb("G0"), pb("G1")], [pb("U0"), pb("U1")], [pb("D0"), pb("D1")]
        g_ok, u_ok, sg_ok, f_ok, fh_ok, fl_ok = sem("g_ok"), sem("u_ok"), sem("sg_ok"), sem("f_ok"), sem("fh_ok"), sem("fl_ok")
        d_ok, o_ok, x_ok, st_ok = sem("d_ok"), sem("o_ok"), sem("x_ok"), sem("st_ok")
        ln = norm_steps(nc, ctx, mem, name + "ln_", X, ident, hTh, hTl, [pb("T0"), pb("T1")])
        wg = WF[:, 0:KT * FI].rearrange("p (k n) -> p k n", k=KT)
        wu = WF[:, KT * FI:2 * KT * FI].rearrange("p (k n) -> p k n", k=KT)
        wd = WF[:, 2 * KT * FI:].rearrange("p (k n) -> p k n", k=NI)
        block = mem.enter_context(nc.Block())

        @block.tensor
        def _(pe):
            def up(tb):
                for it in range(NI):
                    n = tb * NI + it
                    if n >= 2:
                        pe.wait_ge(sg_ok, n - 1)
                        pe.wait_ge(f_ok, n - 1)
                    for w, bank, done in ((wg, GB[n % 2], g_ok), (wu, UB[n % 2], u_ok)):
                        if weights is not None and n == 0:
                            pe.wait_ge(weights["q_ok"], 2 if done is g_ok else 4)
                        for kt in range(KT):
                            a = w[:, kt, it * P:(it + 1) * P]
                            pe.matmul(bank[:], a, hTh[:, kt, tb * TB:(tb + 1) * TB], start=kt == 0, stop=False)
                            m = pe.matmul(bank[:], a, hTl[:, kt, tb * TB:(tb + 1) * TB], start=False,
                                          stop=kt == KT - 1)
                        m.then_inc(done, 1)

            def down(tb):
                pe.wait_ge(fl_ok, (tb + 1) * NI)
                if weights is not None and tb == 0:
                    pe.wait_ge(weights["q_ok"], 6)
                for half in range(2):
                    n = 2 * tb + half
                    if n >= 2:
                        pe.wait_ge(o_ok, n - 1)
                    for j in range(2):
                        c = slice((2 * half + j) * P, (2 * half + j + 1) * P)
                        for it in range(NI):
                            pe.matmul(DB[n % 2][:, j * HID:(j + 1) * HID], fh[:, tb % 2, it, c], wd[:, it, :],
                                      start=it == 0, stop=False)
                            m = pe.matmul(DB[n % 2][:, j * HID:(j + 1) * HID], fl[:, tb % 2, it, c],
                                          wd[:, it, :], start=False, stop=it == NI - 1)
                    m.then_inc(d_ok, 1)

            ln["turn"](pe, 0)
            ln["turn"](pe, 1)
            ln["ready"](pe, 0)
            up(0)
            ln["turn"](pe, 2)
            for tb in range(NTB):
                if tb + 1 < NTB:
                    ln["ready"](pe, tb + 1)
                    up(tb + 1)
                if tb + 3 < NTB:
                    ln["turn"](pe, tb + 3)
                down(tb)

        @block.scalar
        def _(act):
            def high(n):
                tb, it = n // NI, n % NI
                act.wait_ge(f_ok, n + 1)
                if tb >= 2:
                    act.wait_ge(d_ok, 2 * (tb - 1))
                act.activation(fh[:, tb % 2, it, :], f[:, n % 2, :], ACT.Copy).then_inc(fh_ok, 1)

            for b in range(2):
                ln["deviation"](act, b)
            for b in range(2):
                ln["high"](act, b)
                ln["deviation"](act, b + 2)
            if weights is not None:
                act.wait_ge(weights["s_in"], 32)
                weights["rounding"](act, 0)
                for c in range(4):
                    if c + 1 < 4:
                        weights["rounding"](act, c + 1)
                    weights["overflow"](act, c)
            for n in range(NTB * NI):
                tb, it = n // NI, n % NI
                act.wait_ge(g_ok, n + 1)
                if n >= 2:
                    act.wait_ge(f_ok, n - 1)
                act.activation(sg[:, n % 2, :], GB[n % 2][:], ACT.Silu,
                               scale=SCL[:, n % NI:n % NI + 1]).then_inc(sg_ok, 1)
                if n >= 1:
                    high(n - 1)
                if weights is not None and n in (0, 1):
                    weights["rounding"](act, 4 + n)
                if weights is not None and n in (4, 5):
                    weights["overflow"](act, n)
                if it == NI - 1 and tb + 2 < NTB:
                    ln["high"](act, tb + 2)
            high(NTB * NI - 1)

        @block.vector
        def _(dve):
            def scaled(n):
                dve.wait_ge(d_ok, n + 1)
                if n >= 2:
                    dve.wait_ge(x_ok, n - 1)
                dve.tensor_tensor(o[:, n % 2, :, :], DB[n % 2][:].rearrange("p (t n) -> p t n", t=2),
                                  DS[:].unsqueeze(1).broadcast_to([P, 2, HID]), ALU.mult).then_inc(o_ok, 1)

            for b in range(2):
                ln["moments"](dve, b)
            for b in range(2):
                ln["normalise"](dve, b)
            for b in range(2):
                ln["low"](dve, b)
                ln["moments"](dve, b + 2)
            if weights is not None:
                for c in range(4):
                    weights["clamped"](dve, c)
                for c in range(4):
                    weights["rounded"](dve, c)
                    if c >= 1:
                        weights["checked"](dve, c - 1)
                weights["checked"](dve, 3)
                dve.wait_ge(weights["s_in"], 32)
            for n in range(NTB * NI):
                tb, it = n // NI, n % NI
                dve.wait_ge(sg_ok, n + 1)
                dve.wait_ge(u_ok, n + 1)
                if n >= 2:
                    dve.wait_ge(fl_ok, n - 1)
                dve.scalar_tensor_tensor(f[:, n % 2, :], UB[n % 2][:], SCL[:, NI + it:NI + it + 1],
                                         sg[:, n % 2, :], ALU.mult, ALU.mult).then_inc(f_ok, 1)
                if weights is not None and n in (0, 1):
                    weights["clamped"](dve, 4 + n)
                if weights is not None and n in (3, 4):
                    weights["rounded"](dve, 1 + n)
                if weights is not None and n in (6, 7):
                    weights["checked"](dve, n - 2)
                if it == 2 and tb + 2 < NTB:
                    ln["normalise"](dve, tb + 2)
                if it == NI - 1 and tb + 2 < NTB:
                    ln["low"](dve, tb + 2)
                if tb >= 1 and it == NI - 1:
                    scaled(2 * (tb - 1))
                    scaled(2 * (tb - 1) + 1)
            scaled(2 * NTB - 2)
            scaled(2 * NTB - 1)

        @block.gpsimd
        def _(pool):
            def add(n):
                pool.wait_ge(o_ok, n + 1)
                pool.tensor_tensor(X[:, 2 * n:2 * n + 2, :], X[:, 2 * n:2 * n + 2, :], o[:, n % 2, :, :],
                                   ALU.add).then_inc(x_ok, 1)

            if weights is not None:
                for c in range(4):
                    weights["beyond"](pool, c)
            for n in range(NTB * NI):
                tb, it = n // NI, n % NI
                pool.wait_ge(fh_ok, n + 1)
                if tb >= 2:
                    pool.wait_ge(d_ok, 2 * (tb - 1))
                pool.tensor_tensor(fl[:, tb % 2, it, :], f[:, n % 2, :], fh[:, tb % 2, it, :].bitcast(F32),
                                   ALU.subtract).then_inc(fl_ok, 1)
                if weights is not None and n in (1, 2):
                    weights["beyond"](pool, 3 + n)
                if tb >= 1 and it == NI - 1:
                    add(2 * (tb - 1))
                    add(2 * (tb - 1) + 1)
            add(2 * NTB - 2)
            add(2 * NTB - 1)

        if weights is not None:
            @block.sync
            def _(sp):
                weights["sync"](sp)

        if out is not None:
            @block.sync
            def _(sp):
                for n in range(2 * NTB):
                    sp.wait_ge(x_ok, n + 1)
                    sp.dma_start(out[:, 2 * n:2 * n + 2, :], X[:, 2 * n:2 * n + 2, :]).then_inc(st_ok, 16)
                sp.wait_ge(st_ok, 16 * 2 * NTB)


def quantised_weights(nc, ctx, mem, w_ffn, s_ffn, d_ffn, WF, SCL, DS):
    sb = lambda n, s, d: mem.enter_context(nc.sbuf_tensor("qw_" + n, s, d))
    sem = lambda n: ctx.enter_context(nc.semaphore("qw_" + n))
    CN = KT * FI // 2
    assert 2 * CN == NI * HID
    N = 6 * CN
    w = sb("w", [P, N], F32)
    k = sb("k", [P, N], F32)
    e = sb("e", [P, N], FP8)
    h = sb("h", [P, N], FP8)
    hc = sb("hc", [P, N], FP8)
    d = sb("d", [P, 2, CN], F32)
    w_in = [sem(f"w_in{c}") for c in range(6)]
    s_in, k_ok, e_ok, h_ok, hc_ok, d_ok, r_ok, z_ok, q_ok = (sem(n) for n in
        ("s_in", "k_ok", "e_ok", "h_ok", "hc_ok", "d_ok", "r_ok", "z_ok", "q_ok"))
    at = lambda c: slice(c * CN, (c + 1) * CN)

    def sync(sp):
        sp.dma_start(SCL[:], s_ffn).then_inc(s_in, 16)
        sp.dma_start(DS[:], d_ffn).then_inc(s_in, 16)
        for c in range(6):
            sp.dma_start(w[:, at(c)], w_ffn[:, at(c)]).then_inc(w_in[c], 16)

    def overflow(act, c):
        act.wait_ge(r_ok, c + 1)
        act.activation(k[:, at(c)], w[:, at(c)], ACT.Copy, scale=7.4e35).then_inc(z_ok, 1)

    def rounding(act, c):
        act.wait_ge(w_in[c], 16)
        act.activation(h[:, at(c)], w[:, at(c)], ACT.Copy, scale=0.5, saturate=False).then_inc(h_ok, 1)
        act.wait_ge(k_ok, c + 1)
        act.activation(hc[:, at(c)], k[:, at(c)], ACT.Copy, scale=0.5, saturate=False).then_inc(hc_ok, 1)
        act.activation(e[:, at(c)], k[:, at(c)], ACT.Copy, saturate=False).then_inc(e_ok, 1)

    def beyond(pool, c):
        pool.wait_ge(hc_ok, c + 1)
        pool.wait_ge(h_ok, c + 1)
        if c >= 2:
            pool.wait_ge(r_ok, c - 1)
        pool.tensor_tensor(d[:, c % 2, :], h[:, at(c)], hc[:, at(c)], ALU.subtract).then_inc(d_ok, 1)

    def clamped(dve, c):
        dve.wait_ge(w_in[c], 16)
        dve.tensor_scalar(k[:, at(c)], w[:, at(c)], 128.0, -128.0, ALU.min, ALU.max).then_inc(k_ok, 1)

    def rounded(dve, c):
        dve.wait_ge(d_ok, c + 1)
        dve.wait_ge(e_ok, c + 1)
        dve.wait_ge(k_ok, c + 1)
        dve.scalar_tensor_tensor(w[:, at(c)], d[:, c % 2, :], 2.0, e[:, at(c)], ALU.mult, ALU.add).then_inc(r_ok, 1)

    def checked(dve, c):
        dve.wait_ge(z_ok, c + 1)
        dve.wait_ge(r_ok, c + 1)
        dve.scalar_tensor_tensor(WF[:, at(c)], k[:, at(c)], 0.0, w[:, at(c)], ALU.mult, ALU.add).then_inc(q_ok, 1)

    return {"sync": sync, "rounding": rounding, "overflow": overflow, "beyond": beyond, "clamped": clamped,
            "rounded": rounded, "checked": checked, "q_ok": q_ok, "s_in": s_in}


Q_RUNS = ((0, 3), (0, 2), (0, 1))
K_RUNS = ((0, 2), (0, 2), (0, 1), (2, 1))
ND = len(Q_RUNS) + len(K_RUNS)


def gather_stacks(sp, g, QS, KS, q_parts, k_parts, loaded):
    hg, b = g // 2, g % 2
    for dst, src, runs in ((QS, q_parts, Q_RUNS), (KS, k_parts, K_RUNS)):
        row = 0
        for p0, parts in runs:
            sp.dma_start(dst[row:row + SD * parts, :, :].rearrange("r j t -> r (j t)"),
                         src[b, p0:p0 + parts, :, 2 * hg:2 * hg + 2].rearrange("r d i m t -> (r d) (i m t)")
                         ).then_inc(loaded, 16)
            row += SD * parts


def rotary_projections(nc, ctx, X, ident, hTh, hTl, w_att, rope, q_parts, k_parts, V, WOh, WOl, stacks0, s_in0):
    with ExitStack() as mem:
        sb = lambda n, s, d: mem.enter_context(nc.sbuf_tensor("rp_" + n, s, d))
        sem = lambda n: ctx.enter_context(nc.semaphore("rp_" + n))
        pb = lambda n: mem.enter_context(nc.psum_tensor("rp_" + n, [P, TB], F32))
        NQK = KT * 2 * HID
        NV = 2 * NQK
        NO = NV + KT * HID
        Wh = sb("Wh", [P, NO], F32R)
        Wl = sb("Wl", [P, NO], F32R)
        CS = sb("CS", [P, 2, SEQ], F32)
        QP = sb("QP", [P, NPART, BATCH, 2, SEQ], BF16)
        KP = sb("KP", [P, NPART, BATCH, 2, SEQ], BF16)
        Wraw = KP[:].rearrange("p a b m t -> p (a b m t)").bitcast(F32)[:, 0:NO + KT * HID]
        H = stacks0[:].rearrange("p a j t -> p (a j t)").bitcast(F32).rearrange("p (t n) -> p t n", t=NT)
        RS = 3
        t1 = sb("t1", [P, RS, TB], F32)
        t2 = sb("t2", [P, 2, TB], F32)
        QB, SB_, VB = [pb("Q0"), pb("Q1")], [pb("S0"), pb("S1")], [pb("V0"), pb("V1")]
        ln = norm_steps(nc, ctx, mem, "ln3_", X, ident, hTh, hTl, [pb("T0"), pb("T1")], H=H)
        w_in, r_in, h_ok, l_ok = [sem(f"w_in{c}") for c in range(3)], sem("r_in"), sem("h_ok"), sem("l_ok")
        v0_ok = sem("v0_ok")
        pieces = ((0, NQK), (NQK, NV), (NV, NO), (NO, NO + KT * HID))

        def high(act, c):
            a, b = pieces[c]
            act.wait_ge(w_in[min(c, 2)], 16)
            act.activation(Wh[:, a:b] if c < 3 else WOh[:], Wraw[:, a:b], ACT.Copy).then_inc(h_ok, 1)

        def low(pool, c):
            a, b = pieces[c]
            pool.wait_ge(h_ok, c + 1)
            pool.tensor_tensor(Wl[:, a:b] if c < 3 else WOl[:], Wraw[:, a:b],
                               (Wh[:, a:b] if c < 3 else WOh[:]).bitcast(F32), ALU.subtract).then_inc(l_ok, 1)

        p_ok, m_ok, a_ok, p1_ok, r1_ok, p2_ok, p3_ok, out_ok = (sem(n) for n in
            ("p_ok", "m_ok", "a_ok", "p1_ok", "r1_ok", "p2_ok", "p3_ok", "out_ok"))
        vb_ok, ve_ok = sem("vb_ok"), sem("ve_ok")
        part = lambda dst, p, mt, tb: dst[:, p, tb // 2, mt, (tb % 2) * TB:(tb % 2 + 1) * TB]
        steps = [(dst, x, mt, 2 * b + t) for b in range(BATCH) for x, dst in ((0, QP), (2, KP))
                 for mt in range(2) for t in range(2)]
        NS = len(steps)
        def col(w, kt, x, mt):
            at = (x // 2) * NQK + (2 * kt + x % 2) * HID + mt * P
            return w[:, at:at + P]

        block = mem.enter_context(nc.Block())

        @block.sync
        def _(sp):
            for c, (a, b) in enumerate(((0, NQK), (NQK, NV), (NV, NO + KT * HID))):
                sp.dma_start(Wraw[:, a:b], w_att[:, a:b]).then_inc(w_in[c], 16)
                if c == 0:
                    sp.dma_start(CS[:], rope).then_inc(r_in, 16)
            for n in range(1, NS, 2):
                dst, x, mt, tb = steps[n]
                if n == NS // 2 + 1:
                    sp.wait_ge(out_ok, 16 * NS // 4)
                    gather_stacks(sp, 0, stacks0[:, 0], stacks0[:, 1], q_parts, k_parts, s_in0)
                sp.wait_ge(p3_ok, n + 1)
                b = tb // 2
                sp.dma_start((q_parts, k_parts)[x // 2][b, :, :, :, mt].rearrange("r d i t -> (d i) r t"),
                             dst[:, :, b, mt]).then_inc(out_ok, 16)
            sp.wait_ge(out_ok, 16 * NS // 2)
            sp.wait_ge(s_in0, 16 * ND)

        @block.tensor
        def _(pe):
            ln["turn"](pe, 0)
            ln["turn"](pe, 1)
            pe.wait_ge(l_ok, 1)
            for n, (dst, x, mt, tb) in enumerate(steps):
                if n == 4:
                    pe.wait_ge(l_ok, 2)
                ln["ready"](pe, tb)
                if n >= 2:
                    pe.wait_ge(m_ok, 2 * (n - 1))
                for s, bank in ((x, QB[n % 2]), (x + 1, SB_[n % 2])):
                    for kt in range(KT):
                        hi, lo = (h[:, kt, tb * TB:(tb + 1) * TB] for h in (hTh, hTl))
                        a, c = col(Wh, kt, s, mt), col(Wl, kt, s, mt)
                        pe.matmul(bank[:], a, hi, start=kt == 0, stop=False)
                        pe.matmul(bank[:], a, lo, start=False, stop=False)
                        m = pe.matmul(bank[:], c, hi, start=False, stop=kt == KT - 1)
                m.then_inc(p_ok, 1)
                if n == 1:
                    ln["turn"](pe, 2)
                if n == 4:
                    ln["turn"](pe, 3)
            pe.wait_ge(l_ok, 3)
            for n in range(NT // 2):
                if n >= 2:
                    pe.wait_ge(ve_ok, n - 1)
                for j in range(2):
                    t = 2 * n + j
                    for kt in range(KT):
                        hi, lo = (h[:, kt, t * P:(t + 1) * P] for h in (hTh, hTl))
                        a, c = (w[:, NV + kt * HID:NV + (kt + 1) * HID] for w in (Wh, Wl))
                        o = VB[n % 2][:, j * HID:(j + 1) * HID]
                        pe.matmul(o, hi, a, start=kt == 0, stop=False)
                        pe.matmul(o, hi, c, start=False, stop=False)
                        m = pe.matmul(o, lo, a, start=False, stop=kt == KT - 1)
                m.then_inc(vb_ok, 1)

        @block.vector
        def _(dve):
            ln["moments"](dve, 0)
            ln["moments"](dve, 1)
            ln["normalise"](dve, 0)
            ln["normalise"](dve, 1)
            for b in range(2):
                ln["low"](dve, b)
                ln["moments"](dve, b + 2)
            dve.wait_ge(r_in, 16)
            for n in range(NS + 2):
                if n < NS:
                    dst, x, mt, tb = steps[n]
                    dve.wait_ge(p_ok, n + 1)
                    if n >= RS:
                        dve.wait_ge(p3_ok, n - RS + 1)
                    c = (tb % 2) * TB
                    dve.tensor_tensor(t1[:, n % RS, :], QB[n % 2][:], CS[:, 0, c:c + TB], ALU.mult).then_inc(m_ok, 1)
                    if n >= 2:
                        dve.wait_ge(a_ok, n - 1)
                    dve.tensor_tensor(t2[:, n % 2, :], SB_[n % 2][:], CS[:, 1, c:c + TB], ALU.mult).then_inc(m_ok, 1)
                if 1 <= n <= NS:
                    dst, x, mt, tb = steps[n - 1]
                    dve.wait_ge(p1_ok, n)
                    t = t1[:, (n - 1) % RS, :]
                    dve.tensor_tensor(t, t, part(dst, 0, mt, tb), ALU.subtract).then_inc(r1_ok, 1)
                if n >= 2:
                    dst, x, mt, tb = steps[n - 2]
                    dve.wait_ge(p2_ok, n - 1)
                    dve.tensor_tensor(part(dst, 2, mt, tb), t1[:, (n - 2) % RS, :], part(dst, 1, mt, tb),
                                      ALU.subtract).then_inc(p3_ok, 1)
                if n in (0, 2):
                    ln["normalise"](dve, 2 + n // 2)
                if n in (3, 6):
                    ln["low"](dve, 1 + n // 3)

        @block.scalar
        def _(act):
            ln["deviation"](act, 0)
            ln["deviation"](act, 1)
            high(act, 0)
            for b in range(2):
                ln["high"](act, b)
                ln["deviation"](act, b + 2)
            for c in range(1, 4):
                high(act, c)
            for n in range(NS + 1):
                if n == 4:
                    act.wait_ge(l_ok, 4)
                if n < NS:
                    dst, x, mt, tb = steps[n]
                    act.wait_ge(a_ok, n + 1)
                    act.activation(part(dst, 0, mt, tb), t1[:, n % RS, :],
                                   ACT.Copy).then_inc(p1_ok, 1)
                if n >= 1:
                    dst, x, mt, tb = steps[n - 1]
                    act.wait_ge(r1_ok, n)
                    act.activation(part(dst, 1, mt, tb), t1[:, (n - 1) % RS, :],
                                   ACT.Copy).then_inc(p2_ok, 1)
                if n in (2, 5):
                    ln["high"](act, 2 + n // 3)
            act.wait_ge(v0_ok, 5)
            for n in range(NT // 2):
                act.wait_ge(vb_ok, n + 1)
                act.activation(V[:, 2 * n:2 * n + 2, :, 0:SD],
                               VB[n % 2][:].rearrange("p (t h d) -> p t h d", t=2, h=SH),
                               ACT.Copy).then_inc(ve_ok, 1)

        @block.gpsimd
        def _(pool):
            low(pool, 0)
            for n in range(NS):
                pool.wait_ge(m_ok, 2 * n + 2)
                pool.tensor_tensor(t1[:, n % RS, :], t1[:, n % RS, :], t2[:, n % 2, :], ALU.add).then_inc(a_ok, 1)
                if n < 3:
                    low(pool, n + 1)
                if 8 <= n < 12:
                    pool.memset(V[:, 4 * (n - 8):4 * (n - 7), :, SD + 1:32], 0.0).then_inc(v0_ok, 1)
                if n == 12:
                    pool.memset(V[:, :, :, SD:SD + 1], 1.0).then_inc(v0_ok, 1)


def causal_attention(nc, ctx, ident, masks_in, q_parts, k_parts, V, ATT, stacks0, s_in0):
    with ExitStack() as mem:
        sb = lambda n, s, d: mem.enter_context(nc.sbuf_tensor("ca_" + n, s, d))
        sem = lambda n: ctx.enter_context(nc.semaphore("ca_" + n))
        NG2 = BATCH * NG
        NSL = 3
        QS = [stacks0[:, 0]] + [sb(f"QS{i}", [P, HG, SEQ], BF16) for i in range(1, NSL)]
        KS = [stacks0[:, 1]] + [sb(f"KS{i}", [P, HG, SEQ], BF16) for i in range(1, NSL)]
        VG = [sb(f"VG{i}", [P, SEQ // P, HG, 32], F32) for i in range(2)]
        MK = sb("MK", [P, 3, P], BF16)
        MKf = sb("MKf", [P, 3, P], F32)
        PT = sb("PT", [P, 2, HG, TB], F32)
        mx = sb("mx", [P, 2, HG, 8, 2], F32)
        m = sb("m", [P, 2, 2, 8], F32)
        mr = sb("mr", [P, 2, 2, 8], F32)
        NM = sb("NM", [P, HG, 8, MROWS], BF16)
        OT = sb("OT", [P, 2, TB], F32)
        rec = sb("rec", [P, 4, HG], F32)
        pb = lambda n, w=TB: mem.enter_context(nc.psum_tensor("ca_" + n, [P, w], F32))
        S1 = [pb("S10"), pb("S11")]
        ST = [pb("ST0", 2 * TB), pb("ST1", 2 * TB)]
        OB, AUX = pb("OB"), pb("AUX")
        AUXB = AUX[:].bitcast(BF16)
        mk_in, mk_ok, init_ok, one_ok = sem("mk_in"), sem("mk_ok"), sem("init_ok"), sem("one_ok")
        s_in = [s_in0] + [sem(f"s_in{i}") for i in range(1, NSL)]
        v_in = [sem(f"v_in{i}") for i in range(2)]
        m_ok, s1_ok, mx_ok, ch_ok, nm_ok, mt_ok, mtc_ok = (sem(n) for n in ("m_ok", "s1_ok", "mx_ok", "ch_ok", "nm_ok", "mt_ok", "mtc_ok"))
        st_ok, exp_ok, pv_ok, oc_ok, t_ok, rec_ok, nrm_ok = (sem(n) for n in
            ("st_ok", "exp_ok", "pv_ok", "oc_ok", "t_ok", "rec_ok", "nrm_ok"))
        SEGS = [s for long, short in zip(((3, 0), (4, 0), (5, 0), (6, 0), (7, 0), (7, 1)),
                                         ((0, 0), (4, 1), (1, 0), (5, 1), (2, 0), (6, 1))) for s in (long, short)]
        segs = [(j, qt, s) for j in range(HG) for qt, s in SEGS]
        NSEG = len(segs)
        blocks = [(qb, kt) for qb in range(2) for kt in range(4 * qb + 4)]
        NM2 = len(blocks)
        NST = 2 * NM2
        BANKS = S1 + [t[:, h * TB:(h + 1) * TB] for t in ST for h in range(2)]
        LEAD = 10
        N_T1, N_T0 = 4, 13
        N_MX = {9: 0, 11: 1, 21: 2, 23: 3}

        def span(qb, kt):
            q0 = max(qb * TB, kt * P)
            return q0, (qb + 1) * TB - q0

        share = [1 if span(*blocks[n // 2])[1] == P else 2 for n in range(NST)]
        long_steps = [n for n in range(NST) if span(*blocks[n // 2])[1] == TB]
        for n in long_steps[1::3]:
            share[n] += 1
        assert sum(share) == NSEG

        def segments(g, n):
            a = NSEG + LEAD + g * NSEG + sum(share[:n])
            return [(x // NSEG, x % NSEG) for x in range(a, a + share[n]) if x < NSEG * NG2]

        ahead = [(x // NSEG, x % NSEG) for x in range(NSEG + LEAD)]
        AUX_USES = [("mx", 0, j) for j in range(HG)]
        for g in range(NG2):
            for n in range(NST):
                if n == N_T1 and g >= 1:
                    AUX_USES.append(("out", g - 1, 1))
                if n == N_T0:
                    AUX_USES.append(("out", g, 0))
                if n in N_MX and g + 1 < NG2:
                    AUX_USES.append(("mx", g + 1, N_MX[n]))
        AUX_USES.append(("out", NG2 - 1, 1))

        def pass1_bank(at):
            if at < len(ahead):
                return BANKS[at % len(BANKS)], len(BANKS)
            return S1[at % 2], 1 if at < len(ahead) + 2 else 2

        block = mem.enter_context(nc.Block())

        @block.sync
        def _(sp):
            def load(g):
                gather_stacks(sp, g, QS[g % NSL], KS[g % NSL], q_parts, k_parts, s_in[g % NSL])

            def values(g):
                if g >= 2:
                    sp.wait_ge(pv_ok, NM2 * (g - 1))
                sp.dma_start(VG[g % 2][:], V[:, 8 * (g % 2):8 * (g % 2) + 8, HG * (g // 2):HG * (g // 2) + HG, :]
                             ).then_inc(v_in[g % 2], 16)

            sp.dma_start(MKf[:], masks_in).then_inc(mk_in, 16)
            load(1)
            values(0)
            load(2)
            values(1)
            for g in range(3, NG2):
                sp.wait_ge(st_ok, NST * (g - 2))
                load(g)
                values(g - 1)
            values(NG2 - 1)

        @block.gpsimd
        def _(pool):
            for b in range(NSL):
                if b:
                    pool.wait_ge(one_ok, b)
                pool.memset(KS[b][SROWS:KROWS, :, :], 1.0).then_inc(one_ok, 1)

            def parts(g, i):
                n = 4 * (2 * g + i)
                j = slice(2 * i, 2 * i + 2)
                pool.wait_ge(m_ok, 2 * g + i + 1)
                if g >= 1:
                    pool.wait_ge(mt_ok, HG * (g - 1) + 2 * i + 2)
                pool.tensor_scalar(NM[:, j, :, 0], m[:, i], -1.0, None, ALU.mult).then_inc(ch_ok, 1)
                pool.tensor_scalar(mr[:, 0, :, :], m[:, i], -1.0, None, ALU.mult).then_inc(ch_ok, 1)
                pool.wait_ge(ch_ok, n + 2)
                pool.tensor_tensor(mr[:, 1, :, :], mr[:, 0, :, :], NM[:, j, :, 0], ALU.subtract).then_inc(ch_ok, 1)
                pool.wait_ge(ch_ok, n + 3)
                pool.tensor_copy(NM[:, j, :, 1], mr[:, 1, :, :]).then_inc(ch_ok, 1)
                pool.wait_ge(ch_ok, n + 4)
                pool.tensor_tensor(NM[:, j, :, 2], mr[:, 1, :, :], NM[:, j, :, 1], ALU.subtract).then_inc(nm_ok, 1)

            pool.wait_ge(one_ok, NSL)
            for g in range(NG2):
                parts(g, 0)
                parts(g, 1)

        @block.tensor
        def _(pe):
            def aux_free(use):
                at = AUX_USES.index(use)
                if at:
                    kind = AUX_USES[at - 1][0]
                    count = sum(u[0] == kind for u in AUX_USES[:at])
                    pe.wait_ge(mtc_ok if kind == "mx" else nrm_ok, count)

            def pass1(g, s):
                j, qt, half = segs[s]
                at = NSEG * g + s
                if s == 0:
                    pe.wait_ge(s_in[g % NSL], 16 * ND * (g // NSL + 1))
                bank, behind = pass1_bank(at)
                if at >= behind:
                    pe.wait_ge(mx_ok, at - behind + 1)
                Q, K = QS[g % NSL], KS[g % NSL]
                k0, k1 = half * TB, min((half + 1) * TB, (qt + 1) * P)
                ins = pe.matmul(bank[:, 0:k1 - k0], Q[0:SROWS, j, qt * P:(qt + 1) * P], K[0:SROWS, j, k0:k1],
                                start=True, stop=True)
                if k1 == (qt + 1) * P:
                    ins = pe.matmul(bank[:, k1 - P - k0:k1 - k0], MK[:, 0, :], MK[:, 1, :], start=False, stop=True,
                                    skip_group_check=True)
                ins.then_inc(s1_ok, 1)

            def maxima(g, j):
                if j % 2 == 0:
                    pe.wait_ge(nm_ok, 2 * g + j // 2 + 1)
                aux_free(("mx", g, j))
                for qt in range(8):
                    ins = pe.transpose(AUXB[SROWS:KROWS, qt * P:(qt + 1) * P], NM[:, j, qt, :], MK[:, 0, :])
                ins.then_inc(mt_ok, 1)

            def pass2(g, n, h):
                qb, kt = blocks[n // 2]
                q0, w = span(qb, kt)
                if n < 2 and h == 0:
                    pe.wait_ge(mtc_ok, HG * g + 2 * n + 2)
                if h == 0 and NST * g + n >= 2:
                    pe.wait_ge(exp_ok, NST * g + n - 1)
                j = 2 * (n % 2) + h
                out = ST[n % 2][:, h * TB:h * TB + w]
                ins = pe.matmul(out, KS[g % NSL][0:KROWS, j, kt * P:(kt + 1) * P], QS[g % NSL][0:KROWS, j, q0:q0 + w],
                                start=True, stop=True)
                if kt >= 4 * qb:
                    ins = pe.matmul(out[:, 0:P], MK[:, 0, :], MK[:, 2, :], start=False, stop=True,
                                    skip_group_check=True)
                if h == 1:
                    ins.then_inc(st_ok, 1)

            def values(g, mm):
                qb, kt = blocks[mm]
                q0, w = span(qb, kt)
                pe.wait_ge(exp_ok, NST * g + 2 * mm + 2)
                if mm == 0:
                    pe.wait_ge(v_in[g % 2], 16 * (g // 2 + 1))
                if kt == 0 and 2 * g + qb >= 1:
                    pe.wait_ge(oc_ok, 2 * g + qb)
                for j in range(HG):
                    ins = pe.matmul(OB[32 * j:32 * j + 32, q0 - qb * TB:q0 - qb * TB + w], VG[g % 2][:, kt, j, :],
                                    PT[:, mm % 2, j, 0:w], start=kt == 0, stop=kt == 4 * qb + 3,
                                    skip_group_check=True)
                ins.then_inc(pv_ok, 1)

            def back(g, qb):
                pe.wait_ge(oc_ok, 2 * g + qb + 1)
                aux_free(("out", g, qb))
                for t in range(4):
                    ins = pe.transpose(AUX[:, t * P:(t + 1) * P], OT[:, qb, t * P:(t + 1) * P], ident[:])
                ins.then_inc(t_ok, 1)

            pe.wait_ge(mk_ok, 1)
            for g, s in ahead:
                pass1(g, s)
            for j in range(HG):
                maxima(0, j)
            pe.wait_ge(mx_ok, len(ahead))
            pe.wait_ge(one_ok, NSL)
            for g in range(NG2):
                for n in range(NST):
                    todo = segments(g, n)
                    for h in range(2):
                        pass2(g, n, h)
                        for gs, s in todo[h:h + 1]:
                            pass1(gs, s)
                    if n == 1 and g >= 1:
                        values(g - 1, NM2 - 1)
                    if n % 2 == 1 and n >= 3:
                        values(g, (n - 3) // 2)
                    for gs, s in todo[2:]:
                        pass1(gs, s)
                    if n == N_T1 and g >= 1:
                        back(g - 1, 1)
                    if n == N_T0:
                        back(g, 0)
                    if n in N_MX and g + 1 < NG2:
                        maxima(g + 1, N_MX[n])
            values(NG2 - 1, NM2 - 1)
            back(NG2 - 1, 1)

        @block.scalar
        def _(act):
            def maxima(g, j):
                act.wait_ge(mt_ok, HG * g + j + 1)
                act.activation(QS[g % NSL][SROWS:KROWS, j, :], AUXB[SROWS:KROWS, :], ACT.Copy).then_inc(mtc_ok, 1)

            def outputs(g, qb):
                act.wait_ge(pv_ok, NM2 * g + (NM2 if qb else 4))
                act.activation(OT[:, qb, :], OB[:], ACT.Copy).then_inc(oc_ok, 1)

            for j in range(HG):
                maxima(0, j)
            for g in range(NG2):
                for n in range(NST):
                    mm = n // 2
                    q0, w = span(*blocks[mm])
                    act.wait_ge(st_ok, NST * g + n + 1)
                    if n % 2 == 0 and NM2 * g + mm >= 2:
                        act.wait_ge(pv_ok, NM2 * g + mm - 1)
                    hh = n % 2
                    act.activation(PT[:, mm % 2, 2 * hh:2 * hh + 2, 0:w],
                                   ST[n % 2][:].rearrange("p (h q) -> p h q", h=2)[:, :, 0:w],
                                   ACT.Exp, scale=SCALE).then_inc(exp_ok, 1)
                    if n == 1 and g >= 1:
                        outputs(g - 1, 1)
                    if n == N_T0 - 3:
                        outputs(g, 0)
                    if n in N_MX and g + 1 < NG2:
                        maxima(g + 1, N_MX[n])
            outputs(NG2 - 1, 1)

        @block.vector
        def _(dve):
            def pass1(g, s):
                j, qt, half = segs[s]
                at = NSEG * g + s
                dve.wait_ge(s1_ok, at + 1)
                w = min(TB, (qt + 1) * P - half * TB)
                dve.reduce_max(mx[:, g % 2, j, qt, half:half + 1], pass1_bank(at)[0][:, 0:w], AXX).then_inc(mx_ok, 1)
                if s % (NSEG // 2) == NSEG // 2 - 1:
                    i = j // 2
                    dve.wait_ge(mx_ok, NSEG * g + (i + 1) * NSEG // 2)
                    if g >= 1:
                        dve.wait_ge(nm_ok, 2 * (g - 1) + i + 1)
                    dve.tensor_tensor(m[:, i], mx[:, g % 2, 2 * i:2 * i + 2, :, 0], mx[:, g % 2, 2 * i:2 * i + 2, :, 1],
                                      ALU.max).then_inc(m_ok, 1)

            def normalise(g, qb):
                dve.wait_ge(t_ok, 2 * g + qb + 1)
                o = AUX[:].rearrange("p (t j e) -> p t j e", t=4, j=HG)
                dve.reciprocal(rec[:], o[:, :, :, SD]).then_inc(rec_ok, 1)
                dve.wait_ge(rec_ok, 2 * g + qb + 1)
                t = 8 * (g % 2) + 4 * qb
                dve.tensor_tensor(ATT[:, t:t + 4, 64 * (g // 2):64 * (g // 2) + 64].rearrange(
                                      "p t (j d) -> p t j d", j=HG),
                                  o[:, :, :, 0:SD], rec[:].unsqueeze(3).broadcast_to([P, 4, HG, SD]),
                                  ALU.mult).then_inc(nrm_ok, 1)

            dve.memset(mx[:], -3e38).then_inc(init_ok, 1)
            dve.wait_ge(mk_in, 16)
            dve.tensor_copy(MK[:], MKf[:]).then_inc(mk_ok, 1)
            dve.wait_ge(init_ok, 1)
            for g, s in ahead:
                pass1(g, s)
            for g in range(NG2):
                for n in range(NST):
                    for gs, s in segments(g, n):
                        pass1(gs, s)
                    if n == N_T1 and g >= 1:
                        normalise(g - 1, 1)
                    if n == N_T0:
                        normalise(g, 0)
            normalise(NG2 - 1, 1)


def out_projection(nc, ctx, X, ident, ATT, hTh, hTl, WOh, WOl):
    with ExitStack() as mem:
        sem = lambda n: ctx.enter_context(nc.semaphore("op_" + n))
        pb = lambda n: mem.enter_context(nc.psum_tensor("op_" + n, [P, TB], F32))
        banks = [pb(f"O{i}") for i in range(4)]
        p_ok, x_ok = sem("p_ok"), sem("x_ok")
        turned = norm_steps(nc, ctx, mem, "at_", ATT, ident, hTh, hTl, [pb(f"T{i}") for i in range(4)], norm=False)
        block = mem.enter_context(nc.Block())

        @block.tensor
        def _(pe):
            turned["turn"](pe, 0)
            turned["turn"](pe, 1)
            for n in range(NT // 2):
                turned["ready"](pe, n // 2)
                if n >= 4:
                    pe.wait_ge(x_ok, n - 3)
                for j in range(2):
                    t = 2 * n + j
                    o = banks[n % 4][:, j * HID:(j + 1) * HID]
                    for kt in range(KT):
                        hi, lo = (h[:, kt, t * P:(t + 1) * P] for h in (hTh, hTl))
                        a, c = (w[:, kt * HID:(kt + 1) * HID] for w in (WOh, WOl))
                        pe.matmul(o, hi, a, start=kt == 0, stop=False)
                        pe.matmul(o, hi, c, start=False, stop=False)
                        m = pe.matmul(o, lo, a, start=False, stop=kt == KT - 1)
                m.then_inc(p_ok, 1)
                if n % 2 == 1 and n // 2 + 2 < NTB:
                    turned["turn"](pe, n // 2 + 2)

        @block.scalar
        def _(act):
            for b in range(NTB):
                turned["high"](act, b)

        @block.vector
        def _(dve):
            turned["low"](dve, 0)
            turned["low"](dve, 1)
            for n in range(NT // 2):
                dve.wait_ge(p_ok, n + 1)
                dve.tensor_tensor(X[:, 2 * n:2 * n + 2, :], banks[n % 4][:].rearrange("p (t n) -> p t n", t=2),
                                  X[:, 2 * n:2 * n + 2, :], ALU.add).then_inc(x_ok, 1)
                if n % 2 == 1 and n // 2 + 2 < NTB:
                    turned["low"](dve, n // 2 + 2)


def program(nc, hidden, ident_in, w_quads, nw_quads, c_quads, w_ffn, s_ffn, d_ffn, w_att, rope, masks, out):
    with ExitStack() as ctx:
        sb = lambda n, s, d, c=ctx: c.enter_context(nc.sbuf_tensor(n, s, d))
        X = sb("X", [P, NT, HID], F32)
        ident = sb("ident", [P, P], F32)

        def normed(c, name):
            return sb(name + "hTh", [P, KT, TOK], F32R, c), sb(name + "hTl", [P, KT, TOK], F32R, c)

        with ExitStack() as part:
            hTh, hTl = normed(part, "a_")
            linear_attention(nc, ctx, X, ident, ident_in, hTh, hTl, hidden, w_quads, nw_quads, c_quads)

        WF = sb("WF", [P, 2 * KT * FI + NI * HID], F32R)
        SCL = sb("SCL", [P, 2 * NI], F32)
        DS = sb("DS", [P, HID], F32)
        with ExitStack() as part:
            hTh, hTl = normed(part, "b_")
            weights = quantised_weights(nc, ctx, part, w_ffn, s_ffn, d_ffn, WF, SCL, DS)
            ffn(nc, ctx, "f1_", X, ident, hTh, hTl, WF, SCL, DS, weights=weights)

        with ExitStack() as att:
            WOh = sb("WOh", [P, KT * HID], F32R, att)
            WOl = sb("WOl", [P, KT * HID], F32R, att)
            with ExitStack() as heads:
                q_parts, k_parts = (nc.dram_tensor(n, (BATCH, NPART, SD, SH // 2, 2, SEQ), BF16).ap()
                                    for n in ("q_parts", "k_parts"))
                V = sb("V", [P, NT, SH, 32], F32, heads)
                stacks0 = sb("stacks0", [P, 2, HG, SEQ], BF16, heads)
                s_in0 = ctx.enter_context(nc.semaphore("s_in0"))
                with ExitStack() as part:
                    hTh, hTl = normed(part, "c_")
                    rotary_projections(nc, ctx, X, ident, hTh, hTl, w_att, rope, q_parts, k_parts, V, WOh, WOl,
                                       stacks0, s_in0)
                ATT = sb("ATT", [P, NT, HID], F32, heads)
                causal_attention(nc, ctx, ident, masks, q_parts, k_parts, V, ATT, stacks0, s_in0)
                with ExitStack() as part:
                    hTh, hTl = normed(part, "d_")
                    out_projection(nc, ctx, X, ident, ATT, hTh, hTl, WOh, WOl)

        with ExitStack() as part:
            hTh, hTl = normed(part, "e_")
            ffn(nc, ctx, "f2_", X, ident, hTh, hTl, WF, SCL, DS, out)


def rotary_constants():
    import numpy as np
    half = SD // 2
    inv = (np.float32(1.0) / np.float32(10000.0) ** (np.arange(half, dtype=np.float32) / np.float32(half)))
    f = (np.arange(SEQ, dtype=np.float32)[None, :] * inv.astype(np.float32)[:, None]).astype(np.float32)
    row = np.arange(P) // (SH // 2)
    cos = np.cos(f.astype(np.float64))[row // 2]
    sin = np.sin(f.astype(np.float64))[row // 2] * np.where(row % 2 == 0, -1.0, 1.0)[:, None]
    rope = np.stack([cos, sin], 1).astype(np.float32)
    masks = np.zeros((P, 3, P), np.float32)
    masks[:, 0] = np.eye(P)
    masks[:, 1] = np.triu(np.full((P, P), -1e30), 1)
    masks[:, 2] = np.tril(np.full((P, P), -1e30), -1)
    return rope, masks


def linear_constants():
    import numpy as np
    r = (1.0 / 2.0 ** (8.0 / LH)) ** (np.arange(LH, dtype=np.float64) + 1.0)
    slope = np.float32(r * (1.0 + 1e-5)).astype(np.float64)
    i = np.arange(P, dtype=np.float64)
    diff = i[None, :] - i[:, None]
    D = np.where(diff >= 0, np.exp(-slope[:, None, None] * np.maximum(diff, 0)), 0.0)
    QD = np.exp(-slope[:, None] * (i + 1))
    KD = np.exp(-slope[:, None] * (P - 1 - i))
    BD = np.exp(-slope * P)
    c = np.zeros((NQ, P, CW), np.float32)
    for n in range(NQ):
        for h in range(4):
            c[n, :, CD + h * P:CD + (h + 1) * P] = D[4 * n + h]
            c[n, :, CK + h] = KD[4 * n + h]
            rows = slice((h % 2) * LD, (h % 2 + 1) * LD)
            c[n, rows, CQ + (h // 2) * P:CQ + (h // 2 + 1) * P] = QD[4 * n + h]
            c[n, rows, CB + h // 2] = BD[4 * n + h]
    return c


def kernel(**inputs):
    import numpy as np
    import concourse.bacc as bacc
    from concourse.bass_utils import run_bass_kernel_spmd

    a = {n: np.asarray(x) for n, x in inputs.items()}
    hidden = a["L0_attn_a_hidden_states"].reshape(NT, P, HID).transpose(1, 0, 2)
    qkv = a["L0_attn_a_qkv_w"].reshape(NQ, 2, 2, 3, LD, KT, P)
    gate = a["L0_attn_a_gate_w"].reshape(NQ, 4 * LD, KT, P)
    cols = [qkv[:, :, :, 0].reshape(NQ, 4 * LD, KT, P), qkv[:, :, :, 1].reshape(NQ, 4 * LD, KT, P), gate,
            qkv[:, :, :, 2].reshape(NQ, 4 * LD, KT, P)]
    wq = np.concatenate(cols, 1).transpose(0, 3, 2, 1).reshape(NQ, P, KT * QW)
    wo = a["L0_attn_a_out_w"].T.reshape(NQ, 2, P, HID).transpose(0, 2, 1, 3).reshape(NQ, P, 2 * HID)
    arrays = {
        "hidden": hidden, "ident": np.eye(P, dtype=np.float32),
        "w_quads": np.concatenate([wq, wo], 2),
        "nw_quads": a["L0_attn_a_norm_w"].reshape(NQ, 2, P).transpose(0, 2, 1),
        "c_quads": linear_constants(),
    }
    up = [a["L0_ffn_" + n].reshape(KT, P, FI).transpose(1, 0, 2).reshape(P, KT * FI) for n in ("gate_w", "up_w")]
    down = a["L0_ffn_down_w"].reshape(NI, P, HID).transpose(1, 0, 2).reshape(P, NI * HID)
    arrays["w_ffn"] = np.concatenate(up + [down], 1)
    arrays["s_ffn"] = np.concatenate([a["L0_ffn_" + n].reshape(NI, P).T for n in ("gate_scale", "up_scale")], 1)
    arrays["d_ffn"] = np.broadcast_to(a["L0_ffn_down_scale"], (P, HID))
    pairs = np.arange(HID) ^ (SH // 2)
    wq, wk, wv, wo = (a["L0_attn_b_W" + n] for n in "qkvo")
    wq, wk = (w.reshape(SH // 2, 2, SD, HID).transpose(1, 2, 0, 3).reshape(HID, HID) for w in (wq, wk))
    cols = lambda *ws: np.stack([w.T.reshape(KT, P, HID) for w in ws], 2).transpose(1, 0, 2, 3).reshape(P, -1)
    arrays["w_att"] = np.concatenate([cols(wq, wq[pairs]), cols(wk, wk[pairs]), cols(wv), cols(wo)], 1)
    rope, masks = rotary_constants()
    arrays["rope"] = rope
    arrays["masks"] = masks
    nc = bacc.Bacc("TRN2", target_bir_lowering=False, num_devices=1)
    args, arr = [], {}
    for name, x in arrays.items():
        x = np.ascontiguousarray(x)
        arr[name + "_dram"] = x
        args.append(nc.dram_tensor(name + "_dram", x.shape, mybir.dt.from_np(x.dtype), kind="ExternalInput").ap())
    args.append(nc.dram_tensor("out_dram", (P, NT, HID), F32, kind="ExternalOutput").ap())
    program(nc, *args)
    r = run_bass_kernel_spmd(nc, [arr], core_ids=[0])
    return r.results[0]["out_dram"].transpose(1, 0, 2).reshape(BATCH, SEQ, HID)
```
